# Optimizing a Trainium2 kernel written in Bass

```python
import numpy as np
import jax
import jax.numpy as jnp

def _softmax(x, axis=-1):
    return jax.nn.softmax(x, axis=axis)

def _gelu(x):
    return jax.nn.gelu(x, approximate=True)

def _silu(x):
    return jax.nn.silu(x)

def _sigmoid(x):
    return jax.nn.sigmoid(x)

def _layernorm(x, axis=-1, eps=1e-05):
    m = jnp.mean(x, axis=axis, keepdims=True)
    v = jnp.var(x, axis=axis, keepdims=True)
    return (x - m) / jnp.sqrt(v + eps)

def _scatter_add(tgt, idx, src, axis=0):
    return tgt.at[idx].add(src)

def _segment_sum(src, seg, n):
    return jax.ops.segment_sum(src, seg, n)
kernel_name = 'mk_gnn_ffn_d4_gnn_r32_14dfaa'

def setup_inputs(seed: int=0):
    np.random.seed(seed)
    _w = jnp.asarray

    def _rec_inputs():
        import jax
        import jax.numpy as jnp
        _gk = jax.random.key(seed)
        x = -6.415e-05 + 1 * jax.random.normal(jax.random.fold_in(_gk, 1), (625, 512), jnp.float32)
        src = jax.random.randint(jax.random.fold_in(_gk, 2), (20000,), 0, 625, jnp.int32)
        dst = jnp.minimum((625 * jax.random.uniform(jax.random.fold_in(_gk, 3), (20000,)) ** 2.0).astype(jnp.int32), 19999)
        _o = jnp.argsort(dst, stable=True)
        src = src[_o]
        dst = dst[_o]
        edge_attr_4 = 0.00171547 + 0.999346 * jax.random.normal(jax.random.fold_in(_gk, 12), (20000, 4), jnp.float32)
        edge_attr_64 = 0.000279952 + 1.00013 * jax.random.normal(jax.random.fold_in(_gk, 13), (20000, 64), jnp.float32)
        edge_attr_8 = 0.000126197 + 0.999763 * jax.random.normal(jax.random.fold_in(_gk, 14), (20000, 8), jnp.float32)
        edge_type_8 = jax.random.randint(jax.random.fold_in(_gk, 16), (20000,), 0, 8, jnp.int32)
        return (x, src, dst, edge_attr_4, edge_attr_64, edge_attr_8, edge_type_8)
    x, src, dst, edge_attr_4, edge_attr_64, edge_attr_8, edge_type_8 = _rec_inputs()

    def _L0_gnn_setup():
        import jax, jax.numpy as jnp
        import numpy as np
        N = 625
        E = 5000
        D = 512
        R = 8
        key = jax.random.key(seed)
        ks = jax.random.split(key, 8)
        inp = {'input': jax.random.normal(ks[0], (N, D), dtype=jnp.float32), 'heads': jax.random.randint(ks[1], (E,), 0, N), 'tails': jax.random.randint(ks[2], (E,), 0, N), 'rel': jax.random.randint(ks[3], (E,), 0, R), 'W_self': jax.random.normal(ks[4], (D, D), dtype=jnp.float32) * 0.03, 'b_self': jnp.zeros((D,), dtype=jnp.float32), 'W_rel': jax.random.normal(ks[5], (2 * R, D, D), dtype=jnp.float32) * 0.03, 'b_rel': jnp.zeros((2 * R, D), dtype=jnp.float32)}
        return inp
    _L0_gnn_all = _L0_gnn_setup()
    _L0_gnn_in = {k: v for k, v in _L0_gnn_all.items() if k in ('W_self', 'b_self', 'W_rel', 'b_rel')}
    del _L0_gnn_all

    def _L0_ffn_setup():
        import jax, jax.numpy as jnp
        import numpy as np
        ROUTER_JITTER = 0.01
        NEG_INF = -jnp.inf

        def _sparsemixer_eval(scores, num_experts):
            eids = jnp.arange(num_experts)
            max1 = jnp.max(scores, axis=-1, keepdims=True)
            sel1 = jnp.argmax(scores, axis=-1)
            factor1 = jnp.maximum(jnp.abs(scores), max1)
            mask1 = (max1 - scores) / factor1 > 2.0 * ROUTER_JITTER
            mg1 = jnp.where(mask1, NEG_INF, scores)
            p1 = jax.nn.softmax(mg1, axis=-1)
            mult1 = jnp.take_along_axis(p1, sel1[:, None], axis=-1)[:, 0]
            oh1 = sel1[:, None] == eids[None, :]
            masked_scores = jnp.where(oh1, NEG_INF, scores)
            max2 = jnp.max(masked_scores, axis=-1, keepdims=True)
            sel2 = jnp.argmax(masked_scores, axis=-1)
            factor2 = jnp.maximum(jnp.abs(scores), max2)
            mask2 = (max2 - scores) / factor2 > 2.0 * ROUTER_JITTER
            mg2 = jnp.where(mask2, NEG_INF, masked_scores)
            p2 = jax.nn.softmax(mg2, axis=-1)
            mult2 = jnp.take_along_axis(p2, sel2[:, None], axis=-1)[:, 0]
            weights = jnp.stack([mult1, mult2], axis=-1)
            experts = jnp.stack([sel1, sel2], axis=-1)
            return (weights, experts)
        B, S, H, F, E = (2, 64, 512, 1024, 8)
        key = jax.random.key(seed)
        ks = jax.random.split(key, 6)
        scale_h = 1.0 / np.sqrt(H)
        scale_f = 1.0 / np.sqrt(F)
        return {'x': jax.random.normal(ks[0], (B, S, H), dtype=jnp.float32), 'wg': jax.random.normal(ks[1], (H, E), dtype=jnp.float32) * scale_h, 'bg': jax.random.normal(ks[2], (E,), dtype=jnp.float32) * 0.01, 'w1': jax.random.normal(ks[3], (E, H, F), dtype=jnp.float32) * scale_h, 'w3': jax.random.normal(ks[4], (E, H, F), dtype=jnp.float32) * scale_h, 'w2': jax.random.normal(ks[5], (E, F, H), dtype=jnp.float32) * scale_f}
    _L0_ffn_all = _L0_ffn_setup()
    _L0_ffn_in = {k: v for k, v in _L0_ffn_all.items() if k in ('wg', 'bg', 'w1', 'w3', 'w2')}
    del _L0_ffn_all

    def _L1_gnn_setup():
        import jax, jax.numpy as jnp
        import numpy as np
        MUL = 128
        N_NODES = 10000
        N_EDGES = 5000
        R_BASIS = 8
        HIDDEN = 64
        W_NUMEL = 4 * MUL
        SQRT3 = 3.0 ** 0.5
        SILU_2MOM = 1.679177
        AVG_NUM_NEIGHBORS = 10.0

        def _lin_irreps(x0, x1, W0, W1):
            y0 = x0 @ W0 / jnp.sqrt(jnp.float32(W0.shape[0]))
            y1 = jnp.einsum('num,uv->nvm', x1, W1) / jnp.sqrt(jnp.float32(W1.shape[0]))
            return (y0, y1)

        def _forward(node_feats, edge_attrs, edge_feats, edge_index, W_up0, W_up1, W_mlp1, W_mlp2, W_mlp3, W_mlp4, W_out0, W_out1):
            num_nodes = node_feats.shape[0]
            sender, receiver = (edge_index[0], edge_index[1])
            x0 = node_feats[:, :MUL]
            x1 = node_feats[:, MUL:].reshape(num_nodes, MUL, 3)
            x0, x1 = _lin_irreps(x0, x1, W_up0, W_up1)
            h = edge_feats
            for W in (W_mlp1, W_mlp2, W_mlp3):
                h = SILU_2MOM * jax.nn.silu(h @ W / jnp.sqrt(jnp.float32(W.shape[0])))
            tpw = h @ W_mlp4 / jnp.sqrt(jnp.float32(W_mlp4.shape[0]))
            w1, w2, w3, w4 = jnp.split(tpw, 4, axis=-1)
            s0 = x0[sender]
            s1 = x1[sender]
            y0 = edge_attrs[:, 0:1]
            y1 = edge_attrs[:, 1:4]
            p1 = w1 * s0 * y0
            p2 = (w2 * s0)[:, :, None] * y1[:, None, :]
            p3 = w3[:, :, None] * s1 * y0[:, None, :]
            p4 = w4 * jnp.einsum('eum,em->eu', s1, y1) / SQRT3
            m0 = jnp.concatenate([p1, p4], axis=-1)
            m1 = jnp.concatenate([p2, p3], axis=1)
            msg0 = jax.ops.segment_sum(m0, receiver, num_segments=num_nodes)
            msg1 = jax.ops.segment_sum(m1, receiver, num_segments=num_nodes)
            o0, o1 = _lin_irreps(msg0, msg1, W_out0, W_out1)
            out = jnp.concatenate([o0, o1.reshape(num_nodes, 3 * MUL)], axis=-1)
            return out / AVG_NUM_NEIGHBORS
        key = jax.random.key(seed)
        ks = jax.random.split(key, 12)
        rn = lambda k, s: jax.random.normal(k, s, dtype=jnp.float32)
        return {'node_feats': rn(ks[0], (N_NODES, 4 * MUL)), 'edge_attrs': rn(ks[1], (N_EDGES, 4)), 'edge_feats': rn(ks[2], (N_EDGES, R_BASIS)), 'edge_index': jax.random.randint(ks[3], (2, N_EDGES), 0, N_NODES), 'W_up0': rn(ks[4], (MUL, MUL)), 'W_up1': rn(ks[5], (MUL, MUL)), 'W_mlp1': rn(ks[6], (R_BASIS, HIDDEN)), 'W_mlp2': rn(ks[7], (HIDDEN, HIDDEN)), 'W_mlp3': rn(ks[8], (HIDDEN, HIDDEN)), 'W_mlp4': rn(ks[9], (HIDDEN, W_NUMEL)), 'W_out0': rn(ks[10], (2 * MUL, MUL)), 'W_out1': rn(ks[11], (2 * MUL, MUL))}
    _L1_gnn_all = _L1_gnn_setup()
    _L1_gnn_in = {k: v for k, v in _L1_gnn_all.items() if k in ('W_up0', 'W_up1', 'W_mlp1', 'W_mlp2', 'W_mlp3', 'W_mlp4', 'W_out0', 'W_out1')}
    del _L1_gnn_all

    def _L1_ffn_setup():
        import jax, jax.numpy as jnp
        import numpy as np
        B, S, D, F, E = (4, 64, 512, 64, 8)
        key = jax.random.key(seed)
        k = jax.random.split(key, 5)
        x = jax.random.normal(k[0], (B, S, D), dtype=jnp.float32)
        Ws = jax.random.normal(k[1], (D, E), dtype=jnp.float32) * 0.02
        bs = jnp.zeros((E,), dtype=jnp.float32)
        W1 = jax.random.normal(k[2], (E, D, F), dtype=jnp.float32) * 0.02
        b1 = jnp.zeros((E, F), dtype=jnp.float32)
        W2 = jax.random.normal(k[3], (E, F, D), dtype=jnp.float32) * 0.02
        b2 = jnp.zeros((E, D), dtype=jnp.float32)
        return {'x': x, 'Ws': Ws, 'bs': bs, 'W1': W1, 'b1': b1, 'W2': W2, 'b2': b2}
    _L1_ffn_all = _L1_ffn_setup()
    _L1_ffn_in = {k: v for k, v in _L1_ffn_all.items() if k in ('Ws', 'bs', 'W1', 'b1', 'W2', 'b2')}
    del _L1_ffn_all

    def _L2_gnn_setup():
        import jax, jax.numpy as jnp
        import numpy as np
        N_NODES = 625
        N_EDGES = 10000
        D_IN = 512
        D_HID = 512
        EPS = 1e-05

        def _xavier(key, shape):
            fan_in, fan_out = (shape[1], shape[0])
            limit = np.sqrt(6.0 / (fan_in + fan_out)).astype(np.float32)
            return jax.random.uniform(key, shape, jnp.float32, -limit, limit)

        def _sage_conv(h, src, dst, Wl, bl, Wr):
            msg = h[src]
            s = jax.ops.segment_sum(msg, dst, num_segments=N_NODES)
            cnt = jax.ops.segment_sum(jnp.ones((src.shape[0], 1), h.dtype), dst, num_segments=N_NODES)
            agg = s / jnp.maximum(cnt, 1.0)
            return agg @ Wl.T + bl + h @ Wr.T

        def _layer_norm(h, g, b):
            mu = jnp.mean(h, axis=-1, keepdims=True)
            var = jnp.mean((h - mu) ** 2, axis=-1, keepdims=True)
            return (h - mu) * jax.lax.rsqrt(var + EPS) * g + b

        def _prelu(h, a):
            return jnp.where(h >= 0, h, a * h)
        key = jax.random.key(seed)
        ks = jax.random.split(key, 16)
        x = jax.random.normal(ks[0], (N_NODES, D_IN), jnp.float32)
        edge_index = jax.random.randint(ks[1], (2, N_EDGES), 0, N_NODES, jnp.int64)
        dims = [(D_IN, D_HID), (D_HID, D_HID), (D_HID, D_HID)]
        inp = {'x': x, 'edge_index': edge_index}
        for i, (din, dout) in enumerate(dims):
            inp[f'Wl{i}'] = _xavier(ks[2 + 3 * i], (dout, din))
            inp[f'bl{i}'] = jnp.zeros((dout,), jnp.float32)
            inp[f'Wr{i}'] = _xavier(ks[3 + 3 * i], (dout, din))
            inp[f'g{i}'] = jnp.ones((dout,), jnp.float32)
            inp[f'b{i}'] = jnp.zeros((dout,), jnp.float32)
        inp['a_prelu'] = jnp.full((1,), 0.25, jnp.float32)
        return inp
    _L2_gnn_all = _L2_gnn_setup()
    _L2_gnn_in = {k: v for k, v in _L2_gnn_all.items() if k in ('Wl0', 'bl0', 'Wr0', 'g0', 'b0', 'Wl1', 'bl1', 'Wr1', 'g1', 'b1', 'Wl2', 'bl2', 'Wr2', 'g2', 'b2', 'a_prelu')}
    del _L2_gnn_all

    def _L2_ffn_setup():
        import math
        import jax, jax.numpy as jnp
        import numpy as np
        B, T, H, E, K, F = (4, 128, 512, 8, 2, 64)
        CAP_FACTOR, ROUND_TO = (0.3125, 128)

        def _capacity(num_tokens):
            cap = math.ceil(CAP_FACTOR * num_tokens)
            cap = ROUND_TO * math.ceil(cap / ROUND_TO)
            return max(1, min(cap, num_tokens))
        key = jax.random.key(seed)
        k0, k1, k2, k3 = jax.random.split(key, 4)
        x = jax.random.normal(k0, (B, T, H), jnp.float32)
        router_w = jax.random.normal(k1, (H, E), jnp.float32) * 0.02
        w1 = jax.random.normal(k2, (E, H, F), jnp.float32) * (1.0 / np.sqrt(H))
        b1 = jnp.zeros((E, F), jnp.float32)
        w2 = jax.random.normal(k3, (E, F, H), jnp.float32) * (1.0 / np.sqrt(F))
        b2 = jnp.zeros((E, H), jnp.float32)
        return {'x': x, 'router_w': router_w, 'w1': w1, 'b1': b1, 'w2': w2, 'b2': b2}
    _L2_ffn_all = _L2_ffn_setup()
    _L2_ffn_in = {k: v for k, v in _L2_ffn_all.items() if k in ('router_w', 'w1', 'b1', 'w2', 'b2')}
    del _L2_ffn_all

    def _L3_gnn_setup():
        import jax, jax.numpy as jnp
        import numpy as np
        N_NODES = 625
        N_EDGES = 10000
        HIDDEN = 512
        EDGE_DIM = 64
        LN_EPS = 1e-05

        def mish(x):
            return x * jnp.tanh(jax.nn.softplus(x))
        key = jax.random.key(seed)
        ks = jax.random.split(key, 8)
        s = lambda fan_in: 1.0 / np.sqrt(fan_in)
        return {'x': jax.random.normal(ks[0], (N_NODES, HIDDEN), dtype=jnp.float32), 'edge_index': jax.random.randint(ks[1], (2, N_EDGES), 0, N_NODES, dtype=jnp.int64), 'edge_attr': jax.random.normal(ks[2], (N_EDGES, EDGE_DIM), dtype=jnp.float32), 'W1': jax.random.normal(ks[3], (2 * HIDDEN + EDGE_DIM, HIDDEN), dtype=jnp.float32) * s(2 * HIDDEN + EDGE_DIM), 'b1': jnp.zeros((HIDDEN,), dtype=jnp.float32), 'W2': jax.random.normal(ks[4], (HIDDEN, HIDDEN), dtype=jnp.float32) * s(HIDDEN), 'b2': jnp.zeros((HIDDEN,), dtype=jnp.float32), 'W3': jax.random.normal(ks[5], (2 * HIDDEN, HIDDEN), dtype=jnp.float32) * s(2 * HIDDEN), 'b3': jnp.zeros((HIDDEN,), dtype=jnp.float32), 'W4': jax.random.normal(ks[6], (HIDDEN, HIDDEN), dtype=jnp.float32) * s(HIDDEN), 'b4': jnp.zeros((HIDDEN,), dtype=jnp.float32), 'gamma': jnp.ones((HIDDEN,), dtype=jnp.float32), 'beta': jnp.zeros((HIDDEN,), dtype=jnp.float32)}
    _L3_gnn_all = _L3_gnn_setup()
    _L3_gnn_in = {k: v for k, v in _L3_gnn_all.items() if k in ('W1', 'b1', 'W2', 'b2', 'W3', 'b3', 'W4', 'b4', 'gamma', 'beta')}
    del _L3_gnn_all

    def _L3_ffn_setup():
        import jax, jax.numpy as jnp
        import numpy as np
        D_MODEL, D_FF, N_EXPERTS, TOP_K = (512, 64, 8, 2)
        key = jax.random.key(seed)
        ks = jax.random.split(key, 7)
        B, S = (2, 64)
        x = jax.random.normal(ks[0], (B, S, D_MODEL), dtype=jnp.float32)
        s1 = 1.0 / np.sqrt(D_MODEL)
        s2 = 1.0 / np.sqrt(D_FF)
        Wg = jax.random.normal(ks[1], (D_MODEL, N_EXPERTS), dtype=jnp.float32) * s1
        bg = jnp.zeros((N_EXPERTS,), dtype=jnp.float32)
        W1 = jax.random.normal(ks[2], (N_EXPERTS, D_MODEL, D_FF), dtype=jnp.float32) * s1
        b1 = jax.random.normal(ks[3], (N_EXPERTS, D_FF), dtype=jnp.float32) * s1
        W2 = jax.random.normal(ks[4], (N_EXPERTS, D_FF, D_MODEL), dtype=jnp.float32) * s2
        b2 = jax.random.normal(ks[5], (N_EXPERTS, D_MODEL), dtype=jnp.float32) * s2
        return {'x': x, 'Wg': Wg, 'bg': bg, 'W1': W1, 'b1': b1, 'W2': W2, 'b2': b2}
    _L3_ffn_all = _L3_ffn_setup()
    _L3_ffn_in = {k: v for k, v in _L3_ffn_all.items() if k in ('Wg', 'bg', 'W1', 'b1', 'W2', 'b2')}
    del _L3_ffn_all
    return {'x': x, 'src': src, 'dst': dst, 'edge_attr_4': edge_attr_4, 'edge_attr_64': edge_attr_64, 'edge_attr_8': edge_attr_8, 'edge_type_8': edge_type_8, 'L0_gnn_W_self': _L0_gnn_in['W_self'], 'L0_gnn_b_self': _L0_gnn_in['b_self'], 'L0_gnn_W_rel': _L0_gnn_in['W_rel'], 'L0_gnn_b_rel': _L0_gnn_in['b_rel'], 'L0_ffn_wg': _L0_ffn_in['wg'], 'L0_ffn_bg': _L0_ffn_in['bg'], 'L0_ffn_w1': _L0_ffn_in['w1'], 'L0_ffn_w3': _L0_ffn_in['w3'], 'L0_ffn_w2': _L0_ffn_in['w2'], 'L1_gnn_W_up0': _L1_gnn_in['W_up0'], 'L1_gnn_W_up1': _L1_gnn_in['W_up1'], 'L1_gnn_W_mlp1': _L1_gnn_in['W_mlp1'], 'L1_gnn_W_mlp2': _L1_gnn_in['W_mlp2'], 'L1_gnn_W_mlp3': _L1_gnn_in['W_mlp3'], 'L1_gnn_W_mlp4': _L1_gnn_in['W_mlp4'], 'L1_gnn_W_out0': _L1_gnn_in['W_out0'], 'L1_gnn_W_out1': _L1_gnn_in['W_out1'], 'L1_ffn_Ws': _L1_ffn_in['Ws'], 'L1_ffn_bs': _L1_ffn_in['bs'], 'L1_ffn_W1': _L1_ffn_in['W1'], 'L1_ffn_b1': _L1_ffn_in['b1'], 'L1_ffn_W2': _L1_ffn_in['W2'], 'L1_ffn_b2': _L1_ffn_in['b2'], 'L2_gnn_Wl0': _L2_gnn_in['Wl0'], 'L2_gnn_bl0': _L2_gnn_in['bl0'], 'L2_gnn_Wr0': _L2_gnn_in['Wr0'], 'L2_gnn_g0': _L2_gnn_in['g0'], 'L2_gnn_b0': _L2_gnn_in['b0'], 'L2_gnn_Wl1': _L2_gnn_in['Wl1'], 'L2_gnn_bl1': _L2_gnn_in['bl1'], 'L2_gnn_Wr1': _L2_gnn_in['Wr1'], 'L2_gnn_g1': _L2_gnn_in['g1'], 'L2_gnn_b1': _L2_gnn_in['b1'], 'L2_gnn_Wl2': _L2_gnn_in['Wl2'], 'L2_gnn_bl2': _L2_gnn_in['bl2'], 'L2_gnn_Wr2': _L2_gnn_in['Wr2'], 'L2_gnn_g2': _L2_gnn_in['g2'], 'L2_gnn_b2': _L2_gnn_in['b2'], 'L2_gnn_a_prelu': _L2_gnn_in['a_prelu'], 'L2_ffn_router_w': _L2_ffn_in['router_w'], 'L2_ffn_w1': _L2_ffn_in['w1'], 'L2_ffn_b1': _L2_ffn_in['b1'], 'L2_ffn_w2': _L2_ffn_in['w2'], 'L2_ffn_b2': _L2_ffn_in['b2'], 'L3_gnn_W1': _L3_gnn_in['W1'], 'L3_gnn_b1': _L3_gnn_in['b1'], 'L3_gnn_W2': _L3_gnn_in['W2'], 'L3_gnn_b2': _L3_gnn_in['b2'], 'L3_gnn_W3': _L3_gnn_in['W3'], 'L3_gnn_b3': _L3_gnn_in['b3'], 'L3_gnn_W4': _L3_gnn_in['W4'], 'L3_gnn_b4': _L3_gnn_in['b4'], 'L3_gnn_gamma': _L3_gnn_in['gamma'], 'L3_gnn_beta': _L3_gnn_in['beta'], 'L3_ffn_Wg': _L3_ffn_in['Wg'], 'L3_ffn_bg': _L3_ffn_in['bg'], 'L3_ffn_W1': _L3_ffn_in['W1'], 'L3_ffn_b1': _L3_ffn_in['b1'], 'L3_ffn_W2': _L3_ffn_in['W2'], 'L3_ffn_b2': _L3_ffn_in['b2']}

def reference(x, src, dst, edge_attr_4, edge_attr_64, edge_attr_8, edge_type_8, L0_gnn_W_self, L0_gnn_b_self, L0_gnn_W_rel, L0_gnn_b_rel, L0_ffn_wg, L0_ffn_bg, L0_ffn_w1, L0_ffn_w3, L0_ffn_w2, L1_gnn_W_up0, L1_gnn_W_up1, L1_gnn_W_mlp1, L1_gnn_W_mlp2, L1_gnn_W_mlp3, L1_gnn_W_mlp4, L1_gnn_W_out0, L1_gnn_W_out1, L1_ffn_Ws, L1_ffn_bs, L1_ffn_W1, L1_ffn_b1, L1_ffn_W2, L1_ffn_b2, L2_gnn_Wl0, L2_gnn_bl0, L2_gnn_Wr0, L2_gnn_g0, L2_gnn_b0, L2_gnn_Wl1, L2_gnn_bl1, L2_gnn_Wr1, L2_gnn_g1, L2_gnn_b1, L2_gnn_Wl2, L2_gnn_bl2, L2_gnn_Wr2, L2_gnn_g2, L2_gnn_b2, L2_gnn_a_prelu, L2_ffn_router_w, L2_ffn_w1, L2_ffn_b1, L2_ffn_w2, L2_ffn_b2, L3_gnn_W1, L3_gnn_b1, L3_gnn_W2, L3_gnn_b2, L3_gnn_W3, L3_gnn_b3, L3_gnn_W4, L3_gnn_b4, L3_gnn_gamma, L3_gnn_beta, L3_ffn_Wg, L3_ffn_bg, L3_ffn_W1, L3_ffn_b1, L3_ffn_W2, L3_ffn_b2):
    import jax
    import jax.numpy as jnp

    def _L0_gnn_ref(input, heads, tails, rel, W_self, b_self, W_rel, b_rel):
        import jax, jax.numpy as jnp
        import numpy as np
        N = 625
        E = 5000
        D = 512
        R = 8
        h_self = input @ W_self.T + b_self
        H_all = jnp.einsum('rod,nd->rno', W_rel, input) + b_rel[:, None, :]
        msg_to_heads = H_all[rel, tails]
        msg_to_tails = H_all[rel + R, heads]
        agg = jax.ops.segment_sum(msg_to_heads, heads, num_segments=N) + jax.ops.segment_sum(msg_to_tails, tails, num_segments=N)
        return jax.nn.relu(h_self + agg)

    def _L0_ffn_ref(x, wg, bg, w1, w3, w2):
        import jax, jax.numpy as jnp
        import numpy as np
        ROUTER_JITTER = 0.01
        NEG_INF = -jnp.inf

        def _sparsemixer_eval(scores, num_experts):
            eids = jnp.arange(num_experts)
            max1 = jnp.max(scores, axis=-1, keepdims=True)
            sel1 = jnp.argmax(scores, axis=-1)
            factor1 = jnp.maximum(jnp.abs(scores), max1)
            mask1 = (max1 - scores) / factor1 > 2.0 * ROUTER_JITTER
            mg1 = jnp.where(mask1, NEG_INF, scores)
            p1 = jax.nn.softmax(mg1, axis=-1)
            mult1 = jnp.take_along_axis(p1, sel1[:, None], axis=-1)[:, 0]
            oh1 = sel1[:, None] == eids[None, :]
            masked_scores = jnp.where(oh1, NEG_INF, scores)
            max2 = jnp.max(masked_scores, axis=-1, keepdims=True)
            sel2 = jnp.argmax(masked_scores, axis=-1)
            factor2 = jnp.maximum(jnp.abs(scores), max2)
            mask2 = (max2 - scores) / factor2 > 2.0 * ROUTER_JITTER
            mg2 = jnp.where(mask2, NEG_INF, masked_scores)
            p2 = jax.nn.softmax(mg2, axis=-1)
            mult2 = jnp.take_along_axis(p2, sel2[:, None], axis=-1)[:, 0]
            weights = jnp.stack([mult1, mult2], axis=-1)
            experts = jnp.stack([sel1, sel2], axis=-1)
            return (weights, experts)
        B, S, H = x.shape
        E = w1.shape[0]
        xt = x.reshape(-1, H)
        scores = jax.nn.softmax(xt @ wg + bg, axis=-1)
        routing_weights, selected_experts = _sparsemixer_eval(scores, E)
        eids = jnp.arange(E)
        comb = jnp.sum(routing_weights[:, :, None] * (selected_experts[:, :, None] == eids[None, None, :]).astype(xt.dtype), axis=1)
        out = jnp.zeros_like(xt)
        for e in range(E):
            h = jax.nn.gelu(xt @ w1[e], approximate=False) * (xt @ w3[e])
            out = out + comb[:, e:e + 1] * (h @ w2[e])
        return out.reshape(B, S, H)

    def _L1_gnn_ref(node_feats, edge_attrs, edge_feats, edge_index, W_up0, W_up1, W_mlp1, W_mlp2, W_mlp3, W_mlp4, W_out0, W_out1):
        import jax, jax.numpy as jnp
        import numpy as np
        MUL = 128
        N_NODES = 10000
        N_EDGES = 5000
        R_BASIS = 8
        HIDDEN = 64
        W_NUMEL = 4 * MUL
        SQRT3 = 3.0 ** 0.5
        SILU_2MOM = 1.679177
        AVG_NUM_NEIGHBORS = 10.0

        def _lin_irreps(x0, x1, W0, W1):
            y0 = x0 @ W0 / jnp.sqrt(jnp.float32(W0.shape[0]))
            y1 = jnp.einsum('num,uv->nvm', x1, W1) / jnp.sqrt(jnp.float32(W1.shape[0]))
            return (y0, y1)

        def _forward(node_feats, edge_attrs, edge_feats, edge_index, W_up0, W_up1, W_mlp1, W_mlp2, W_mlp3, W_mlp4, W_out0, W_out1):
            num_nodes = node_feats.shape[0]
            sender, receiver = (edge_index[0], edge_index[1])
            x0 = node_feats[:, :MUL]
            x1 = node_feats[:, MUL:].reshape(num_nodes, MUL, 3)
            x0, x1 = _lin_irreps(x0, x1, W_up0, W_up1)
            h = edge_feats
            for W in (W_mlp1, W_mlp2, W_mlp3):
                h = SILU_2MOM * jax.nn.silu(h @ W / jnp.sqrt(jnp.float32(W.shape[0])))
            tpw = h @ W_mlp4 / jnp.sqrt(jnp.float32(W_mlp4.shape[0]))
            w1, w2, w3, w4 = jnp.split(tpw, 4, axis=-1)
            s0 = x0[sender]
            s1 = x1[sender]
            y0 = edge_attrs[:, 0:1]
            y1 = edge_attrs[:, 1:4]
            p1 = w1 * s0 * y0
            p2 = (w2 * s0)[:, :, None] * y1[:, None, :]
            p3 = w3[:, :, None] * s1 * y0[:, None, :]
            p4 = w4 * jnp.einsum('eum,em->eu', s1, y1) / SQRT3
            m0 = jnp.concatenate([p1, p4], axis=-1)
            m1 = jnp.concatenate([p2, p3], axis=1)
            msg0 = jax.ops.segment_sum(m0, receiver, num_segments=num_nodes)
            msg1 = jax.ops.segment_sum(m1, receiver, num_segments=num_nodes)
            o0, o1 = _lin_irreps(msg0, msg1, W_out0, W_out1)
            out = jnp.concatenate([o0, o1.reshape(num_nodes, 3 * MUL)], axis=-1)
            return out / AVG_NUM_NEIGHBORS
        return _forward(node_feats, edge_attrs, edge_feats, edge_index, W_up0, W_up1, W_mlp1, W_mlp2, W_mlp3, W_mlp4, W_out0, W_out1)

    def _L1_ffn_ref(x, Ws, bs, W1, b1, W2, b2):
        import jax, jax.numpy as jnp
        import numpy as np
        B, S, D, F, E = (4, 64, 512, 64, 8)
        Bb, Ss, Dd = x.shape
        xt = x.reshape(-1, Dd)
        logits = xt @ Ws + bs
        probs = jax.nn.softmax(logits, axis=-1)
        prob_max = jnp.max(probs, axis=-1)
        routes = jnp.argmax(probs, axis=-1)
        onehot = jax.nn.one_hot(routes, W1.shape[0], dtype=xt.dtype)

        def expert_ffn(w1, bb1, w2, bb2):
            h = jax.nn.gelu(xt @ w1 + bb1, approximate=False)
            return h @ w2 + bb2
        y = jax.vmap(expert_ffn)(W1, b1, W2, b2)
        out = jnp.einsum('te,etd->td', onehot, y)
        out = out * prob_max[:, None]
        return out.reshape(Bb, Ss, Dd)

    def _L2_gnn_ref(x, edge_index, Wl0, bl0, Wr0, g0, b0, Wl1, bl1, Wr1, g1, b1, Wl2, bl2, Wr2, g2, b2, a_prelu):
        import jax, jax.numpy as jnp
        import numpy as np
        N_NODES = 625
        N_EDGES = 10000
        D_IN = 512
        D_HID = 512
        EPS = 1e-05

        def _xavier(key, shape):
            fan_in, fan_out = (shape[1], shape[0])
            limit = np.sqrt(6.0 / (fan_in + fan_out)).astype(np.float32)
            return jax.random.uniform(key, shape, jnp.float32, -limit, limit)

        def _sage_conv(h, src, dst, Wl, bl, Wr):
            msg = h[src]
            s = jax.ops.segment_sum(msg, dst, num_segments=N_NODES)
            cnt = jax.ops.segment_sum(jnp.ones((src.shape[0], 1), h.dtype), dst, num_segments=N_NODES)
            agg = s / jnp.maximum(cnt, 1.0)
            return agg @ Wl.T + bl + h @ Wr.T

        def _layer_norm(h, g, b):
            mu = jnp.mean(h, axis=-1, keepdims=True)
            var = jnp.mean((h - mu) ** 2, axis=-1, keepdims=True)
            return (h - mu) * jax.lax.rsqrt(var + EPS) * g + b

        def _prelu(h, a):
            return jnp.where(h >= 0, h, a * h)
        src, dst = (edge_index[0], edge_index[1])
        params = [(Wl0, bl0, Wr0, g0, b0), (Wl1, bl1, Wr1, g1, b1), (Wl2, bl2, Wr2, g2, b2)]
        h = x
        residual = 0.0
        for Wl, bl, Wr, g, b in params:
            h = residual + _sage_conv(h, src, dst, Wl, bl, Wr)
            h = _layer_norm(h, g, b)
            h = _prelu(h, a_prelu)
            residual = h
        return h

    def _L2_ffn_ref(x, router_w, w1, b1, w2, b2):
        import math
        import jax, jax.numpy as jnp
        import numpy as np
        B, T, H, E, K, F = (4, 128, 512, 8, 2, 64)
        CAP_FACTOR, ROUND_TO = (0.3125, 128)

        def _capacity(num_tokens):
            cap = math.ceil(CAP_FACTOR * num_tokens)
            cap = ROUND_TO * math.ceil(cap / ROUND_TO)
            return max(1, min(cap, num_tokens))
        Bc, Tc, Hc = x.shape
        n = Bc * Tc
        cap = _capacity(n)
        flat = x.reshape(n, Hc)
        logits = (flat @ router_w).astype(jnp.float32)
        sel_logits, expert_idx = jax.lax.top_k(logits, K)
        weights = jax.nn.softmax(sel_logits, axis=-1)
        fe = expert_idx.reshape(-1).astype(jnp.int32)
        fw = weights.reshape(-1)
        tok = jnp.broadcast_to(jnp.arange(n, dtype=jnp.int32)[:, None], expert_idx.shape).reshape(-1)
        order = jnp.argsort(fe)
        se, st, sw = (fe[order], tok[order], fw[order])
        counts = jnp.bincount(se, length=E)
        offsets = (jnp.cumsum(counts) - counts).astype(jnp.int32)
        slot = jnp.arange(se.shape[0], dtype=jnp.int32) - offsets[se]
        keep = slot < cap
        sw = jnp.where(keep, sw, 0.0)
        sx = flat[st]
        expert_inputs = jnp.zeros((E, cap, Hc), flat.dtype).at[se, slot].set(sx, mode='drop')
        h = jax.nn.gelu(jnp.einsum('ech,ehf->ecf', expert_inputs, w1) + b1[:, None, :])
        out = jnp.einsum('ecf,efh->ech', h, w2) + b2[:, None, :]
        clipped = jnp.minimum(counts, cap)
        valid = (jnp.arange(cap, dtype=jnp.int32)[None, :] < clipped[:, None])[..., None]
        out = jnp.where(valid, out, 0)
        slot_c = jnp.minimum(slot, cap - 1)
        gathered = out[se, slot_c] * sw[:, None].astype(out.dtype)
        combined = jnp.zeros((n, Hc), out.dtype).at[st].add(gathered)
        return combined.reshape(Bc, Tc, Hc)

    def _L3_gnn_ref(x, edge_index, edge_attr, W1, b1, W2, b2, W3, b3, W4, b4, gamma, beta):
        import jax, jax.numpy as jnp
        import numpy as np
        N_NODES = 625
        N_EDGES = 10000
        HIDDEN = 512
        EDGE_DIM = 64
        LN_EPS = 1e-05

        def mish(x):
            return x * jnp.tanh(jax.nn.softplus(x))
        src, dst = (edge_index[0], edge_index[1])
        edge_feat = jnp.concatenate([x[src], x[dst], edge_attr], axis=-1)
        h = mish(edge_feat @ W1 + b1)
        messages = mish(h @ W2 + b2)
        agg = jax.ops.segment_sum(messages, dst, num_segments=x.shape[0])
        u = mish(jnp.concatenate([x, agg], axis=-1) @ W3 + b3)
        out = u @ W4 + b4
        y = x + out
        mu = jnp.mean(y, axis=-1, keepdims=True)
        var = jnp.mean(jnp.square(y - mu), axis=-1, keepdims=True)
        return (y - mu) * jax.lax.rsqrt(var + LN_EPS) * gamma + beta

    def _L3_ffn_ref(x, Wg, bg, W1, b1, W2, b2):
        import jax, jax.numpy as jnp
        import numpy as np
        D_MODEL, D_FF, N_EXPERTS, TOP_K = (512, 64, 8, 2)
        B, S, D = x.shape
        xt = x.reshape(B * S, D)
        gate_logits = xt @ Wg + bg
        gate_scores = jax.nn.softmax(gate_logits, axis=-1)
        topk_scores, topk_idx = jax.lax.top_k(gate_scores, TOP_K)
        topk_scores = topk_scores / jnp.sum(topk_scores, axis=-1, keepdims=True)
        combine = jnp.sum(jax.nn.one_hot(topk_idx, N_EXPERTS, dtype=xt.dtype) * topk_scores[..., None], axis=1)
        h = jax.nn.gelu(jnp.einsum('td,edf->etf', xt, W1) + b1[:, None, :], approximate=False)
        expert_out = jnp.einsum('etf,efd->etd', h, W2) + b2[:, None, :]
        out = jnp.einsum('te,etd->td', combine, expert_out)
        return out.reshape(B, S, D)
    edge_index = jnp.stack([src, dst])
    x = x + _L0_gnn_ref(_layernorm(x, axis=-1), src, dst, edge_type_8, L0_gnn_W_self, L0_gnn_b_self, L0_gnn_W_rel, L0_gnn_b_rel)
    x = x + _L0_ffn_ref(_layernorm(x, axis=-1)[None], L0_ffn_wg, L0_ffn_bg, L0_ffn_w1, L0_ffn_w3, L0_ffn_w2)[0]
    x = x + _L1_gnn_ref(_layernorm(x, axis=-1), edge_attr_4, edge_attr_8, edge_index, L1_gnn_W_up0, L1_gnn_W_up1, L1_gnn_W_mlp1, L1_gnn_W_mlp2, L1_gnn_W_mlp3, L1_gnn_W_mlp4, L1_gnn_W_out0, L1_gnn_W_out1)
    x = x + _L1_ffn_ref(_layernorm(x, axis=-1)[None], L1_ffn_Ws, L1_ffn_bs, L1_ffn_W1, L1_ffn_b1, L1_ffn_W2, L1_ffn_b2)[0]
    x = x + _L2_gnn_ref(_layernorm(x, axis=-1), edge_index, L2_gnn_Wl0, L2_gnn_bl0, L2_gnn_Wr0, L2_gnn_g0, L2_gnn_b0, L2_gnn_Wl1, L2_gnn_bl1, L2_gnn_Wr1, L2_gnn_g1, L2_gnn_b1, L2_gnn_Wl2, L2_gnn_bl2, L2_gnn_Wr2, L2_gnn_g2, L2_gnn_b2, L2_gnn_a_prelu)
    x = x + _L2_ffn_ref(_layernorm(x, axis=-1)[None], L2_ffn_router_w, L2_ffn_w1, L2_ffn_b1, L2_ffn_w2, L2_ffn_b2)[0]
    x = x + _L3_gnn_ref(_layernorm(x, axis=-1), edge_index, edge_attr_64, L3_gnn_W1, L3_gnn_b1, L3_gnn_W2, L3_gnn_b2, L3_gnn_W3, L3_gnn_b3, L3_gnn_W4, L3_gnn_b4, L3_gnn_gamma, L3_gnn_beta)
    x = x + _L3_ffn_ref(_layernorm(x, axis=-1)[None], L3_ffn_Wg, L3_ffn_bg, L3_ffn_W1, L3_ffn_b1, L3_ffn_W2, L3_ffn_b2)[0]
    return x

_drawn_inputs = setup_inputs


def setup_inputs(seed=0):
    import zlib

    import numpy as np

    out = dict(_drawn_inputs(seed))
    spreads = {'L0_gnn_b_self': (0.0, 0.1),
     'L0_gnn_b_rel': (0.0, 0.1),
     'L1_ffn_bs': (0.0, 0.8),
     'L1_ffn_b1': (0.0, 0.8),
     'L1_ffn_b2': (0.0, 0.703),
     'L2_gnn_bl0': (0.0, 0.319),
     'L2_gnn_g0': (1.0, 0.2),
     'L2_gnn_b0': (0.0, 0.291),
     'L2_gnn_bl1': (0.0, 0.336),
     'L2_gnn_g1': (1.0, 0.2),
     'L2_gnn_b1': (0.0, 0.286),
     'L2_gnn_bl2': (0.0, 0.33),
     'L2_gnn_g2': (1.0, 0.2),
     'L2_gnn_b2': (0.0, 0.28),
     'L2_ffn_b1': (0.0, 0.599),
     'L2_ffn_b2': (0.0, 0.385),
     'L3_gnn_b1': (0.0, 0.284),
     'L3_gnn_b2': (0.0, 0.278),
     'L3_gnn_b3': (0.0, 2.0),
     'L3_gnn_b4': (0.0, 0.8),
     'L3_gnn_gamma': (1.0, 0.2),
     'L3_gnn_beta': (0.0, 0.305),
     'L3_ffn_bg': (0.0, 0.331)}
    factors = {'edge_attr_64': 3.536,
     'L1_ffn_Ws': 7.02,
     'L1_ffn_W1': 8.0,
     'L1_ffn_W2': 8.0,
     'L3_ffn_b1': 8.0,
     'L3_ffn_b2': 2.962}
    for name, (base, spread) in spreads.items():
        noise = np.random.default_rng([zlib.crc32(name.encode()), seed]).standard_normal(out[name].shape)
        drawn = base * np.exp(spread * noise) if base else spread * noise
        out[name] = jnp.asarray(drawn.astype(out[name].dtype))
    for name, factor in factors.items():
        out[name] = (out[name] * factor).astype(out[name].dtype)
    return out
```

```python
import concourse.bass as bass
from concourse import mybir
from contextlib import ExitStack
import math

F32 = mybir.dt.float32
I32 = mybir.dt.int32
ACT = mybir.ActivationFunctionType
ALU = mybir.AluOpType
X = mybir.AxisListType.X

N, D, E = 625, 512, 20000
P, J = 125, 5
TILES = E // P
U = 4
TURNS = TILES // U
KT = D // 128
R = 8
NE = 8
HALVES = ((0, 313), (313, 312))
EPS = 1e-5
BIG = 3.0e38
SILU_2MOM = 1.679177


class Chain:

    def __init__(self, eng, sem, start=0):
        self.eng, self.sem, self.n = eng, sem, start

    def __call__(self, ins):
        self.n += 1
        ins.then_inc(self.sem, 1)
        self.eng.wait_ge(self.sem, self.n)


class Core:

    def __init__(self, nc, ctx, a):
        self.nc, self.ctx, self.a = nc, ctx, a
        sb = lambda name, shape, dt=F32: ctx.enter_context(nc.sbuf_tensor(name, shape, dt))
        self.x = sb("x", [P, J, D])
        self.xn = sb("xn", [P, J, D])
        self.xnT = sb("xnT", [128, KT, N])
        self.ident = sb("ident", [128, 128])
        self.iota = sb("iota", [P, N])
        self.dst_f = sb("dst_f", [P, TILES])
        self.src_f = sb("src_f", [P, TILES])
        self.src_i = sb("src_i", [P, TILES], I32)
        self.dst_i = sb("dst_i", [P, TILES], I32)
        self.first_i = sb("first_i", [1, TILES], I32)
        self.narrow_i = sb("narrow_i", [1, 1], I32)
        self.dst_w = sb("dst_w", [P, TILES])
        self.ones = sb("ones", [1, 128])
        self.zeros = sb("zeros", [1, D])
        self.comb = sb("comb", [P, J, NE])
        self.half_pi = sb("half_pi", [P, 1])
        self.adjT = sb("adjT", [P, J, N])
        self.tail_row = sb("tail_row", [P, TILES], I32)
        self.head_row = sb("head_row", [P, TILES], I32)
        self.rel_table = nc.dram_tensor("rel_table", (2 * R * N, D), F32).ap()
        self.s0_table = nc.dram_tensor("s0_table", (N, 128), F32).ap()
        self.s1_table = nc.dram_tensor("s1_table", (N, 384), F32).ap()
        self.xs_table = nc.dram_tensor("xs_table", (N, D), F32).ap()
        self.xd_table = nc.dram_tensor("xd_table", (N, D), F32).ap()
        self.norm_uses = 0
        self.gathered = [ctx.enter_context(nc.semaphore(f"gathered{b}")) for b in range(U)]
        self.gather_count = 0
        self.used = []
        self.nsem = {k: ctx.enter_context(nc.semaphore("norm_" + k)) for k in
                     ("stats", "var", "root", "rows_ready", "transposed", "evacuated")}

    def sem(self, name):
        self.used.append(self.nc.alloc_semaphore(name=name))
        return self.used[-1]

    def gathers(self, n):
        before = self.gather_count
        self.gather_count += TURNS * n * 16
        return before

    def recycle(self):
        blk = self.nc.Block()
        with blk:
            @blk.gpsimd
            def _(pool):
                for s in self.used:
                    pool.sem_clear(s)
        for s in self.used:
            self.nc.release_semaphore(s)
        self.used = []


def col(j, w=P):
    return slice(j * w, (j + 1) * w)


def setup(c):
    nc, a = c.nc, c.a
    with ExitStack() as ctx:
        rel_i = ctx.enter_context(nc.sbuf_tensor("rel_i", [P, TILES], I32))
        rel_f = ctx.enter_context(nc.sbuf_tensor("rel_f", [P, TILES], F32))
        T2 = TILES // 2
        sb = lambda n, s, dt=F32: ctx.enter_context(nc.sbuf_tensor(n, s, dt))
        by_tile, by_tile_f = sb("by_tile", [T2, 2, P], I32), sb("by_tile_f", [T2, 2, P])
        span, tile_of = sb("span", [T2, 2, 2]), sb("tile_of", [T2, 2, 2])
        diag, ones80, widest = sb("diag", [T2, 2, T2, 2]), sb("ones80", [T2, P]), sb("widest", [1, 1])
        spread_out = ctx.enter_context(nc.psum_tensor("spread_out", [P, 2, TILES], F32))
        loaded, ready = c.sem("setup_loaded"), c.sem("setup_steps")
        spans_ready, spread = c.sem("spans_ready"), c.sem("spread")
        blk = ctx.enter_context(nc.Block())

        @blk.sync
        def _(sp):
            sp.dma_start(c.src_i[:], a["src"]).then_inc(loaded, 16)
            sp.dma_start(c.dst_i[:], a["dst"]).then_inc(loaded, 16)
            sp.dma_start(rel_i[:], a["rel"]).then_inc(loaded, 16)
            sp.dma_start(c.x[:], a["x"].rearrange("(j p) d -> p j d", p=P)).then_inc(loaded, 16)
            sp.dma_start(c.iota[:], a["iota"].partition_broadcast(P)).then_inc(loaded, 16)
            sp.dma_start(c.ident[:], a["ident"]).then_inc(loaded, 16)
            sp.dma_start(by_tile[:], a["dst_by_tile"]).then_inc(loaded, 16)

        @blk.tensor
        def _(pe):
            pe.wait_ge(spans_ready, 1)
            pe.matmul(spread_out[:, 0, :], ones80[:], diag[:, 0].rearrange("t i h -> t (i h)"), start=True, stop=True)
            pe.matmul(spread_out[:, 1, :], ones80[:], diag[:, 1].rearrange("t i h -> t (i h)"), start=True,
                      stop=True).then_inc(spread, 1)

        @blk.vector
        def _(dve):
            step = Chain(dve, ready)
            step(dve.memset(ones80[:], 1.0))
            step(dve.memset(c.ones[:], 1.0))
            step(dve.memset(c.zeros[:], 0.0))
            step(dve.memset(c.half_pi[:], math.pi / 2))
            dve.wait_ge(loaded, 7 * 16)
            step(dve.tensor_copy(by_tile_f[:], by_tile[:]))
            step(dve.tensor_reduce(span[:, 0, :], by_tile_f[:], X, ALU.min))
            step(dve.tensor_reduce(span[:, 1, :], by_tile_f[:], X, ALU.max))
            step(dve.tensor_scalar(tile_of[:], span[:], float(P), None, ALU.is_ge))
            for k in range(2, J):
                step(dve.scalar_tensor_tensor(tile_of[:], span[:], float(k * P), tile_of[:], ALU.is_ge, ALU.add))
            step(dve.tensor_scalar(tile_of[:, 0, :], tile_of[:, 0, :], float(J - 2), None, ALU.min))
            step(dve.tensor_tensor(tile_of[:, 1, :], tile_of[:, 1, :], tile_of[:, 0, :], ALU.subtract))
            for r in range(2):
                step(dve.tensor_tensor(diag[:, r], c.ident[0:T2, 0:T2].unsqueeze(2).broadcast_to([T2, T2, 2]),
                                       tile_of[:, r, :].unsqueeze(1).broadcast_to([T2, T2, 2]), ALU.mult))
            dve.sem_inc(spans_ready, 1)
            dve.wait_ge(spread, 1)
            step(dve.tensor_copy(c.first_i[:], spread_out[0:1, 0, :]))
            step(dve.tensor_reduce(widest[:], spread_out[0:1, 1, :], X, ALU.max))
            step(dve.tensor_scalar(widest[:], widest[:], 1.0, None, ALU.is_le))
            step(dve.tensor_copy(c.narrow_i[:], widest[:]))
            step(dve.tensor_copy(c.src_f[:], c.src_i[:]))
            step(dve.tensor_copy(c.dst_f[:], c.dst_i[:]))
            step(dve.scalar_tensor_tensor(c.dst_w[:], spread_out[:, 0, :], -float(P), c.dst_f[:], ALU.mult, ALU.add))
            step(dve.tensor_copy(rel_f[:], rel_i[:]))
            step(dve.scalar_tensor_tensor(c.tail_row[:], rel_f[:], float(N), c.dst_f[:], ALU.mult, ALU.add))
            step(dve.scalar_tensor_tensor(rel_f[:], rel_f[:], float(N), c.src_f[:], ALU.mult, ALU.add))
            step(dve.tensor_scalar(c.head_row[:], rel_f[:], float(R * N), None, ALU.add))


def norm(c):
    nc, s = c.nc, c.nsem
    v = c.norm_uses
    c.norm_uses += 1
    with ExitStack() as ctx:
        st = ctx.enter_context(nc.sbuf_tensor(f"bn_st{v}", [P, J, 6], F32))
        mv = ctx.enter_context(nc.sbuf_tensor(f"bn_mv{v}", [P, J, 2], F32))
        tp = ctx.enter_context(nc.psum_tensor(f"norm_tp{v}", [128, J, 512], F32))
        blk = ctx.enter_context(nc.Block())

        @blk.vector
        def _(dve):
            for j in range(J):
                dve.bn_stats(st[:, j, :], c.x[:, j, :]).then_inc(s["stats"], 1)
            for j in range(J):
                dve.wait_ge(s["stats"], (v * J + j + 1))
                dve.bn_aggr(mv[:, j, :], st[:, j, :]).then_inc(s["var"], 1)
            dve.wait_ge(s["var"], v * 7 + 5)
            dve.tensor_scalar(mv[:, :, 1], mv[:, :, 1], EPS, None, ALU.add).then_inc(s["var"], 1)
            dve.wait_ge(s["root"], v + 1)
            dve.reciprocal(mv[:, :, 1], mv[:, :, 1]).then_inc(s["var"], 1)
            dve.wait_ge(s["var"], v * 7 + 7)
            for j in range(J):
                dve.tensor_scalar(c.xn[:, j, :], c.x[:, j, :], mv[:, j, 0:1], mv[:, j, 1:2],
                                  ALU.subtract, ALU.mult).then_inc(s["rows_ready"], 1)

        @blk.scalar
        def _(act):
            act.wait_ge(s["var"], v * 7 + 6)
            act.activation(mv[:, :, 1], mv[:, :, 1], ACT.Sqrt).then_inc(s["root"], 1)
            for j in range(J):
                act.wait_ge(s["transposed"], v * J + j + 1)
                act.activation(c.xnT[:, :, col(j)], tp[:, j, 0:KT * P].rearrange("q (k p) -> q k p", k=KT),
                               ACT.Copy).then_inc(s["evacuated"], 1)

        @blk.tensor
        def _(pe):
            for j in range(J):
                pe.wait_ge(s["rows_ready"], v * J + j + 1)
                for k in range(KT):
                    ins = pe.transpose(tp[:, j, col(k)], c.xn[:, j, col(k, 128)], c.ident[0:P, 0:P])
                ins.then_inc(s["transposed"], 1)


def open_accumulators(pe, c, acc):
    for j in range(J):
        pe.matmul(acc[:, j, :], c.zeros[:, 0:P], c.zeros[:], start=True, stop=False)


def target_hot(dve, c, out, t, narrow):
    if narrow:
        return dve.tensor_scalar(out[:, 0:2 * P], c.iota[:, 0:2 * P], c.dst_w[:, at(t)], None, ALU.is_equal)
    return dve.tensor_scalar(out, c.iota[:], c.dst_f[:, at(t)], None, ALU.is_equal)


def add_targets(pe, c, acc, hot, parts, t, narrow):
    if narrow:
        first = pe.value_load(c.first_i[0:1, at(t)], min_val=0, max_val=J - 2)
        for n in range(2):
            for part in parts:
                ins = pe.matmul(acc[:, bass.ds(first + n, 1), :].rearrange("p a f -> p (a f)"), hot[:, col(n)], part,
                                start=False, stop=False)
        return ins
    for n in range(J):
        for part in parts:
            ins = pe.matmul(acc[:, n, :], hot[:, col(n)], part, start=False, stop=False)
    return ins


def for_width(eng, c, body):
    narrow = eng.value_load(c.narrow_i[0:1, 0:1], min_val=0, max_val=1)
    with eng.If(narrow == 1):
        body(True)
    with eng.Else():
        body(False)


def close_accumulators(pe, c, acc):
    for j in range(J):
        ins = pe.matmul(acc[:, j, :], c.zeros[:, 0:P], c.zeros[:], start=False, stop=True)
    return ins


def rel_tables(c, h_self):
    nc, a = c.nc, c.a
    G = 2 * R // 2
    with ExitStack() as ctx:
        w = ctx.enter_context(nc.sbuf_tensor("relw", [128, 2, KT, D], F32))
        b = ctx.enter_context(nc.sbuf_tensor("relb", [1, 2, D], F32))
        stage = ctx.enter_context(nc.sbuf_tensor("relstage", [P, 2, J, D], F32))
        ps = ctx.enter_context(nc.psum_tensor("relps", [P, J, 512], F32))
        w_loaded = [c.sem(f"relw_loaded{i}") for i in range(2)]
        product, evacuated = c.sem("rel_product"), c.sem("rel_evacuated")
        stored = [c.sem(f"rel_stored{i}") for i in range(2)]
        blk = ctx.enter_context(nc.Block())
        wv = a["W_rel"].rearrange("(g t k q) o -> g t q k o", t=2, k=KT, q=128)
        bv = a["b_rel"].rearrange("(g t) o -> g t o", t=2)
        table = c.rel_table.rearrange("(g t j p) o -> g t p j o", t=2, j=J, p=P)

        @blk.sync
        def _(sp):
            sp.sem_inc(product, 2 * J)
            with sp.Fori(0, G) as g:
                for i in range(2):
                    sp.wait_ge(product, g * (2 * J) + (i + 1) * J)
                    sp.dma_start(w[:, i], wv[g, i]).then_inc(w_loaded[i], 16)
                    sp.dma_start(b[:, i], bv[g, i:i + 1]).then_inc(w_loaded[i], 16)
            sp.wait_ge(product, 2 * G * J + J)
            sp.dma_start(w[:, 0], a["W_self"].rearrange("(k q) o -> q k o", q=128)).then_inc(w_loaded[0], 16)
            sp.dma_start(b[:, 0], a["b_self"]).then_inc(w_loaded[0], 16)

        def products(pe, i, bank_free):
            for j in range(J):
                pe.wait_ge(evacuated, bank_free + j + 1)
                for k in range(KT):
                    pe.matmul(ps[:, j, :], c.xnT[:, k, col(j)], w[:, i, k, :], start=(k == 0), stop=False)
                pe.matmul(ps[:, j, :], c.ones[:, 0:P], b[:, i, :], start=False, stop=True).then_inc(product, 1)

        @blk.tensor
        def _(pe):
            pe.sem_inc(evacuated, J)
            with pe.Fori(0, G) as g:
                for i in range(2):
                    pe.wait_ge(w_loaded[i], g * 32 + 32)
                    products(pe, i, g * (2 * J) + i * J)
            pe.wait_ge(w_loaded[0], G * 32 + 32)
            products(pe, 0, 2 * G * J)

        @blk.scalar
        def _(act):
            for i in range(2):
                act.sem_inc(stored[i], 16)
            with act.Fori(0, G) as g:
                for i in range(2):
                    act.wait_ge(stored[i], g * 16 + 16)
                    for j in range(J):
                        act.wait_ge(product, g * (2 * J) + (i + 2) * J + j + 1)
                        act.activation(stage[:, i, j, :], ps[:, j, :], ACT.Copy).then_inc(evacuated, 1)
                    act.wait_ge(evacuated, g * (2 * J) + (i + 2) * J)
                    act.dma_start(table[g, i], stage[:, i]).then_inc(stored[i], 16)
            for j in range(J):
                act.wait_ge(product, (2 * G + 2) * J + j + 1)
                act.activation(h_self[:, j, :], ps[:, j, :], ACT.Copy).then_inc(evacuated, 1)
            for i in range(2):
                act.wait_ge(stored[i], 16 * (G + 1))


def rel_edges(c, h_self):
    nc = c.nc
    FR = mybir.dt.float32r
    with ExitStack() as ctx:
        sb = lambda n, s, dt=F32: ctx.enter_context(nc.sbuf_tensor(f"re_{n}", s, dt))
        ix = sb("ix", [P, U, 2], I32); rows = sb("rows", [P, U, 2, D])
        high = sb("high", [P, 2, 2, D], FR); low = sb("low", [P, 2, 2, D], FR)
        src_hot = sb("src_hot", [P, 2, N], FR); dst_hot = sb("dst_hot", [P, 2, N], FR)
        acc = ctx.enter_context(nc.psum_tensor("re_acc", [P, J, 512], F32))
        indexed, go = c.sem("re_indexed"), c.sem("re_go")
        gathered, before = c.gathered, c.gathers(2)
        hot_ready, high_ready, low_ready, scattered, steps = (c.sem(f"re_{n}") for n in (
            "hot_ready", "high_ready", "low_ready", "scattered", "steps"))
        blk = ctx.enter_context(nc.Block())

        @blk.gpsimd
        def _(pool):
            pool.sem_inc(low_ready, U)

            def fetch(t, b):
                pool.wait_ge(low_ready, t + 1)
                pool.tensor_copy(ix[:, b, 0:1], c.tail_row[:, at(t)]).then_inc(indexed, 1)
                pool.tensor_copy(ix[:, b, 1:2], c.head_row[:, at(t)]).then_inc(indexed, 1)
                pool.wait_ge(indexed, t * 2 + 2)
                pool.sem_inc(go, 1)
                for h in range(2):
                    pool.indirect_dma_start(rows[:, b, h, :], None, c.rel_table, bass.IndirectOffsetOnAxis(
                        ap=ix[:, b, h:h + 1], axis=0)).then_inc(gathered[b], 16)
            rounds(pool, [(fetch, 0)])

        @blk.scalar
        def _(act):
            def split_high(t, b):
                act.wait_ge(gathered[b], filled(t, b, 2) + before)
                act.wait_ge(scattered, t + 1)
                act.activation(high[:, b % 2], rows[:, b], ACT.Copy).then_inc(high_ready, 1)
            rounds(act, [(split_high, 0)])

        @blk.vector
        def _(dve):
            def hots(narrow):
                def stage(t, b):
                    dve.wait_ge(scattered, t + 1)
                    dve.tensor_scalar(src_hot[:, b % 2, :], c.iota[:], c.src_f[:, at(t)], None,
                                      ALU.is_equal).then_inc(hot_ready, 1)
                    target_hot(dve, c, dst_hot[:, b % 2, :], t, narrow).then_inc(hot_ready, 1)
                return stage

            def split_low(t, b):
                dve.wait_ge(high_ready, t + 1)
                dve.tensor_tensor(low[:, b % 2], rows[:, b], high[:, b % 2].bitcast(F32), ALU.subtract).then_inc(low_ready, 1)

            for_width(dve, c, lambda narrow: rounds(dve, [(hots(narrow), 0), (split_low, 0)]))
            dve.wait_ge(scattered, TILES + 2 + 1)
            step = Chain(dve, steps)
            for j in range(J):
                step(dve.tensor_tensor(h_self[:, j, :], h_self[:, j, :], acc[:, j, :], ALU.add))
                dve.scalar_tensor_tensor(c.x[:, j, :], h_self[:, j, :], 0.0, c.x[:, j, :], ALU.max, ALU.add)

        @blk.tensor
        def _(pe):
            def scatter(narrow):
                def stage(t, b):
                    p = b % 2
                    pe.wait_ge(hot_ready, t * 2 + 2)
                    pe.wait_ge(high_ready, t + 1)
                    pe.wait_ge(low_ready, t + U + 1)
                    for j in range(J):
                        for part in (high, low):
                            pe.matmul(acc[:, j, :], src_hot[:, p, col(j)], part[:, p, 0, :], start=False, stop=False)
                    add_targets(pe, c, acc, dst_hot[:, p, :], [high[:, p, 1, :], low[:, p, 1, :]], t,
                                narrow).then_inc(scattered, 1)
                return stage

            pe.sem_inc(scattered, 2)
            open_accumulators(pe, c, acc)
            for_width(pe, c, lambda narrow: rounds(pe, [(scatter(narrow), 0)]))
            close_accumulators(pe, c, acc).then_inc(scattered, 1)


class Router:

    def __init__(self, c, ctx, tag):
        sb = lambda n, shape: ctx.enter_context(c.nc.sbuf_tensor(f"{tag}_{n}", shape, F32))
        self.c = c
        self.s = sb("s", [P, J, NE])
        self.e = sb("e", [P, J, NE])
        self.t = sb("t", [P, J, NE])
        self.mk = sb("mk", [P, J, NE])
        self.kp = sb("kp", [P, J, NE])
        self.oh1 = sb("oh1", [P, J, NE])
        self.oh2 = sb("oh2", [P, J, NE])
        self.m1, self.m2 = sb("m1", [P, J]), sb("m2", [P, J])
        self.r = sb("r", [P, J])
        self.ids = c.iota[:, 0:NE].unsqueeze(1).broadcast_to([P, J, NE])
        self.steps = c.sem(f"{tag}_steps")
        self.exps = c.sem(f"{tag}_exps")

    def wide(self, m):
        return m[:].unsqueeze(2).broadcast_to([P, J, NE])

    def first_max(self, dve, step, s, m, oh):
        t = self.t
        step(dve.tensor_reduce(m[:], s[:], X, ALU.max))
        step(dve.tensor_tensor(t[:], s[:], self.wide(m), ALU.is_equal))
        step(dve.scalar_tensor_tensor(t[:], t[:], -float(NE), self.ids, ALU.mult, ALU.add))
        step(dve.tensor_reduce(self.r[:], t[:], X, ALU.min))
        step(dve.tensor_tensor(oh[:], t[:], self.wide(self.r), ALU.is_equal))

    def exp_of(self, dve, step, s, m, n):
        step(dve.tensor_tensor(self.e[:], s[:], self.wide(m), ALU.subtract))
        dve.wait_ge(self.exps, n)

    def normalise(self, dve, step, out):
        step(dve.tensor_reduce(self.r[:], self.e[:], X, ALU.add))
        step(dve.reciprocal(self.r[:], self.r[:]))
        step(dve.tensor_tensor(out[:], self.e[:], self.wide(self.r), ALU.mult))


def route(c, dve, q, kind, logits, lg_ready, marks, capacity=None):
    step = Chain(dve, q.steps)
    dve.wait_ge(lg_ready, 1)
    step(dve.tensor_copy(q.s[:], logits))
    n_exp = [0]

    def exponential(s, m):
        step(dve.tensor_tensor(q.e[:], s[:], q.wide(m), ALU.subtract))
        marks.append(step.n)
        n_exp[0] += 1
        dve.wait_ge(q.exps, n_exp[0])

    def softmax():
        step(dve.tensor_reduce(q.m1[:], q.s[:], X, ALU.max))
        exponential(q.s, q.m1)
        q.normalise(dve, step, q.s)

    def second_max():
        step(dve.scalar_tensor_tensor(q.mk[:], q.oh1[:], -BIG, q.s[:], ALU.mult, ALU.add))
        q.first_max(dve, step, q.mk, q.m2, q.oh2)

    def keep_near(m):
        step(dve.tensor_tensor(q.t[:], q.s[:], q.wide(m), ALU.max))
        step(dve.reciprocal(q.t[:], q.t[:]))
        step(dve.tensor_tensor(q.kp[:], q.wide(m), q.s[:], ALU.subtract))
        step(dve.tensor_tensor(q.kp[:], q.kp[:], q.t[:], ALU.mult))
        step(dve.tensor_scalar(q.kp[:], q.kp[:], 0.02, None, ALU.is_le))

    def masked_share(oh, m):
        exponential(q.s, m)
        step(dve.tensor_tensor(q.e[:], q.e[:], q.kp[:], ALU.mult))
        step(dve.tensor_reduce(q.r[:], q.e[:], X, ALU.add))
        step(dve.reciprocal(q.r[:], q.r[:]))
        step(dve.tensor_tensor(q.e[:], q.e[:], oh[:], ALU.mult))
        step(dve.tensor_tensor(q.e[:], q.e[:], q.wide(q.r), ALU.mult))

    if kind == "sparsemixer":
        softmax()
        q.first_max(dve, step, q.s, q.m1, q.oh1)
        keep_near(q.m1)
        masked_share(q.oh1, q.m1)
        step(dve.tensor_copy(c.comb[:], q.e[:]))
        second_max()
        keep_near(q.m2)
        step(dve.scalar_tensor_tensor(q.t[:], q.oh1[:], 0.0, q.kp[:], ALU.is_equal, ALU.mult))
        step(dve.tensor_copy(q.kp[:], q.t[:]))
        masked_share(q.oh2, q.m2)
        step(dve.tensor_tensor(c.comb[:], c.comb[:], q.e[:], ALU.add))
    elif kind == "switch":
        softmax()
        q.first_max(dve, step, q.s, q.m1, q.oh1)
        step(dve.tensor_tensor(c.comb[:], q.s[:], q.oh1[:], ALU.mult))
    elif kind == "top2_scores":
        softmax()
        q.first_max(dve, step, q.s, q.m1, q.oh1)
        second_max()
        step(dve.tensor_tensor(q.t[:], q.oh1[:], q.oh2[:], ALU.add))
        step(dve.tensor_tensor(q.e[:], q.s[:], q.t[:], ALU.mult))
        q.normalise(dve, step, c.comb)
    elif kind == "top2_capacity":
        q.first_max(dve, step, q.s, q.m1, q.oh1)
        second_max()
        step(dve.tensor_tensor(q.mk[:], q.oh1[:], q.oh2[:], ALU.add))
        q.mask_step = step.n
        exponential(q.s, q.m1)
        step(dve.tensor_tensor(q.e[:], q.e[:], q.mk[:], ALU.mult))
        q.normalise(dve, step, c.comb)
        ranks, rank_ready, cap = capacity
        dve.wait_ge(rank_ready, 1)
        step(dve.scalar_tensor_tensor(c.comb[:], ranks, float(cap), c.comb[:], ALU.is_lt, ALU.mult))
    return step


def ffn_small(c, tag, kind, gelu):
    nc, a = c.nc, c.a
    norm(c)
    with ExitStack() as ctx:
        sb = lambda n, s, dt=F32: ctx.enter_context(nc.sbuf_tensor(f"{tag}_{n}", s, dt))
        pb = lambda n, s: ctx.enter_context(nc.psum_tensor(f"{tag}_{n}", s, F32))
        q = Router(c, ctx, tag)
        wg = sb("wg", [128, KT, NE]); bg = sb("bg", [1, NE])
        w1 = sb("w1", [128, KT, D]); b1 = sb("b1", [128, KT])
        w2 = sb("w2", [128, KT, D]); b2 = sb("b2", [NE, D])
        spread = sb("spread", [NE, D]); earlier = sb("earlier", [P, P]); every = sb("every", [P, P])
        hT = sb("hT", [128, KT, N]); combT = sb("combT", [NE, N])
        small = pb("small", [128, 512])
        lg = small[0:P, 0:J * NE].rearrange("p (j e) -> p j e", e=NE)
        ranks = small[0:P, 64:64 + J * NE].rearrange("p (j e) -> p j e", e=NE)
        big = pb("big", [128, 4, 512])
        ctp = pb("ctp", [NE, 2, 512])
        router_loaded, up_loaded, down_loaded = (c.sem(f"{tag}_{n}_loaded") for n in ("router", "up", "down"))
        lg_ready, rank_ready = c.sem(f"{tag}_lg_ready"), c.sem(f"{tag}_rank_ready")
        consts, up_ready, gelu_done = c.sem(f"{tag}_consts"), c.sem(f"{tag}_up_ready"), c.sem(f"{tag}_gelu_done")
        ct_ready, ct_copied = c.sem(f"{tag}_ct_ready"), c.sem(f"{tag}_ct_copied")
        spread_ready, scaled = c.sem(f"{tag}_spread_ready"), c.sem(f"{tag}_scaled")
        down_ready, added = c.sem(f"{tag}_down_ready"), c.sem(f"{tag}_added")
        blk = ctx.enter_context(nc.Block())
        marks = []

        @blk.sync
        def _(sp):
            sp.dma_start(wg[:], a[f"{tag}_wg"].rearrange("(k q) e -> q k e", q=128)).then_inc(router_loaded, 16)
            sp.dma_start(bg[:], a[f"{tag}_bg"]).then_inc(router_loaded, 16)
            sp.dma_start(w1[:], a[f"{tag}_w1"].rearrange("(k q) f -> q k f", q=128)).then_inc(up_loaded, 16)
            sp.dma_start(b1[:], a[f"{tag}_b1"]).then_inc(up_loaded, 16)
            sp.dma_start(w2[:], a[f"{tag}_w2"].rearrange("(k q) f -> q k f", q=128)).then_inc(down_loaded, 16)
            sp.dma_start(b2[:], a[f"{tag}_b2"]).then_inc(down_loaded, 16)
            sp.dma_start(spread[:], a["spread"]).then_inc(down_loaded, 16)
            sp.dma_start(earlier[:], a["earlier"]).then_inc(down_loaded, 16)

        @blk.vector
        def _(dve):
            dve.memset(every[:], 1.0).then_inc(consts, 1)
            step = route(c, dve, q, kind, lg, lg_ready, marks, (ranks, rank_ready, CAPACITY))
            q.comb_step = step.n
            for n in range(2 * KT):
                k, (h0, hn) = n // 2, HALVES[n % 2]
                dve.wait_ge(gelu_done, n + 1)
                dve.wait_ge(spread_ready, n + 1)
                dve.tensor_tensor(hT[:, k, h0:h0 + hn], hT[:, k, h0:h0 + hn], big[:, n % 4, 0:hn],
                                  ALU.mult).then_inc(scaled, 1)
            for j in range(J):
                dve.wait_ge(down_ready, j + 1)
                dve.tensor_tensor(c.x[:, j, :], c.x[:, j, :], big[0:P, j % 4, :], ALU.add).then_inc(added, 1)

        @blk.scalar
        def _(act):
            for i, m in enumerate(marks[:]):
                act.wait_ge(q.steps, m)
                act.activation(q.e[:], q.e[:], ACT.Exp).then_inc(q.exps, 1)
            act.wait_ge(up_loaded, 32)
            for n in range(2 * KT):
                k, (h0, hn) = n // 2, HALVES[n % 2]
                act.wait_ge(up_ready, n + 1)
                act.activation(hT[:, k, h0:h0 + hn], big[:, n % 4, 0:hn], gelu, bias=b1[:, k:k + 1]).then_inc(gelu_done, 1)
            for i, (first, n) in enumerate(((0, 4), (4, 1))):
                act.wait_ge(ct_ready, i + 1)
                act.activation(combT[:, first * P:(first + n) * P], ctp[:, i, 0:n * P], ACT.Copy).then_inc(ct_copied, 1)

        @blk.tensor
        def _(pe):
            pe.wait_ge(router_loaded, 32)
            for j in range(J):
                for k in range(KT):
                    pe.matmul(lg[:, j, :], c.xnT[:, k, col(j)], wg[:, k, :], start=(k == 0), stop=False)
                ins = pe.matmul(lg[:, j, :], c.ones[:, 0:P], bg[:], start=False, stop=True)
            ins.then_inc(lg_ready, 1)
            pe.wait_ge(up_loaded, 32)
            for n in range(2 * KT):
                m, (h0, hn) = n // 2, HALVES[n % 2]
                if n >= 4:
                    pe.wait_ge(gelu_done, n - 3)
                for k in range(KT):
                    ins = pe.matmul(big[:, n % 4, 0:hn], w1[:, k, col(m, 128)], c.xnT[:, k, h0:h0 + hn],
                                    start=(k == 0), stop=(k == KT - 1))
                ins.then_inc(up_ready, 1)
            pe.wait_ge(down_loaded, 64)
            if kind == "top2_capacity":
                pe.wait_ge(q.steps, q.mask_step)
                pe.wait_ge(consts, 1)
                for j in range(J):
                    for i in range(j):
                        pe.matmul(ranks[:, j, :], every[:], q.mk[:, i, :], start=(i == 0), stop=False)
                    ins = pe.matmul(ranks[:, j, :], earlier[:], q.mk[:, j, :], start=(j == 0), stop=True)
                ins.then_inc(rank_ready, 1)
            pe.wait_ge(q.steps, q.comb_step)
            for j in range(J):
                ins = pe.transpose(ctp[:, j // 4, col(j % 4)], c.comb[:, j, :], c.ident[0:P, 0:P])
                if j >= 3:
                    ins.then_inc(ct_ready, 1)
            pe.wait_ge(ct_copied, 2)
            for n in range(2 * KT):
                k, (h0, hn) = n // 2, HALVES[n % 2]
                if n < 4:
                    pe.wait_ge(gelu_done, n + 5)
                else:
                    pe.wait_ge(scaled, n - 3)
                pe.matmul(big[:, n % 4, 0:hn], spread[:, col(k, 128)], combT[:, h0:h0 + hn],
                          start=True, stop=True).then_inc(spread_ready, 1)
            pe.wait_ge(scaled, 2 * KT)
            for j in range(J):
                if j >= 4:
                    pe.wait_ge(added, j - 3)
                for k in range(KT):
                    pe.matmul(big[0:P, j % 4, :], hT[:, k, col(j)], w2[:, k, :], start=(k == 0), stop=False)
                pe.matmul(big[0:P, j % 4, :], combT[:, col(j)], b2[:], start=False, stop=True).then_inc(down_ready, 1)


CAPACITY = min(128 * math.ceil(math.ceil(0.3125 * N) / 128), N)


def ffn_large(c):
    nc, a = c.nc, c.a
    FM = 8
    norm(c)
    with ExitStack() as ctx:
        sb = lambda n, s, dt=F32: ctx.enter_context(nc.sbuf_tensor(f"fl_{n}", s, dt))
        pb = lambda n, s: ctx.enter_context(nc.psum_tensor(f"fl_{n}", s, F32))
        q = Router(c, ctx, "fl")
        wg = sb("wg", [128, KT, NE]); bg = sb("bg", [1, NE])
        w1 = sb("w1", [128, KT, 1024]); w3 = sb("w3", [128, KT, 1024])
        w2 = sb("w2", [128, FM, D])
        g = sb("g", [128, 2, 313]); hT = sb("hT", [128, FM, N])
        small = pb("small", [128, 512])
        lg = small[0:P, 0:J * NE].rearrange("p (j e) -> p j e", e=NE)
        up = pb("up", [128, 2, 2, 512])
        down = pb("down", [P, 2, 512])
        router_loaded, up_loaded, down_loaded = c.sem("fl_router_loaded"), c.sem("fl_up_loaded"), c.sem("fl_down_loaded")
        lg_ready, up_ready, gelu_done = c.sem("fl_lg_ready"), c.sem("fl_up_ready"), c.sem("fl_gelu_done")
        h_ready, down_ready, added = c.sem("fl_h_ready"), c.sem("fl_down_ready"), c.sem("fl_added")
        blk = ctx.enter_context(nc.Block())
        marks = []
        NH = 2 * FM

        @blk.sync
        def _(sp):
            sp.dma_start(wg[:], a["fl_wg"].rearrange("(k q) e -> q k e", q=128)).then_inc(router_loaded, 16)
            sp.dma_start(bg[:], a["fl_bg"]).then_inc(router_loaded, 16)
            sp.sem_inc(h_ready, NH)
            sp.sem_inc(down_ready, J)
            w1v = a["fl_w1"].rearrange("e (k q) f -> e q k f", q=128)
            w3v = a["fl_w3"].rearrange("e (k q) f -> e q k f", q=128)
            w2v = a["fl_w2"].rearrange("e (k q) f -> e q k f", q=128)
            with sp.Fori(0, NE) as e:
                sp.wait_ge(h_ready, e * NH + NH)
                sp.dma_start(w1[:], w1v[e]).then_inc(up_loaded, 16)
                sp.dma_start(w3[:], w3v[e]).then_inc(up_loaded, 16)
                sp.wait_ge(down_ready, e * J + J)
                sp.dma_start(w2[:], w2v[e]).then_inc(down_loaded, 16)

        @blk.vector
        def _(dve):
            route(c, dve, q, "sparsemixer", lg, lg_ready, marks)
            with dve.Fori(0, NE) as e:
                for n in range(NH):
                    m, (h0, hn) = n // 2, HALVES[n % 2]
                    if n == 0:
                        dve.wait_ge(down_ready, e * J + J)
                    dve.wait_ge(gelu_done, e * NH + n + 1)
                    dve.tensor_tensor(hT[:, m, h0:h0 + hn], g[:, n % 2, 0:hn], up[:, 1, n % 2, 0:hn],
                                      ALU.mult).then_inc(h_ready, 1)
                for j in range(J):
                    dve.wait_ge(down_ready, e * J + J + j + 1)
                    dve.scalar_tensor_tensor(c.x[:, j, :], down[:, j % 2, :], c.comb[:, j, bass.ds(e, 1)],
                                             c.x[:, j, :], ALU.mult, ALU.add).then_inc(added, 1)

        @blk.scalar
        def _(act):
            for m in marks:
                act.wait_ge(q.steps, m)
                act.activation(q.e[:], q.e[:], ACT.Exp).then_inc(q.exps, 1)
            with act.Fori(0, NE) as e:
                for n in range(NH):
                    m, (h0, hn) = n // 2, HALVES[n % 2]
                    act.wait_ge(up_ready, e * NH + n + 1)
                    act.wait_ge(h_ready, e * NH + NH + n - 1)
                    act.activation(g[:, n % 2, 0:hn], up[:, 0, n % 2, 0:hn], ACT.Gelu).then_inc(gelu_done, 1)

        @blk.tensor
        def _(pe):
            pe.wait_ge(router_loaded, 32)
            for j in range(J):
                for k in range(KT):
                    pe.matmul(lg[:, j, :], c.xnT[:, k, col(j)], wg[:, k, :], start=(k == 0), stop=False)
                ins = pe.matmul(lg[:, j, :], c.ones[:, 0:P], bg[:], start=False, stop=True)
            ins.then_inc(lg_ready, 1)
            pe.sem_inc(added, 2)
            with pe.Fori(0, NE) as e:
                pe.wait_ge(up_loaded, e * 32 + 32)
                for n in range(NH):
                    m, (h0, hn) = n // 2, HALVES[n % 2]
                    pe.wait_ge(h_ready, e * NH + NH + n - 1)
                    for s, w in enumerate((w1, w3)):
                        for k in range(KT):
                            ins = pe.matmul(up[:, s, n % 2, 0:hn], w[:, k, col(m, 128)], c.xnT[:, k, h0:h0 + hn],
                                            start=(k == 0), stop=(k == KT - 1))
                    ins.then_inc(up_ready, 1)
                pe.wait_ge(down_loaded, e * 16 + 16)
                pe.wait_ge(h_ready, e * NH + 2 * NH)
                for j in range(J):
                    pe.wait_ge(added, e * J + j + 1)
                    for m in range(FM):
                        ins = pe.matmul(down[:, j % 2, :], hT[:, m, col(j)], w2[:, m, :], start=(m == 0), stop=(m == FM - 1))
                    ins.then_inc(down_ready, 1)


LAST = 4


class Tile:

    def __init__(self, u, off):
        self.u, self.off = u, off

    def __add__(self, n):
        return self.u * U + (self.off + n)

    def __mul__(self, n):
        return Scaled(self.u * (U * n), self.off * n)


class Scaled:
    def __init__(self, v, off):
        self.v, self.off = v, off

    def __add__(self, n):
        return self.v + (self.off + n)


def rounds(eng, stages):
    for r in range(LAST):
        for stage, lag in stages:
            if r >= lag:
                stage(r - lag, (r - lag) % U)
    with eng.Fori(0, (TILES - LAST) // U) as u:
        for b in range(U):
            for stage, lag in stages:
                stage(Tile(u, LAST + b - lag), (b - lag) % U)
    for r in range(TILES, TILES + LAST):
        for stage, lag in stages:
            if r - lag < TILES:
                stage(r - lag, (r - lag) % U)


def filled(t, b, n=1):
    if isinstance(t, int):
        return (t // U + 1) * 16 * n
    return t.u * (16 * n) + (t.off // U + 1) * 16 * n


def half(b):
    return slice(64 * (b % 2), 64 * (b % 2) + 64)


def at(t):
    return bass.ds(t + 0, 1)


def mace_nodes(c):
    nc, a = c.nc, c.a
    norm(c)
    with ExitStack() as ctx:
        sb = lambda n, s: ctx.enter_context(nc.sbuf_tensor(f"mn_{n}", s, F32))
        w = sb("w", [128, 2, 128]); vT = sb("vT", [128, 3, N]); stage = sb("stage", [P, J, D])
        tp = ctx.enter_context(nc.psum_tensor("mn_tp", [128, 2, 512], F32))
        ps = ctx.enter_context(nc.psum_tensor("mn_ps", [P, 2, 512], F32))
        loaded, turned, copied = c.sem("mn_loaded"), c.sem("mn_turned"), c.sem("mn_copied")
        product, staged, stored = c.sem("mn_product"), c.sem("mn_staged"), c.sem("mn_stored")
        blk = ctx.enter_context(nc.Block())

        @blk.sync
        def _(sp):
            sp.dma_start(w[:, 0], a["W_up0"]).then_inc(loaded, 16)
            sp.dma_start(w[:, 1], a["W_up1"]).then_inc(loaded, 16)
            sp.wait_ge(staged, J)
            sp.dma_start(c.s0_table.rearrange("(j p) f -> p j f", p=P), stage[:, :, 0:128]).then_inc(stored, 16)
            sp.dma_start(c.s1_table.rearrange("(j p) f -> p j f", p=P), stage[:, :, 128:512]).then_inc(stored, 16)
            sp.wait_ge(stored, 32)

        @blk.tensor
        def _(pe):
            for j in range(J):
                if j >= 2:
                    pe.wait_ge(copied, j - 1)
                v = c.xn[:, j, 128:512].rearrange("p (u m) -> p m u", m=3)
                for m in range(3):
                    ins = pe.transpose(tp[:, j % 2, col(m)], v[:, m, :], c.ident[0:P, 0:P])
                ins.then_inc(turned, 1)
            pe.wait_ge(loaded, 32)
            for j in range(J):
                pe.wait_ge(copied, j + 1)
                if j >= 2:
                    pe.wait_ge(staged, j - 1)
                pe.matmul(ps[:, j % 2, 0:128], c.xnT[:, 0, col(j)], w[:, 0], start=True, stop=True)
                for m in range(3):
                    ins = pe.matmul(ps[:, j % 2, col(m + 1, 128)], vT[:, m, col(j)], w[:, 1], start=True, stop=True)
                ins.then_inc(product, 1)

        @blk.scalar
        def _(act):
            for j in range(J):
                act.wait_ge(turned, j + 1)
                act.activation(vT[:, :, col(j)], tp[:, j % 2, 0:3 * P].rearrange("q (m p) -> q m p", m=3),
                               ACT.Copy).then_inc(copied, 1)

        @blk.vector
        def _(dve):
            for j in range(J):
                dve.wait_ge(product, j + 1)
                dve.tensor_scalar(stage[:, j, :], ps[:, j % 2, :], 128.0 ** -0.5, None, ALU.mult).then_inc(staged, 1)


def mace_mlp(c, h3T):
    nc, a = c.nc, c.a
    CH = U * P
    G = E // 2 // CH // 2
    with ExitStack() as ctx:
        sb = lambda n, s: ctx.enter_context(nc.sbuf_tensor(f"mm_{n}", s, F32))
        f = sb("f", [16, 2, CH]); w1 = sb("w1", [16, 128]); w2 = sb("w2", [128, 128]); w3 = sb("w3", [128, 128])
        h = sb("h", [128, 2, 2, CH])
        ps = ctx.enter_context(nc.psum_tensor("mm_ps", [128, 2, 3, 512], F32))
        cleared, w_loaded, f_loaded = c.sem("mm_cleared"), c.sem("mm_w_loaded"), [c.sem(f"mm_f_loaded{i}") for i in range(2)]
        product, active = [[c.sem(f"mm_{n}{i}") for i in range(2)] for n in ("product", "active")]
        blk = ctx.enter_context(nc.Block())

        @blk.vector
        def _(dve):
            for t in (w1, w2, w3):
                dve.memset(t[:], 0.0).then_inc(cleared, 1)

        @blk.sync
        def _(sp):
            sp.wait_ge(cleared, 3)
            for t, n, k in ((w1, "W_mlp1", 8), (w2, "W_mlp2", 64), (w3, "W_mlp3", 64)):
                for i in range(2):
                    sp.dma_start(t[i * k:(i + 1) * k, col(i, 64)], a[n]).then_inc(w_loaded, 16)
            for i in range(2):
                sp.sem_inc(product[i], 3)
            with sp.Fori(0, G) as g:
                for i in range(2):
                    sp.wait_ge(product[i], g * 3 + 1)
                    sp.dma_start(f[:, i, :], a["ea8T"][:, bass.ds(g * (2 * CH) + i * CH, CH)]).then_inc(f_loaded[i], 16)

        @blk.tensor
        def _(pe):
            pe.wait_ge(w_loaded, 96)
            for i in range(2):
                pe.sem_inc(active[i], 3)
            with pe.Fori(0, G) as g:
                for n, w in enumerate((w1, w2, w3)):
                    for i in range(2):
                        if n == 0:
                            pe.wait_ge(f_loaded[i], g * 16 + 16)
                        pe.wait_ge(active[i], g * 3 + 3 + n)
                        rhs = f[:, i, :] if n == 0 else h[:, i, n - 1, :]
                        pe.matmul(ps[:, i, n, 0:CH], w[:], rhs, start=True, stop=True).then_inc(product[i], 1)

        @blk.scalar
        def _(act):
            with act.Fori(0, G) as g:
                for n in range(3):
                    for i in range(2):
                        act.wait_ge(product[i], g * 3 + 4 + n)
                        out = h[:, i, n, :] if n < 2 else h3T[:, bass.ds(g * (2 * CH) + i * CH, CH)]
                        scale = 8.0 ** -0.5 if n == 0 else SILU_2MOM / 8.0
                        act.activation(out, ps[:, i, n, 0:CH], ACT.Silu, scale=scale).then_inc(active[i], 1)


def mace_edges(c, h3T, vector, agg):
    nc, a = c.nc, c.a
    tag = "mv" if vector else "ms"
    W = 384 if vector else 128
    table = c.s1_table if vector else c.s0_table
    K = SILU_2MOM / 8.0
    with ExitStack() as ctx:
        sb = lambda n, s, dt=F32: ctx.enter_context(nc.sbuf_tensor(f"{tag}_{n}", s, dt))
        ix = sb("ix", [P, U], I32); rows = sb("rows", [P, U, W]); hs = sb("hs", [128, U, P])
        w4 = sb("w4", [128, 256]); ea = sb("ea", [P, TILES, 4])
        hot = sb("hot", [P, U, N]); msg = sb("msg", [P, U, D]); part = sb("part", [P, U, 256])
        acc = ctx.enter_context(nc.psum_tensor(f"{tag}_acc", [P, J, 512], F32))
        tpw = ctx.enter_context(nc.psum_tensor(f"{tag}_tpw", [P, 2, 512], F32))
        loaded, indexed, go, h_staged = (c.sem(f"{tag}_{n}") for n in ("loaded", "indexed", "go", "h_staged"))
        gathered, before = c.gathered, c.gathers(1)
        w_ready, w_used, hot_ready, msg_ready, scattered, inner, copied = (c.sem(f"{tag}_{n}") for n in (
            "w_ready", "w_used", "hot_ready", "msg_ready", "scattered", "inner", "copied"))
        blk = ctx.enter_context(nc.Block())

        @blk.sync
        def _(sp):
            for i in range(2):
                sp.dma_start(w4[col(i, 64)], a["W_mlp4"][:, 256:512] if vector else a["W_mlp4"][:, 0:256]).then_inc(loaded, 16)
            sp.dma_start(ea[:], a["ea4"]).then_inc(loaded, 16)

        @blk.gpsimd
        def _(pool):
            def fetch(t, b):
                pool.wait_ge(scattered, t + 1)
                pool.tensor_copy(ix[:, b:b + 1], c.src_i[:, at(t)]).then_inc(indexed, 1)
                pool.wait_ge(indexed, t + 1)
                pool.sem_inc(go, 1)
                pool.indirect_dma_start(rows[:, b, :], None, table, bass.IndirectOffsetOnAxis(
                    ap=ix[:, b:b + 1], axis=0)).then_inc(gathered[b], 16)
            rounds(pool, [(fetch, 0)])

        @blk.tensor
        def _(pe):
            def weights(t, b):
                pe.wait_ge(h_staged, t + 1)
                pe.wait_ge(w_used, t + 1)
                pe.matmul(tpw[:, b % 2, 0:256], hs[half(b), b, :], w4[half(b), :], start=True, stop=True).then_inc(w_ready, 1)

            def scatter(narrow):
                def stage(t, b):
                    pe.wait_ge(hot_ready, t + 1)
                    pe.wait_ge(msg_ready, t + 1)
                    add_targets(pe, c, acc, hot[:, b, :], [msg[:, b, :]], t, narrow).then_inc(scattered, 1)
                return stage

            pe.sem_inc(scattered, U)
            pe.sem_inc(w_used, 2)
            open_accumulators(pe, c, acc)
            pe.wait_ge(loaded, 48)
            for_width(pe, c, lambda narrow: rounds(pe, [(weights, 0), (scatter(narrow), 1)]))
            close_accumulators(pe, c, acc).then_inc(scattered, 1)

        @blk.vector
        def _(dve):
            def prepare(narrow):
                def stage(t, b):
                    dve.wait_ge(scattered, t + 1)
                    target_hot(dve, c, hot[:, b, :], t, narrow).then_inc(hot_ready, 1)
                return stage

            def gathered_rows(t, b):
                dve.wait_ge(gathered[b], filled(t, b) + before)

            def scalar_messages(t, b):
                gathered_rows(t, b)
                dve.wait_ge(w_ready, t + 1)
                v = part[:, b, :].rearrange("p (g f) -> p g f", g=2)
                dve.scalar_tensor_tensor(v, tpw[:, b % 2, 0:256].rearrange("p (g f) -> p g f", g=2), K,
                                         rows[:, b, :].unsqueeze(1).broadcast_to([P, 2, 128]),
                                         ALU.mult, ALU.mult).then_inc(w_used, 1)
                dve.wait_ge(w_used, t + 3)
                dve.tensor_scalar(msg[:, b, 0:128], v[:, 0, :], ea[:, at(t), 0], None, ALU.mult).then_inc(inner, 1)
                dve.tensor_tensor(msg[:, b, 128:512].rearrange("p (m f) -> p m f", m=3),
                                  v[:, 1:2, :].broadcast_to([P, 3, 128]),
                                  ea[:, at(t), 1:4].rearrange("p a m -> p (a m)").unsqueeze(2).broadcast_to([P, 3, 128]),
                                  ALU.mult).then_inc(msg_ready, 1)

            def vector_messages(t, b):
                gathered_rows(t, b)
                dve.wait_ge(w_ready, t + 1)
                s1 = rows[:, b, :].rearrange("p (m f) -> p m f", m=3)
                dot, w3y = part[:, b, 0:128], part[:, b, 128:256]
                dve.tensor_scalar(w3y, tpw[:, b % 2, 0:128], ea[:, at(t), 0], K, ALU.mult, ALU.mult).then_inc(inner, 1)
                dve.tensor_scalar(dot, s1[:, 0, :], ea[:, at(t), 1], None, ALU.mult).then_inc(inner, 1)
                dve.wait_ge(inner, t * 4 + 2)
                dve.scalar_tensor_tensor(dot, s1[:, 1, :], ea[:, at(t), 2], dot, ALU.mult, ALU.add).then_inc(inner, 1)
                dve.tensor_tensor(msg[:, b, 128:512].rearrange("p (m f) -> p m f", m=3), s1,
                                  w3y.unsqueeze(1).broadcast_to([P, 3, 128]), ALU.mult)
                dve.wait_ge(inner, t * 4 + 3)
                dve.scalar_tensor_tensor(dot, s1[:, 2, :], ea[:, at(t), 3], dot, ALU.mult, ALU.add).then_inc(inner, 1)
                dve.wait_ge(inner, t * 4 + 4)
                dve.scalar_tensor_tensor(msg[:, b, 0:128], tpw[:, b % 2, 128:256], K * 3.0 ** -0.5, dot,
                                         ALU.mult, ALU.mult).then_inc(w_used, 1)
                dve.wait_ge(w_used, t + 3)
                dve.sem_inc(msg_ready, 1)

            dve.wait_ge(loaded, 48)
            messages = vector_messages if vector else scalar_messages
            for_width(dve, c, lambda narrow: rounds(dve, [(prepare(narrow), 0), (messages, 0)]))

        @blk.scalar
        def _(act):
            def stage_hidden(t, b):
                pair = t // 2 if isinstance(t, int) else t.u * (U // 2) + t.off // 2
                act.wait_ge(scattered, t + 1)
                act.activation(hs[half(b), b, :], h3T.rearrange("q (t p) -> q t p", p=P)[half(b), at(pair), :].rearrange(
                    "q a p -> q (a p)"), ACT.Copy).then_inc(h_staged, 1)
            rounds(act, [(stage_hidden, 0)])
            act.wait_ge(scattered, U + TILES + 1)
            for j in range(J):
                act.activation(agg[:, j, :], acc[:, j, :], ACT.Copy).then_inc(copied, 1)


def mace_out(c, agg_s, agg_v):
    nc, a = c.nc, c.a
    with ExitStack() as ctx:
        sb = lambda n, s: ctx.enter_context(nc.sbuf_tensor(f"mo_{n}", s, F32))
        w = sb("w", [128, 2, 2, 128])
        aT = sb("aT", [128, 2, 4, N])
        tp = ctx.enter_context(nc.psum_tensor("mo_tp", [128, 2, 512], F32))
        ps = ctx.enter_context(nc.psum_tensor("mo_ps", [P, 2, 512], F32))
        loaded, turned, copied, product, added = (c.sem(f"mo_{n}") for n in (
            "loaded", "turned", "copied", "product", "added"))
        blk = ctx.enter_context(nc.Block())

        @blk.sync
        def _(sp):
            for i in range(2):
                sp.dma_start(w[:, i], a[f"W_out{i}"].rearrange("(h q) f -> q h f", q=128)).then_inc(loaded, 16)

        @blk.tensor
        def _(pe):
            for n in range(2 * J):
                j, agg = n // 2, (agg_s, agg_v)[n % 2]
                if n >= 2:
                    pe.wait_ge(copied, n - 1)
                for g in range(4):
                    ins = pe.transpose(tp[:, n % 2, col(g)], agg[:, j, col(g, 128)], c.ident[0:P, 0:P])
                ins.then_inc(turned, 1)
            pe.wait_ge(loaded, 32)
            for j in range(J):
                pe.wait_ge(copied, 2 * j + 2)
                if j >= 2:
                    pe.wait_ge(added, 2 * (j - 1))
                for g in range(4):
                    for h in range(2):
                        ins = pe.matmul(ps[:, j % 2, col(g, 128)], aT[:, h, g, col(j)], w[:, min(g, 1), h],
                                        start=(h == 0), stop=(h == 1))
                ins.then_inc(product, 1)

        @blk.scalar
        def _(act):
            for n in range(2 * J):
                act.wait_ge(turned, n + 1)
                act.activation(aT[:, n % 2, :, col(n // 2)], tp[:, n % 2, 0:4 * P].rearrange("q (g p) -> q g p", g=4),
                               ACT.Copy).then_inc(copied, 1)

        @blk.vector
        def _(dve):
            for j in range(J):
                dve.wait_ge(product, j + 1)
                dve.scalar_tensor_tensor(c.x[:, j, 0:128], ps[:, j % 2, 0:128], 1 / 160, c.x[:, j, 0:128],
                                         ALU.mult, ALU.add).then_inc(added, 1)
                v = c.x[:, j, 128:512].rearrange("p (v m) -> p m v", m=3)
                dve.scalar_tensor_tensor(v, ps[:, j % 2, 128:512].rearrange("p (m v) -> p m v", m=3), 1 / 160, v,
                                         ALU.mult, ALU.add).then_inc(added, 1)


def adjacency(c, degree):
    nc = c.nc
    BF = mybir.dt.bfloat16
    with ExitStack() as ctx:
        hot = ctx.enter_context(nc.sbuf_tensor("ad_hot", [P, U, 2, N], BF))
        one = ctx.enter_context(nc.sbuf_tensor("ad_one", [P, 1], F32))
        acc = ctx.enter_context(nc.psum_tensor("ad_acc", [P, 7, 512], F32))
        cnt = ctx.enter_context(nc.psum_tensor("ad_cnt", [P, 512], F32))
        hot_ready, counted, copied, summed, done = (c.sem(f"ad_{n}") for n in (
            "hot_ready", "counted", "copied", "summed", "done"))
        blk = ctx.enter_context(nc.Block())
        pieces = []
        for i in range(J):
            n = 0
            while n < J:
                unit = i * J + n
                width = min(4 - unit % 4, J - n)
                pieces.append((i, n, width, unit // 4, unit % 4))
                n += width

        @blk.vector
        def _(dve):
            dve.memset(one[:], 1.0).then_inc(done, 1)
            with dve.Fori(0, TURNS) as u:
                for b in range(U):
                    dve.wait_ge(counted, u * U + b + 1)
                    for h, key in enumerate((c.src_f, c.dst_f)):
                        dve.tensor_scalar(hot[:, b, h, :], c.iota[:], key[:, at(u * U + b)], None,
                                          ALU.is_equal).then_inc(hot_ready, 1)
            dve.wait_ge(summed, 1)
            dve.tensor_scalar(degree[:], cnt[:, 0:J], 1.0, None, ALU.max).then_inc(done, 1)
            dve.wait_ge(done, 2)
            dve.reciprocal(degree[:], degree[:]).then_inc(done, 1)

        @blk.tensor
        def _(pe):
            pe.sem_inc(counted, U)
            for k in range(7):
                pe.matmul(acc[:, k, :], c.zeros[:, 0:P], c.zeros[:], start=True, stop=False)
            with pe.Fori(0, TURNS) as u:
                for b in range(U):
                    pe.wait_ge(hot_ready, u * (2 * U) + 2 * b + 2)
                    for i, n, width, bank, place in pieces:
                        ins = pe.matmul(acc[:, bank, place * P:(place + width) * P], hot[:, b, 0, col(i)],
                                        hot[:, b, 1, n * P:(n + width) * P], start=False, stop=False)
                    ins.then_inc(counted, 1)
            for k in range(7):
                ins = pe.matmul(acc[:, k, :], c.zeros[:, 0:P], c.zeros[:], start=False, stop=True)
            ins.then_inc(counted, 1)
            pe.wait_ge(copied, 7)
            pe.wait_ge(done, 1)
            for j in range(J):
                for i in range(J):
                    ins = pe.matmul(cnt[:, j:j + 1], c.adjT[:, i, col(j)], one[:], start=(i == 0), stop=(i == J - 1))
            ins.then_inc(summed, 1)

        @blk.scalar
        def _(act):
            flat = c.adjT[:].rearrange("p i n -> p (i n)")
            act.wait_ge(counted, U + TILES + 1)
            for k in range(7):
                w = min(4 * P, J * N - k * 4 * P)
                act.activation(flat[:, k * 4 * P:k * 4 * P + w], acc[:, k, 0:w], ACT.Copy).then_inc(copied, 1)


def sage_layer(c, l, h, degree, final):
    nc, a = c.nc, c.a
    tag = f"sg{l}"
    with ExitStack() as ctx:
        sb = lambda n, s: ctx.enter_context(nc.sbuf_tensor(f"{tag}_{n}", s, F32))
        wl = sb("wl", [128, KT, D]); wr = sb("wr", [128, KT, D]); bl = sb("bl", [1, D])
        gain = sb("gain", [P, D]); bias = sb("bias", [P, D]); slope = sb("slope", [P, 1])
        agg = sb("agg", [P, J, D]); aggT = sb("aggT", [128, KT, N]); hT = sb("hT", [128, KT, N])
        y = sb("y", [P, J, D]); st = sb("st", [P, J, 6]); mv = sb("mv", [P, J, 2])
        acc = ctx.enter_context(nc.psum_tensor(f"{tag}_acc", [P, J, 512], F32))
        tp = ctx.enter_context(nc.psum_tensor(f"{tag}_tp", [128, 3, 512], F32))
        w_loaded, n_loaded = c.sem(f"{tag}_w_loaded"), c.sem(f"{tag}_n_loaded")
        summed, averaged, turned, copied, product = (c.sem(f"{tag}_{n}") for n in (
            "summed", "averaged", "turned", "copied", "product"))
        steps, var_ready, rooted = c.sem(f"{tag}_steps"), c.sem(f"{tag}_var_ready"), c.sem(f"{tag}_rooted")
        blk = ctx.enter_context(nc.Block())

        @blk.sync
        def _(sp):
            sp.dma_start(wl[:], a[f"Wl{l}"].rearrange("(k q) f -> q k f", q=128)).then_inc(w_loaded, 16)
            sp.dma_start(wr[:], a[f"Wr{l}"].rearrange("(k q) f -> q k f", q=128)).then_inc(w_loaded, 16)
            sp.dma_start(bl[:], a[f"bl{l}"]).then_inc(w_loaded, 16)
            sp.dma_start(gain[:], a[f"g{l}"].partition_broadcast(P)).then_inc(n_loaded, 16)
            sp.dma_start(bias[:], a[f"b{l}"].partition_broadcast(P)).then_inc(n_loaded, 16)
            sp.dma_start(slope[:], a["a_prelu"].partition_broadcast(P)).then_inc(n_loaded, 16)

        @blk.tensor
        def _(pe):
            for j in range(J):
                for i in range(J):
                    ins = pe.matmul(acc[:, j, :], c.adjT[:, i, col(j)], h[:, i, :], start=(i == 0), stop=(i == J - 1))
                ins.then_inc(summed, 1)
            for n in range(2 * J):
                j, s = n % J, (h, agg)[n // J]
                if n >= 3:
                    pe.wait_ge(copied, n - 2)
                if n >= J:
                    pe.wait_ge(averaged, j + 1)
                for k in range(KT):
                    ins = pe.transpose(tp[:, n % 3, col(k)], s[:, j, col(k, 128)], c.ident[0:P, 0:P])
                ins.then_inc(turned, 1)
            pe.wait_ge(w_loaded, 48)
            for j in range(J):
                pe.wait_ge(averaged, j + 1)
                pe.wait_ge(copied, J + j + 1)
                for k in range(KT):
                    pe.matmul(acc[:, j, :], hT[:, k, col(j)], wr[:, k, :], start=(k == 0), stop=False)
                for k in range(KT):
                    pe.matmul(acc[:, j, :], aggT[:, k, col(j)], wl[:, k, :], start=False, stop=False)
                pe.matmul(acc[:, j, :], c.ones[:, 0:P], bl[:], start=False, stop=True).then_inc(product, 1)

        @blk.scalar
        def _(act):
            for n in range(2 * J):
                act.wait_ge(turned, n + 1)
                act.activation((hT, aggT)[n // J][:, :, col(n % J)],
                               tp[:, n % 3, 0:KT * P].rearrange("q (k p) -> q k p", k=KT), ACT.Copy).then_inc(copied, 1)
            act.wait_ge(var_ready, 1)
            act.activation(mv[:, :, 1], mv[:, :, 1], ACT.Sqrt).then_inc(rooted, 1)

        @blk.vector
        def _(dve):
            step = Chain(dve, steps)
            for j in range(J):
                dve.wait_ge(summed, j + 1)
                dve.tensor_scalar(agg[:, j, :], acc[:, j, :], degree[:, j:j + 1], None, ALU.mult).then_inc(averaged, 1)
            for j in range(J):
                dve.wait_ge(product, j + 1)
                if l == 0:
                    step(dve.tensor_copy(y[:, j, :], acc[:, j, :]))
                else:
                    step(dve.tensor_tensor(y[:, j, :], acc[:, j, :], h[:, j, :], ALU.add))
                step(dve.bn_stats(st[:, j, :], y[:, j, :]))
                step(dve.bn_aggr(mv[:, j, :], st[:, j, :]))
            dve.tensor_scalar(mv[:, :, 1], mv[:, :, 1], EPS, None, ALU.add).then_inc(var_ready, 1)
            dve.wait_ge(rooted, 1)
            step(dve.reciprocal(mv[:, :, 1], mv[:, :, 1]))
            dve.wait_ge(n_loaded, 48)
            for j in range(J):
                step(dve.tensor_scalar(y[:, j, :], y[:, j, :], mv[:, j, 0:1], mv[:, j, 1:2], ALU.subtract, ALU.mult))
                step(dve.tensor_tensor(y[:, j, :], y[:, j, :], gain[:], ALU.mult))
                step(dve.tensor_tensor(y[:, j, :], y[:, j, :], bias[:], ALU.add))
                step(dve.tensor_scalar(agg[:, j, :], y[:, j, :], 0.0, slope[:], ALU.min, ALU.mult))
                step(dve.scalar_tensor_tensor(h[:, j, :], y[:, j, :], 0.0, agg[:, j, :], ALU.max, ALU.add))
                if final:
                    step(dve.tensor_tensor(c.x[:, j, :], c.x[:, j, :], h[:, j, :], ALU.add))


def edge_nodes(c):
    nc, a = c.nc, c.a
    norm(c)
    with ExitStack() as ctx:
        sb = lambda n, s: ctx.enter_context(nc.sbuf_tensor(f"en_{n}", s, F32))
        w = sb("w", [128, 2, KT, D]); b = sb("b", [1, D]); stage = sb("stage", [P, 2, J, D])
        ps = ctx.enter_context(nc.psum_tensor("en_ps", [P, 4, 512], F32))
        loaded, product, staged, stored = (c.sem(f"en_{n}") for n in ("loaded", "product", "staged", "stored"))
        blk = ctx.enter_context(nc.Block())

        @blk.sync
        def _(sp):
            for s in range(2):
                sp.dma_start(w[:, s], a["E_W1"][s * D:(s + 1) * D].rearrange("(k q) f -> q k f", q=128)).then_inc(loaded, 16)
            sp.dma_start(b[:], a["E_b1"]).then_inc(loaded, 16)
            for s, table in enumerate((c.xs_table, c.xd_table)):
                sp.wait_ge(staged, (s + 1) * J)
                sp.dma_start(table.rearrange("(j p) f -> p j f", p=P), stage[:, s]).then_inc(stored, 16)
            sp.wait_ge(stored, 32)

        @blk.tensor
        def _(pe):
            pe.wait_ge(loaded, 48)
            for n in range(2 * J):
                s, j = n // J, n % J
                if n >= 4:
                    pe.wait_ge(staged, n - 3)
                for k in range(KT):
                    ins = pe.matmul(ps[:, n % 4, :], c.xnT[:, k, col(j)], w[:, s, k, :], start=(k == 0),
                                    stop=(k == KT - 1 and s == 0))
                if s == 1:
                    ins = pe.matmul(ps[:, n % 4, :], c.ones[:, 0:P], b[:], start=False, stop=True)
                ins.then_inc(product, 1)

        @blk.scalar
        def _(act):
            for n in range(2 * J):
                act.wait_ge(product, n + 1)
                act.activation(stage[:, n // J, n % J, :], ps[:, n % 4, :], ACT.Copy).then_inc(staged, 1)


def edge_messages(c, agg):
    nc, a = c.nc, c.a
    with ExitStack() as ctx:
        sb = lambda n, s, dt=F32: ctx.enter_context(nc.sbuf_tensor(f"em_{n}", s, dt))
        ix = sb("ix", [P, U, 2], I32); rows = sb("rows", [P, U, 2, D]); ea = sb("ea", [64, U, P])
        w1 = sb("w1", [64, D]); w2 = sb("w2", [128, KT, D]); b2 = sb("b2", [P, D])
        z1 = sb("z1", [P, 2, D]); q1 = sb("q1", [P, 2, D]); h = sb("h", [P, 2, D]); hT = sb("hT", [128, 2, KT, P])
        z2 = sb("z2", [P, 2, D]); q2 = sb("q2", [P, 2, D]); msg = sb("msg", [P, 2, D]); hot = sb("hot", [P, 2, N])
        acc = ctx.enter_context(nc.psum_tensor("em_acc", [P, J, 512], F32))
        z1p = ctx.enter_context(nc.psum_tensor("em_z1p", [P, 512], F32))
        z2p = ctx.enter_context(nc.psum_tensor("em_z2p", [P, 512], F32))
        tp = ctx.enter_context(nc.psum_tensor("em_tp", [128, 512], F32))
        (w_loaded, indexed, go, edge_product, z1_partial, z1_ready, q1_ready, h_part, h_ready, turned, hT_ready, product,
         z2_ready, q2_ready, m_part, msg_ready, hot_ready, scattered, copied, sig1, sig2) = (c.sem(f"em_{n}") for n in (
            "w_loaded", "indexed", "go", "edge_product", "z1_partial", "z1_ready", "q1_ready", "h_part", "h_ready",
            "turned", "hT_ready", "product", "z2_ready", "q2_ready", "m_part", "msg_ready", "hot_ready",
            "scattered", "copied", "sig1", "sig2"))
        gathered, before = c.gathered, c.gathers(2)
        ea_loaded = [c.sem(f"em_ea_loaded{b}") for b in range(U)]
        blk = ctx.enter_context(nc.Block())

        @blk.sync
        def _(sp):
            sp.dma_start(w1[:], a["E_W1"][2 * D:2 * D + 64]).then_inc(w_loaded, 16)
            sp.dma_start(w2[:], a["E_W2"].rearrange("(k q) f -> q k f", q=128)).then_inc(w_loaded, 16)
            sp.dma_start(b2[:], a["E_b2"].partition_broadcast(P)).then_inc(w_loaded, 16)
            sp.sem_inc(edge_product, U)

            def fetch(t, b):
                sp.wait_ge(edge_product, t + 1)
                sp.dma_start(ea[:, b, :], a["ea64T"][:, bass.ds(t * P + 0, P)]).then_inc(ea_loaded[b], 16)
            rounds(sp, [(fetch, 0)])

        @blk.gpsimd
        def _(pool):
            pool.sem_inc(z1_ready, U)

            def fetch(t, b):
                pool.wait_ge(z1_ready, t + 1)
                pool.tensor_copy(ix[:, b, 0:1], c.src_i[:, at(t)]).then_inc(indexed, 1)
                pool.tensor_copy(ix[:, b, 1:2], c.dst_i[:, at(t)]).then_inc(indexed, 1)
                pool.wait_ge(indexed, t * 2 + 2)
                pool.sem_inc(go, 1)
                for n, table in enumerate((c.xs_table, c.xd_table)):
                    pool.indirect_dma_start(rows[:, b, n, :], None, table, bass.IndirectOffsetOnAxis(
                        ap=ix[:, b, n:n + 1], axis=0)).then_inc(gathered[b], 16)
            rounds(pool, [(fetch, 0)])

        @blk.tensor
        def _(pe):
            def edge_part(t, b):
                pe.wait_ge(ea_loaded[b], filled(t, b))
                pe.wait_ge(z1_partial, t + 1)
                pe.matmul(z1p[0:P, :], ea[:, b, :], w1[:], start=True, stop=True).then_inc(edge_product, 1)

            def turn_h(t, b):
                pe.wait_ge(h_ready, t + 1)
                pe.wait_ge(hT_ready, t + 1)
                for k in range(KT):
                    ins = pe.transpose(tp[:, col(k)], h[:, b % 2, col(k, 128)], c.ident[0:P, 0:P])
                ins.then_inc(turned, 1)

            def second(t, b):
                pe.wait_ge(hT_ready, t + 2)
                pe.wait_ge(z2_ready, t + 1)
                for k in range(KT):
                    ins = pe.matmul(z2p[0:P, :], hT[:, b % 2, k, :], w2[:, k, :], start=(k == 0), stop=(k == KT - 1))
                ins.then_inc(product, 1)

            def scatter(narrow):
                def stage(t, b):
                    pe.wait_ge(msg_ready, t + 3)
                    pe.wait_ge(hot_ready, t + 1)
                    add_targets(pe, c, acc, hot[:, b % 2, :], [msg[:, b % 2, :]], t, narrow).then_inc(scattered, 1)
                return stage

            pe.sem_inc(z1_partial, 1)
            pe.sem_inc(z2_ready, 1)
            pe.sem_inc(hT_ready, 1)
            pe.sem_inc(scattered, 2)
            open_accumulators(pe, c, acc)
            pe.wait_ge(w_loaded, 48)
            for_width(pe, c, lambda narrow: rounds(
                pe, [(edge_part, 0), (turn_h, 1), (second, 2), (scatter(narrow), 4)]))
            close_accumulators(pe, c, acc).then_inc(scattered, 1)

        @blk.vector
        def _(dve):
            def first(t, b):
                p = b % 2
                dve.wait_ge(edge_product, t + U + 1)
                dve.wait_ge(gathered[b], filled(t, b, 2) + before)
                dve.tensor_tensor(z1[:, p, :], z1p[0:P, :], rows[:, b, 0, :], ALU.add).then_inc(z1_partial, 1)
                dve.wait_ge(z1_partial, t + 2)
                dve.tensor_tensor(z1[:, p, :], z1[:, p, :], rows[:, b, 1, :], ALU.add).then_inc(z1_ready, 1)

            def hidden(t, b):
                p = b % 2
                dve.wait_ge(q1_ready, t + 1)
                dve.tensor_tensor(h[:, p, :], z1[:, p, :], q1[:, p, :], ALU.mult).then_inc(h_ready, 1)

            def output(t, b):
                dve.wait_ge(product, t + 1)
                dve.wait_ge(msg_ready, t + 1)
                dve.tensor_tensor(z2[:, b % 2, :], z2p[0:P, :], b2[:], ALU.add).then_inc(z2_ready, 1)

            def message(narrow):
                def stage(t, b):
                    p = b % 2
                    dve.wait_ge(scattered, t + 1)
                    target_hot(dve, c, hot[:, p, :], t, narrow).then_inc(hot_ready, 1)
                    dve.wait_ge(q2_ready, t + 1)
                    dve.tensor_tensor(msg[:, p, :], z2[:, p, :], q2[:, p, :], ALU.mult).then_inc(msg_ready, 1)
                return stage

            dve.wait_ge(w_loaded, 48)
            dve.sem_inc(msg_ready, 2)
            for_width(dve, c, lambda narrow: rounds(
                dve, [(first, 0), (hidden, 1), (output, 2), (message(narrow), 3)]))

        @blk.scalar
        def _(act):
            def angle(z, q, ready, sig):
                def stage(t, b):
                    p = b % 2
                    act.wait_ge(ready[0], t + 1 + ready[1])
                    act.activation(q[:, p, :], z[:, p, :], ACT.Sigmoid, scale=-1.0).then_inc(sig, 1)
                    act.wait_ge(sig, t * 2 + 1)
                    act.activation(q[:, p, :], q[:, p, :], ACT.Arctan).then_inc(sig, 1)
                return stage

            def factor(q, sig, done):
                def stage(t, b):
                    act.wait_ge(sig, t * 2 + 2)
                    act.activation(q[:, b % 2, :], q[:, b % 2, :], ACT.Sin, scale=-2.0, bias=c.half_pi[:]).then_inc(done, 1)
                return stage

            def copy_turned(t, b):
                act.wait_ge(turned, t + 1)
                act.activation(hT[:, b % 2, :, :], tp[:, 0:KT * P].rearrange("q (k p) -> q k p", k=KT),
                               ACT.Copy).then_inc(hT_ready, 1)

            rounds(act, [(angle(z1, q1, (z1_ready, U), sig1), 0), (copy_turned, 1), (angle(z2, q2, (z2_ready, 1), sig2), 2),
                         (factor(q1, sig1, q1_ready), 0), (factor(q2, sig2, q2_ready), 2)])
            act.wait_ge(scattered, 2 + TILES + 1)
            for j in range(J):
                act.activation(agg[:, j, :], acc[:, j, :], ACT.Copy).then_inc(copied, 1)


def edge_out(c, agg):
    nc, a = c.nc, c.a
    with ExitStack() as ctx:
        sb = lambda n, s: ctx.enter_context(nc.sbuf_tensor(f"eo_{n}", s, F32))
        w3 = sb("w3", [128, 2 * KT, D]); w4 = sb("w4", [128, KT, D]); b3 = sb("b3", [1, D]); b4 = sb("b4", [1, D])
        gain = sb("gain", [P, D]); bias = sb("bias", [P, D])
        aggT = sb("aggT", [128, KT, N]); uT = sb("uT", [128, KT, N])
        z = sb("z", [P, J, D]); q = sb("q", [P, J, D]); y = sb("y", [P, J, D])
        st = sb("st", [P, J, 6]); mv = sb("mv", [P, J, 2])
        acc = ctx.enter_context(nc.psum_tensor("eo_acc", [P, J, 512], F32))
        tp = ctx.enter_context(nc.psum_tensor("eo_tp", [128, 3, 512], F32))
        (w_loaded, n_loaded, turned, copied, product, taken, squared, q_ready, u_ready, out_ready, steps, var_ready,
         rooted) = (c.sem(f"eo_{n}") for n in (
            "w_loaded", "n_loaded", "turned", "copied", "product", "taken", "squared", "q_ready", "u_ready",
            "out_ready", "steps", "var_ready", "rooted"))
        blk = ctx.enter_context(nc.Block())

        @blk.sync
        def _(sp):
            sp.dma_start(w3[:], a["E_W3"].rearrange("(k q) f -> q k f", q=128)).then_inc(w_loaded, 16)
            sp.dma_start(b3[:], a["E_b3"]).then_inc(w_loaded, 16)
            sp.dma_start(w4[:], a["E_W4"].rearrange("(k q) f -> q k f", q=128)).then_inc(w_loaded, 16)
            sp.dma_start(b4[:], a["E_b4"]).then_inc(w_loaded, 16)
            sp.dma_start(gain[:], a["E_gamma"].partition_broadcast(P)).then_inc(n_loaded, 16)
            sp.dma_start(bias[:], a["E_beta"].partition_broadcast(P)).then_inc(n_loaded, 16)

        @blk.tensor
        def _(pe):
            for n in range(J):
                if n >= 3:
                    pe.wait_ge(copied, n - 2)
                for k in range(KT):
                    ins = pe.transpose(tp[:, n % 3, col(k)], agg[:, n, col(k, 128)], c.ident[0:P, 0:P])
                ins.then_inc(turned, 1)
            pe.wait_ge(w_loaded, 64)
            for j in range(J):
                pe.wait_ge(copied, j + 1)
                for k in range(2 * KT):
                    lhs = c.xnT[:, k, col(j)] if k < KT else aggT[:, k - KT, col(j)]
                    pe.matmul(acc[:, j, :], lhs, w3[:, k, :], start=(k == 0), stop=False)
                pe.matmul(acc[:, j, :], c.ones[:, 0:P], b3[:], start=False, stop=True).then_inc(product, 1)
            for j in range(J):
                pe.wait_ge(u_ready, j + 1)
                pe.wait_ge(copied, J if j < 1 else J + j - 1)
                for k in range(KT):
                    ins = pe.transpose(tp[:, j % 3, col(k)], y[:, j, col(k, 128)], c.ident[0:P, 0:P])
                ins.then_inc(turned, 1)
            for j in range(J):
                pe.wait_ge(copied, J + j + 1)
                for k in range(KT):
                    pe.matmul(acc[:, j, :], uT[:, k, col(j)], w4[:, k, :], start=(k == 0), stop=False)
                pe.matmul(acc[:, j, :], c.ones[:, 0:P], b4[:], start=False, stop=True).then_inc(out_ready, 1)

        @blk.scalar
        def _(act):
            def copy(n, dst):
                act.wait_ge(turned, n + 1)
                act.activation(dst[:, :, col(n % J)], tp[:, n % J % 3, 0:KT * P].rearrange("q (k p) -> q k p", k=KT),
                               ACT.Copy).then_inc(copied, 1)
            for n in range(J):
                copy(n, aggT)
            for j in range(J):
                act.wait_ge(taken, j + 1)
                act.activation(q[:, j, :], z[:, j, :], ACT.Sigmoid, scale=-1.0).then_inc(squared, 1)
                act.wait_ge(squared, 2 * j + 1)
                act.activation(q[:, j, :], q[:, j, :], ACT.Arctan).then_inc(squared, 1)
            for j in range(J):
                act.wait_ge(squared, 2 * j + 2)
                act.activation(q[:, j, :], q[:, j, :], ACT.Sin, scale=-2.0, bias=c.half_pi[:]).then_inc(q_ready, 1)
            for n in range(J, 2 * J):
                copy(n, uT)
            act.wait_ge(var_ready, 1)
            act.activation(mv[:, :, 1], mv[:, :, 1], ACT.Sqrt).then_inc(rooted, 1)

        @blk.vector
        def _(dve):
            step = Chain(dve, steps)
            for j in range(J):
                dve.wait_ge(product, j + 1)
                dve.tensor_copy(z[:, j, :], acc[:, j, :]).then_inc(taken, 1)
            for j in range(J):
                dve.wait_ge(q_ready, j + 1)
                dve.tensor_tensor(y[:, j, :], z[:, j, :], q[:, j, :], ALU.mult).then_inc(u_ready, 1)
            dve.wait_ge(copied, 2 * J)
            for j in range(J):
                dve.wait_ge(out_ready, j + 1)
                step(dve.tensor_tensor(y[:, j, :], acc[:, j, :], c.xn[:, j, :], ALU.add))
                step(dve.bn_stats(st[:, j, :], y[:, j, :]))
                step(dve.bn_aggr(mv[:, j, :], st[:, j, :]))
            dve.tensor_scalar(mv[:, :, 1], mv[:, :, 1], EPS, None, ALU.add).then_inc(var_ready, 1)
            dve.wait_ge(rooted, 1)
            step(dve.reciprocal(mv[:, :, 1], mv[:, :, 1]))
            dve.wait_ge(n_loaded, 32)
            for j in range(J):
                step(dve.tensor_scalar(y[:, j, :], y[:, j, :], mv[:, j, 0:1], mv[:, j, 1:2], ALU.subtract, ALU.mult))
                step(dve.tensor_tensor(y[:, j, :], y[:, j, :], gain[:], ALU.mult))
                step(dve.tensor_tensor(y[:, j, :], y[:, j, :], bias[:], ALU.add))
                step(dve.tensor_tensor(c.x[:, j, :], c.x[:, j, :], y[:, j, :], ALU.add))


def store(c):
    with ExitStack() as ctx:
        stored = c.sem("out_stored")
        blk = ctx.enter_context(c.nc.Block())

        @blk.sync
        def _(sp):
            sp.dma_start(c.a["out"].rearrange("(j p) d -> p j d", p=P), c.x[:]).then_inc(stored, 16)
            sp.wait_ge(stored, 16)


def program(nc, a):
    ctx = ExitStack()
    with ctx:
        c = Core(nc, ctx, a)
        buf = lambda s, name, shape: s.enter_context(nc.sbuf_tensor(name, shape, F32))
        setup(c)
        if STAGES >= 1:
            norm(c)
            with ExitStack() as s:
                h_self = buf(s, "h_self", [P, J, D])
                rel_tables(c, h_self)
                rel_edges(c, h_self)
        c.recycle()
        if STAGES >= 2:
            ffn_large(c)
        if STAGES >= 3:
            mace_nodes(c)
            with ExitStack() as s:
                agg_s, agg_v = buf(s, "agg_s", [P, J, D]), buf(s, "agg_v", [P, J, D])
                with ExitStack() as s2:
                    h3T = buf(s2, "h3T", [128, E // 2])
                    mace_mlp(c, h3T)
                    mace_edges(c, h3T, False, agg_s)
                    mace_edges(c, h3T, True, agg_v)
                mace_out(c, agg_s, agg_v)
        c.recycle()
        if STAGES >= 4:
            ffn_small(c, "f1", "switch", ACT.Gelu)
        c.recycle()
        if STAGES >= 5:
            with ExitStack() as s:
                degree = buf(s, "degree", [P, J])
                adjacency(c, degree)
                norm(c)
                for l in range(3):
                    sage_layer(c, l, c.xn, degree, l == 2)
        if STAGES >= 6:
            ffn_small(c, "f2", "top2_capacity", ACT.Gelu_apprx_tanh)
        c.recycle()
        if STAGES >= 7:
            edge_nodes(c)
            with ExitStack() as s:
                agg = buf(s, "agg_e", [P, J, D])
                edge_messages(c, agg)
                edge_out(c, agg)
        if STAGES >= 8:
            ffn_small(c, "f3", "top2_scores", ACT.Gelu)
        store(c)


STAGES = 8


def kernel(**v):
    import numpy as np
    import concourse.bacc as bacc
    from concourse.bass_utils import run_bass_kernel_spmd as run

    v = {k: np.asarray(x) for k, x in v.items()}
    cut = lambda x: x.reshape(2, TILES // 2, P, -1).transpose(1, 0, 2, 3).reshape(TILES, P, -1)
    tiles = lambda x: cut(x)[:, :, 0].T
    row = lambda x: x.reshape(1, -1)
    arrays = {
        "x": v["x"], "src": tiles(v["src"]), "dst": tiles(v["dst"]), "rel": tiles(v["edge_type_8"]),
        "dst_by_tile": v["dst"].reshape(2, TILES // 2, P).transpose(1, 0, 2),
        "ea4": cut(v["edge_attr_4"]).transpose(1, 0, 2),
        "ea8T": v["edge_attr_8"].reshape(2, E // 2, 8).transpose(0, 2, 1).reshape(16, E // 2),
        "ea64T": cut(v["edge_attr_64"]).reshape(E, 64).T,
        "iota": np.arange(N, dtype=np.float32), "ident": np.eye(128, dtype=np.float32),
        "spread": np.repeat(np.eye(NE, dtype=np.float32), 64, axis=1),
        "earlier": np.triu(np.ones((P, P), dtype=np.float32), 1),
        "W_self": v["L0_gnn_W_self"].T, "b_self": row(v["L0_gnn_b_self"]),
        "W_rel": v["L0_gnn_W_rel"].transpose(0, 2, 1).reshape(-1, D), "b_rel": v["L0_gnn_b_rel"],
        "fl_wg": v["L0_ffn_wg"], "fl_bg": row(v["L0_ffn_bg"]), "fl_w1": v["L0_ffn_w1"], "fl_w3": v["L0_ffn_w3"],
        "fl_w2": v["L0_ffn_w2"], "a_prelu": v["L2_gnn_a_prelu"],
    }
    for n in ("W_up0", "W_up1", "W_mlp1", "W_mlp2", "W_mlp3", "W_mlp4", "W_out0", "W_out1"):
        arrays[n] = v["L1_gnn_" + n]
    for l in range(3):
        arrays[f"Wl{l}"], arrays[f"Wr{l}"] = v[f"L2_gnn_Wl{l}"].T, v[f"L2_gnn_Wr{l}"].T
        arrays[f"bl{l}"], arrays[f"g{l}"], arrays[f"b{l}"] = row(v[f"L2_gnn_bl{l}"]), v[f"L2_gnn_g{l}"], v[f"L2_gnn_b{l}"]
    for n in ("W1", "W2", "W3", "W4", "gamma", "beta", "b2"):
        arrays["E_" + n] = v["L3_gnn_" + n]
    for n in ("b1", "b3", "b4"):
        arrays["E_" + n] = row(v["L3_gnn_" + n])
    zero_bias = np.zeros((1, NE), np.float32)
    for tag, wg, bg, m in (("f1", "L1_ffn_Ws", "L1_ffn_bs", ("W1", "b1", "W2", "b2")),
                           ("f2", "L2_ffn_router_w", None, ("w1", "b1", "w2", "b2")),
                           ("f3", "L3_ffn_Wg", "L3_ffn_bg", ("W1", "b1", "W2", "b2"))):
        w1, b1, w2, b2 = (v[wg[:7] + n] for n in m)
        arrays[tag + "_wg"], arrays[tag + "_bg"] = v[wg], row(v[bg]) if bg else zero_bias
        arrays[tag + "_w1"] = w1.transpose(1, 0, 2).reshape(D, D)
        arrays[tag + "_b1"] = b1.reshape(KT, 128).T
        arrays[tag + "_w2"], arrays[tag + "_b2"] = w2.reshape(D, D), b2
    arrays = {k: np.ascontiguousarray(x) for k, x in arrays.items()}
    nc = bacc.Bacc("TRN2", target_bir_lowering=False, num_devices=1)
    a = {k: nc.dram_tensor("in_" + k, x.shape, mybir.dt.from_np(x.dtype), kind="ExternalInput").ap()
         for k, x in arrays.items()}
    a["out"] = nc.dram_tensor("out", (N, D), F32, kind="ExternalOutput").ap()
    program(nc, a)
    r = run(nc, [{"in_" + k: x for k, x in arrays.items()}], core_ids=[0])
    return r.results[0]["out"]
```

```python
import concourse.bass as bass
from concourse import mybir
from contextlib import ExitStack
import math

F32 = mybir.dt.float32
I32 = mybir.dt.int32
ACT = mybir.ActivationFunctionType
ALU = mybir.AluOpType
X = mybir.AxisListType.X

N, D, E = 625, 512, 20000
P, J = 125, 5
TILES = E // P
U = 4
TURNS = TILES // U
KT = D // 128
R = 8
NE = 8
HALVES = ((0, 313), (313, 312))
EPS = 1e-5
BIG = 3.0e38
SILU_2MOM = 1.679177


class Chain:

    def __init__(self, eng, sem, start=0):
        self.eng, self.sem, self.n = eng, sem, start

    def __call__(self, ins):
        self.n += 1
        ins.then_inc(self.sem, 1)
        self.eng.wait_ge(self.sem, self.n)


class Core:

    def __init__(self, nc, ctx, a):
        self.nc, self.ctx, self.a = nc, ctx, a
        sb = lambda name, shape, dt=F32: ctx.enter_context(nc.sbuf_tensor(name, shape, dt))
        self.x = sb("x", [P, J, D])
        self.xn = sb("xn", [P, J, D])
        self.xnT = sb("xnT", [128, KT, N])
        self.ident = sb("ident", [128, 128])
        self.iota = sb("iota", [P, N])
        self.dst_f = sb("dst_f", [P, TILES])
        self.src_f = sb("src_f", [P, TILES])
        self.src_i = sb("src_i", [P, TILES], I32)
        self.dst_i = sb("dst_i", [P, TILES], I32)
        self.first_i = sb("first_i", [1, TILES], I32)
        self.narrow_i = sb("narrow_i", [1, 1], I32)
        self.dst_w = sb("dst_w", [P, TILES])
        self.ones = sb("ones", [1, 128])
        self.zeros = sb("zeros", [1, D])
        self.comb = sb("comb", [P, J, NE])
        self.half_pi = sb("half_pi", [P, 1])
        self.adjT = sb("adjT", [P, J, N])
        self.tail_row = sb("tail_row", [P, TILES], I32)
        self.head_row = sb("head_row", [P, TILES], I32)
        self.rel_table = nc.dram_tensor("rel_table", (2 * R * N, D), F32).ap()
        self.s0_table = nc.dram_tensor("s0_table", (N, 128), F32).ap()
        self.s1_table = nc.dram_tensor("s1_table", (N, 384), F32).ap()
        self.xs_table = nc.dram_tensor("xs_table", (N, D), F32).ap()
        self.xd_table = nc.dram_tensor("xd_table", (N, D), F32).ap()
        self.norm_uses = 0
        self.gathered = [ctx.enter_context(nc.semaphore(f"gathered{b}")) for b in range(U)]
        self.gather_count = 0
        self.used = []
        self.nsem = {k: ctx.enter_context(nc.semaphore("norm_" + k)) for k in
                     ("stats", "var", "root", "rows_ready", "transposed", "evacuated")}

    def sem(self, name):
        self.used.append(self.nc.alloc_semaphore(name=name))
        return self.used[-1]

    def gathers(self, n):
        before = self.gather_count
        self.gather_count += TURNS * n * 16
        return before

    def recycle(self):
        blk = self.nc.Block()
        with blk:
            @blk.gpsimd
            def _(pool):
                for s in self.used:
                    pool.sem_clear(s)
        for s in self.used:
            self.nc.release_semaphore(s)
        self.used = []


def col(j, w=P):
    return slice(j * w, (j + 1) * w)


def setup(c):
    nc, a = c.nc, c.a
    with ExitStack() as ctx:
        rel_i = ctx.enter_context(nc.sbuf_tensor("rel_i", [P, TILES], I32))
        rel_f = ctx.enter_context(nc.sbuf_tensor("rel_f", [P, TILES], F32))
        T2 = TILES // 2
        sb = lambda n, s, dt=F32: ctx.enter_context(nc.sbuf_tensor(n, s, dt))
        by_tile, by_tile_f = sb("by_tile", [T2, 2, P], I32), sb("by_tile_f", [T2, 2, P])
        span, tile_of = sb("span", [T2, 2, 2]), sb("tile_of", [T2, 2, 2])
        diag, ones80, widest = sb("diag", [T2, 2, T2, 2]), sb("ones80", [T2, P]), sb("widest", [1, 1])
        spread_out = ctx.enter_context(nc.psum_tensor("spread_out", [P, 2, TILES], F32))
        loaded, ready = c.sem("setup_loaded"), c.sem("setup_steps")
        spans_ready, spread = c.sem("spans_ready"), c.sem("spread")
        blk = ctx.enter_context(nc.Block())

        @blk.sync
        def _(sp):
            sp.dma_start(c.src_i[:], a["src"]).then_inc(loaded, 16)
            sp.dma_start(c.dst_i[:], a["dst"]).then_inc(loaded, 16)
            sp.dma_start(rel_i[:], a["rel"]).then_inc(loaded, 16)
            sp.dma_start(c.x[:], a["x"].rearrange("(j p) d -> p j d", p=P)).then_inc(loaded, 16)
            sp.dma_start(c.iota[:], a["iota"].partition_broadcast(P)).then_inc(loaded, 16)
            sp.dma_start(c.ident[:], a["ident"]).then_inc(loaded, 16)
            sp.dma_start(by_tile[:], a["dst_by_tile"]).then_inc(loaded, 16)

        @blk.tensor
        def _(pe):
            pe.wait_ge(spans_ready, 1)
            pe.matmul(spread_out[:, 0, :], ones80[:], diag[:, 0].rearrange("t i h -> t (i h)"), start=True, stop=True)
            pe.matmul(spread_out[:, 1, :], ones80[:], diag[:, 1].rearrange("t i h -> t (i h)"), start=True,
                      stop=True).then_inc(spread, 1)

        @blk.vector
        def _(dve):
            step = Chain(dve, ready)
            step(dve.memset(ones80[:], 1.0))
            step(dve.memset(c.ones[:], 1.0))
            step(dve.memset(c.zeros[:], 0.0))
            step(dve.memset(c.half_pi[:], math.pi / 2))
            dve.wait_ge(loaded, 7 * 16)
            step(dve.tensor_copy(by_tile_f[:], by_tile[:]))
            step(dve.tensor_reduce(span[:, 0, :], by_tile_f[:], X, ALU.min))
            step(dve.tensor_reduce(span[:, 1, :], by_tile_f[:], X, ALU.max))
            step(dve.tensor_scalar(tile_of[:], span[:], float(P), None, ALU.is_ge))
            for k in range(2, J):
                step(dve.scalar_tensor_tensor(tile_of[:], span[:], float(k * P), tile_of[:], ALU.is_ge, ALU.add))
            step(dve.tensor_scalar(tile_of[:, 0, :], tile_of[:, 0, :], float(J - 2), None, ALU.min))
            step(dve.tensor_tensor(tile_of[:, 1, :], tile_of[:, 1, :], tile_of[:, 0, :], ALU.subtract))
            for r in range(2):
                step(dve.tensor_tensor(diag[:, r], c.ident[0:T2, 0:T2].unsqueeze(2).broadcast_to([T2, T2, 2]),
                                       tile_of[:, r, :].unsqueeze(1).broadcast_to([T2, T2, 2]), ALU.mult))
            dve.sem_inc(spans_ready, 1)
            dve.wait_ge(spread, 1)
            step(dve.tensor_copy(c.first_i[:], spread_out[0:1, 0, :]))
            step(dve.tensor_reduce(widest[:], spread_out[0:1, 1, :], X, ALU.max))
            step(dve.tensor_scalar(widest[:], widest[:], 1.0, None, ALU.is_le))
            step(dve.tensor_copy(c.narrow_i[:], widest[:]))
            step(dve.tensor_copy(c.src_f[:], c.src_i[:]))
            step(dve.tensor_copy(c.dst_f[:], c.dst_i[:]))
            step(dve.scalar_tensor_tensor(c.dst_w[:], spread_out[:, 0, :], -float(P), c.dst_f[:], ALU.mult, ALU.add))
            step(dve.tensor_copy(rel_f[:], rel_i[:]))
            step(dve.scalar_tensor_tensor(c.tail_row[:], rel_f[:], float(N), c.dst_f[:], ALU.mult, ALU.add))
            step(dve.scalar_tensor_tensor(rel_f[:], rel_f[:], float(N), c.src_f[:], ALU.mult, ALU.add))
            step(dve.tensor_scalar(c.head_row[:], rel_f[:], float(R * N), None, ALU.add))


def norm(c):
    nc, s = c.nc, c.nsem
    v = c.norm_uses
    c.norm_uses += 1
    with ExitStack() as ctx:
        st = ctx.enter_context(nc.sbuf_tensor(f"bn_st{v}", [P, J, 6], F32))
        mv = ctx.enter_context(nc.sbuf_tensor(f"bn_mv{v}", [P, J, 2], F32))
        tp = ctx.enter_context(nc.psum_tensor(f"norm_tp{v}", [128, J, 512], F32))
        blk = ctx.enter_context(nc.Block())

        @blk.vector
        def _(dve):
            for j in range(J):
                dve.bn_stats(st[:, j, :], c.x[:, j, :]).then_inc(s["stats"], 1)
            for j in range(J):
                dve.wait_ge(s["stats"], (v * J + j + 1))
                dve.bn_aggr(mv[:, j, :], st[:, j, :]).then_inc(s["var"], 1)
            dve.wait_ge(s["var"], v * 7 + 5)
            dve.tensor_scalar(mv[:, :, 1], mv[:, :, 1], EPS, None, ALU.add).then_inc(s["var"], 1)
            dve.wait_ge(s["root"], v + 1)
            dve.reciprocal(mv[:, :, 1], mv[:, :, 1]).then_inc(s["var"], 1)
            dve.wait_ge(s["var"], v * 7 + 7)
            for j in range(J):
                dve.tensor_scalar(c.xn[:, j, :], c.x[:, j, :], mv[:, j, 0:1], mv[:, j, 1:2],
                                  ALU.subtract, ALU.mult).then_inc(s["rows_ready"], 1)

        @blk.scalar
        def _(act):
            act.wait_ge(s["var"], v * 7 + 6)
            act.activation(mv[:, :, 1], mv[:, :, 1], ACT.Sqrt).then_inc(s["root"], 1)
            for j in range(J):
                act.wait_ge(s["transposed"], v * J + j + 1)
                act.activation(c.xnT[:, :, col(j)], tp[:, j, 0:KT * P].rearrange("q (k p) -> q k p", k=KT),
                               ACT.Copy).then_inc(s["evacuated"], 1)

        @blk.tensor
        def _(pe):
            for j in range(J):
                pe.wait_ge(s["rows_ready"], v * J + j + 1)
                for k in range(KT):
                    ins = pe.transpose(tp[:, j, col(k)], c.xn[:, j, col(k, 128)], c.ident[0:P, 0:P])
                ins.then_inc(s["transposed"], 1)


def open_accumulators(pe, c, acc):
    for j in range(J):
        pe.matmul(acc[:, j, :], c.zeros[:, 0:P], c.zeros[:], start=True, stop=False)


def target_hot(dve, c, out, t, narrow):
    if narrow:
        return dve.tensor_scalar(out[:, 0:2 * P], c.iota[:, 0:2 * P], c.dst_w[:, at(t)], None, ALU.is_equal)
    return dve.tensor_scalar(out, c.iota[:], c.dst_f[:, at(t)], None, ALU.is_equal)


def add_targets(pe, c, acc, hot, parts, t, narrow):
    if narrow:
        first = pe.value_load(c.first_i[0:1, at(t)], min_val=0, max_val=J - 2)
        for n in range(2):
            for part in parts:
                ins = pe.matmul(acc[:, bass.ds(first + n, 1), :].rearrange("p a f -> p (a f)"), hot[:, col(n)], part,
                                start=False, stop=False)
        return ins
    for n in range(J):
        for part in parts:
            ins = pe.matmul(acc[:, n, :], hot[:, col(n)], part, start=False, stop=False)
    return ins


def for_width(eng, c, body):
    narrow = eng.value_load(c.narrow_i[0:1, 0:1], min_val=0, max_val=1)
    with eng.If(narrow == 1):
        body(True)
    with eng.Else():
        body(False)


def close_accumulators(pe, c, acc):
    for j in range(J):
        ins = pe.matmul(acc[:, j, :], c.zeros[:, 0:P], c.zeros[:], start=False, stop=True)
    return ins


def rel_tables(c, h_self):
    nc, a = c.nc, c.a
    G = 2 * R // 2
    FR = mybir.dt.float32r
    with ExitStack() as ctx:
        sb = lambda n, s, dt=F32: ctx.enter_context(nc.sbuf_tensor(f"rel_{n}", s, dt))
        w = sb("w", [128, 2, KT, D]); w_high = sb("w_high", [128, 2, KT, D], FR); w_low = sb("w_low", [128, 2, KT, D], FR)
        x_high = sb("x_high", [128, KT, N], FR); x_low = sb("x_low", [128, KT, N], FR)
        bias = sb("bias", [P, 2, D]); stage = sb("stage", [P, 2, J, D])
        ps = ctx.enter_context(nc.psum_tensor("rel_ps", [P, J, 512], F32))
        w_loaded = [c.sem(f"rel_w_loaded{i}") for i in range(2)]
        bias_loaded = [c.sem(f"rel_bias_loaded{i}") for i in range(2)]
        stored = [c.sem(f"rel_stored{i}") for i in range(2)]
        x_high_ready, x_low_ready, high_ready, low_ready, product, evacuated = (c.sem(f"rel_{n}") for n in (
            "x_high_ready", "x_low_ready", "high_ready", "low_ready", "product", "evacuated"))
        blk = ctx.enter_context(nc.Block())
        wv = a["W_rel"].rearrange("(r k q) o -> r q k o", k=KT, q=128)
        table = c.rel_table.rearrange("(g t j p) o -> g t p j o", t=2, j=J, p=P)

        @blk.sync
        def _(sp):
            def load(r, g, i):
                sp.wait_ge(low_ready, r + 1)
                sp.dma_start(w[:, i], wv[r]).then_inc(w_loaded[i], 16)
                sp.wait_ge(evacuated, r * J + J)
                sp.dma_start(bias[:, i], a["b_rel"][r].partition_broadcast(P)).then_inc(bias_loaded[i], 16)

            sp.sem_inc(low_ready, 2)
            sp.sem_inc(evacuated, 2 * J)
            with sp.Fori(0, G) as g:
                for i in range(2):
                    load(g * 2 + i, g, i)
            load(2 * G, G, 0)

        @blk.scalar
        def _(act):
            def split_high(r, g, i):
                act.wait_ge(w_loaded[i], g * 16 + 16)
                act.wait_ge(product, r * J + J)
                act.activation(w_high[:, i], w[:, i], ACT.Copy).then_inc(high_ready, 1)

            act.sem_inc(product, 2 * J)
            act.activation(x_high[:], c.xnT[:], ACT.Copy).then_inc(x_high_ready, 1)
            split_high(0, 0, 0)
            with act.Fori(0, G) as g:
                for i in range(2):
                    split_high(g * 2 + i + 1, g + i, 1 - i)
                    act.wait_ge(evacuated, g * (2 * J) + (i + 3) * J)
                    act.dma_start(table[g, i], stage[:, i]).then_inc(stored[i], 16)
            for i in range(2):
                act.wait_ge(stored[i], 16 * (G + 1))

        @blk.vector
        def _(dve):
            def split_low(r, i):
                dve.wait_ge(high_ready, r + 1)
                dve.wait_ge(product, r * J + J)
                dve.tensor_tensor(w_low[:, i], w[:, i], w_high[:, i].bitcast(F32), ALU.subtract).then_inc(low_ready, 1)

            def evacuate(r, g, i, out):
                dve.wait_ge(bias_loaded[i], g * 16 + 16)
                for j in range(J):
                    dve.wait_ge(product, r * J + (2 * J + j + 1))
                    dve.tensor_tensor(out[:, j, :], ps[:, j, :], bias[:, i, :], ALU.add).then_inc(evacuated, 1)

            for i in range(2):
                dve.sem_inc(stored[i], 16)
            dve.wait_ge(x_high_ready, 1)
            dve.tensor_tensor(x_low[:], c.xnT[:], x_high[:].bitcast(F32), ALU.subtract).then_inc(x_low_ready, 1)
            split_low(0, 0)
            with dve.Fori(0, G) as g:
                for i in range(2):
                    split_low(g * 2 + i + 1, 1 - i)
                    dve.wait_ge(stored[i], g * 16 + 16)
                    evacuate(g * 2 + i, g, i, stage[:, i])
            evacuate(2 * G, G, 0, h_self)

        @blk.tensor
        def _(pe):
            def products(r, i):
                pe.wait_ge(low_ready, r + 3)
                terms = [(x, y, k) for k in range(KT) for x, y in
                         ((x_high, w_high), (x_low, w_high), (x_high, w_low))]
                for j in range(J):
                    pe.wait_ge(evacuated, r * J + (J + j + 1))
                    for n, (x, y, k) in enumerate(terms):
                        ins = pe.matmul(ps[:, j, :], x[:, k, col(j)], y[:, i, k, :], start=(n == 0),
                                        stop=(n == len(terms) - 1))
                    ins.then_inc(product, 1)

            pe.wait_ge(x_low_ready, 1)
            with pe.Fori(0, G) as g:
                for i in range(2):
                    products(g * 2 + i, i)
            products(2 * G, 0)


def rel_edges(c, h_self):
    nc = c.nc
    FR = mybir.dt.float32r
    with ExitStack() as ctx:
        sb = lambda n, s, dt=F32: ctx.enter_context(nc.sbuf_tensor(f"re_{n}", s, dt))
        ix = sb("ix", [P, U, 2], I32); rows = sb("rows", [P, U, 2, D])
        high = sb("high", [P, 2, 2, D], FR); low = sb("low", [P, 2, 2, D], FR)
        src_hot = sb("src_hot", [P, 2, N], FR); dst_hot = sb("dst_hot", [P, 2, N], FR)
        acc = ctx.enter_context(nc.psum_tensor("re_acc", [P, J, 512], F32))
        indexed, go = c.sem("re_indexed"), c.sem("re_go")
        gathered, before = c.gathered, c.gathers(2)
        hot_ready, high_ready, low_ready, scattered, steps = (c.sem(f"re_{n}") for n in (
            "hot_ready", "high_ready", "low_ready", "scattered", "steps"))
        blk = ctx.enter_context(nc.Block())

        @blk.gpsimd
        def _(pool):
            pool.sem_inc(low_ready, U)

            def fetch(t, b):
                pool.wait_ge(low_ready, t + 1)
                pool.tensor_copy(ix[:, b, 0:1], c.tail_row[:, at(t)]).then_inc(indexed, 1)
                pool.tensor_copy(ix[:, b, 1:2], c.head_row[:, at(t)]).then_inc(indexed, 1)
                pool.wait_ge(indexed, t * 2 + 2)
                pool.sem_inc(go, 1)
                for h in range(2):
                    pool.indirect_dma_start(rows[:, b, h, :], None, c.rel_table, bass.IndirectOffsetOnAxis(
                        ap=ix[:, b, h:h + 1], axis=0)).then_inc(gathered[b], 16)
            rounds(pool, [(fetch, 0)])

        @blk.scalar
        def _(act):
            def split_high(t, b):
                act.wait_ge(gathered[b], filled(t, b, 2) + before)
                act.wait_ge(scattered, t + 1)
                act.activation(high[:, b % 2], rows[:, b], ACT.Copy).then_inc(high_ready, 1)
            rounds(act, [(split_high, 0)])

        @blk.vector
        def _(dve):
            def hots(narrow):
                def stage(t, b):
                    dve.wait_ge(scattered, t + 1)
                    dve.tensor_scalar(src_hot[:, b % 2, :], c.iota[:], c.src_f[:, at(t)], None,
                                      ALU.is_equal).then_inc(hot_ready, 1)
                    target_hot(dve, c, dst_hot[:, b % 2, :], t, narrow).then_inc(hot_ready, 1)
                return stage

            def split_low(t, b):
                dve.wait_ge(high_ready, t + 1)
                dve.tensor_tensor(low[:, b % 2], rows[:, b], high[:, b % 2].bitcast(F32), ALU.subtract).then_inc(low_ready, 1)

            for_width(dve, c, lambda narrow: rounds(dve, [(hots(narrow), 0), (split_low, 0)]))
            dve.wait_ge(scattered, TILES + 2 + 1)
            step = Chain(dve, steps)
            for j in range(J):
                step(dve.tensor_tensor(h_self[:, j, :], h_self[:, j, :], acc[:, j, :], ALU.add))
                dve.scalar_tensor_tensor(c.x[:, j, :], h_self[:, j, :], 0.0, c.x[:, j, :], ALU.max, ALU.add)

        @blk.tensor
        def _(pe):
            def scatter(narrow):
                def stage(t, b):
                    p = b % 2
                    pe.wait_ge(hot_ready, t * 2 + 2)
                    pe.wait_ge(high_ready, t + 1)
                    pe.wait_ge(low_ready, t + U + 1)
                    for j in range(J):
                        for part in (high, low):
                            pe.matmul(acc[:, j, :], src_hot[:, p, col(j)], part[:, p, 0, :], start=False, stop=False)
                    add_targets(pe, c, acc, dst_hot[:, p, :], [high[:, p, 1, :], low[:, p, 1, :]], t,
                                narrow).then_inc(scattered, 1)
                return stage

            pe.sem_inc(scattered, 2)
            open_accumulators(pe, c, acc)
            for_width(pe, c, lambda narrow: rounds(pe, [(scatter(narrow), 0)]))
            close_accumulators(pe, c, acc).then_inc(scattered, 1)


class Router:

    def __init__(self, c, ctx, tag):
        sb = lambda n, shape: ctx.enter_context(c.nc.sbuf_tensor(f"{tag}_{n}", shape, F32))
        self.c = c
        self.s = sb("s", [P, J, NE])
        self.e = sb("e", [P, J, NE])
        self.t = sb("t", [P, J, NE])
        self.mk = sb("mk", [P, J, NE])
        self.kp = sb("kp", [P, J, NE])
        self.oh1 = sb("oh1", [P, J, NE])
        self.oh2 = sb("oh2", [P, J, NE])
        self.m1, self.m2 = sb("m1", [P, J]), sb("m2", [P, J])
        self.r = sb("r", [P, J])
        self.ids = c.iota[:, 0:NE].unsqueeze(1).broadcast_to([P, J, NE])
        self.steps = c.sem(f"{tag}_steps")
        self.exps = c.sem(f"{tag}_exps")

    def wide(self, m):
        return m[:].unsqueeze(2).broadcast_to([P, J, NE])

    def first_max(self, dve, step, s, m, oh):
        t = self.t
        step(dve.tensor_reduce(m[:], s[:], X, ALU.max))
        step(dve.tensor_tensor(t[:], s[:], self.wide(m), ALU.is_equal))
        step(dve.scalar_tensor_tensor(t[:], t[:], -float(NE), self.ids, ALU.mult, ALU.add))
        step(dve.tensor_reduce(self.r[:], t[:], X, ALU.min))
        step(dve.tensor_tensor(oh[:], t[:], self.wide(self.r), ALU.is_equal))

    def exp_of(self, dve, step, s, m, n):
        step(dve.tensor_tensor(self.e[:], s[:], self.wide(m), ALU.subtract))
        dve.wait_ge(self.exps, n)

    def normalise(self, dve, step, out):
        step(dve.tensor_reduce(self.r[:], self.e[:], X, ALU.add))
        step(dve.reciprocal(self.r[:], self.r[:]))
        step(dve.tensor_tensor(out[:], self.e[:], self.wide(self.r), ALU.mult))


def route(c, dve, q, kind, logits, lg_ready, marks, capacity=None):
    step = Chain(dve, q.steps)
    dve.wait_ge(lg_ready, 1)
    step(dve.tensor_copy(q.s[:], logits))
    n_exp = [0]

    def exponential(s, m):
        step(dve.tensor_tensor(q.e[:], s[:], q.wide(m), ALU.subtract))
        marks.append(step.n)
        n_exp[0] += 1
        dve.wait_ge(q.exps, n_exp[0])

    def softmax():
        step(dve.tensor_reduce(q.m1[:], q.s[:], X, ALU.max))
        exponential(q.s, q.m1)
        q.normalise(dve, step, q.s)

    def second_max():
        step(dve.scalar_tensor_tensor(q.mk[:], q.oh1[:], -BIG, q.s[:], ALU.mult, ALU.add))
        q.first_max(dve, step, q.mk, q.m2, q.oh2)

    def keep_near(m):
        step(dve.tensor_tensor(q.t[:], q.s[:], q.wide(m), ALU.max))
        step(dve.reciprocal(q.t[:], q.t[:]))
        step(dve.tensor_tensor(q.kp[:], q.wide(m), q.s[:], ALU.subtract))
        step(dve.tensor_tensor(q.kp[:], q.kp[:], q.t[:], ALU.mult))
        step(dve.tensor_scalar(q.kp[:], q.kp[:], 0.02, None, ALU.is_le))

    def masked_share(oh, m):
        exponential(q.s, m)
        step(dve.tensor_tensor(q.e[:], q.e[:], q.kp[:], ALU.mult))
        step(dve.tensor_reduce(q.r[:], q.e[:], X, ALU.add))
        step(dve.reciprocal(q.r[:], q.r[:]))
        step(dve.tensor_tensor(q.e[:], q.e[:], oh[:], ALU.mult))
        step(dve.tensor_tensor(q.e[:], q.e[:], q.wide(q.r), ALU.mult))

    if kind == "sparsemixer":
        softmax()
        q.first_max(dve, step, q.s, q.m1, q.oh1)
        keep_near(q.m1)
        masked_share(q.oh1, q.m1)
        step(dve.tensor_copy(c.comb[:], q.e[:]))
        second_max()
        keep_near(q.m2)
        step(dve.scalar_tensor_tensor(q.t[:], q.oh1[:], 0.0, q.kp[:], ALU.is_equal, ALU.mult))
        step(dve.tensor_copy(q.kp[:], q.t[:]))
        masked_share(q.oh2, q.m2)
        step(dve.tensor_tensor(c.comb[:], c.comb[:], q.e[:], ALU.add))
    elif kind == "switch":
        softmax()
        q.first_max(dve, step, q.s, q.m1, q.oh1)
        step(dve.tensor_tensor(c.comb[:], q.s[:], q.oh1[:], ALU.mult))
    elif kind == "top2_scores":
        softmax()
        q.first_max(dve, step, q.s, q.m1, q.oh1)
        second_max()
        step(dve.tensor_tensor(q.t[:], q.oh1[:], q.oh2[:], ALU.add))
        step(dve.tensor_tensor(q.e[:], q.s[:], q.t[:], ALU.mult))
        q.normalise(dve, step, c.comb)
    elif kind == "top2_capacity":
        q.first_max(dve, step, q.s, q.m1, q.oh1)
        second_max()
        step(dve.tensor_tensor(q.mk[:], q.oh1[:], q.oh2[:], ALU.add))
        q.mask_step = step.n
        exponential(q.s, q.m1)
        step(dve.tensor_tensor(q.e[:], q.e[:], q.mk[:], ALU.mult))
        q.normalise(dve, step, c.comb)
        ranks, rank_ready, cap = capacity
        dve.wait_ge(rank_ready, 1)
        step(dve.scalar_tensor_tensor(c.comb[:], ranks, float(cap), c.comb[:], ALU.is_lt, ALU.mult))
    return step


def ffn_small(c, tag, kind, gelu):
    nc, a = c.nc, c.a
    norm(c)
    with ExitStack() as ctx:
        sb = lambda n, s, dt=F32: ctx.enter_context(nc.sbuf_tensor(f"{tag}_{n}", s, dt))
        pb = lambda n, s: ctx.enter_context(nc.psum_tensor(f"{tag}_{n}", s, F32))
        q = Router(c, ctx, tag)
        wg = sb("wg", [128, KT, NE]); bg = sb("bg", [1, NE])
        w1 = sb("w1", [128, KT, D]); b1 = sb("b1", [128, KT])
        w2 = sb("w2", [128, KT, D]); b2 = sb("b2", [NE, D])
        spread = sb("spread", [NE, D]); earlier = sb("earlier", [P, P]); every = sb("every", [P, P])
        hT = sb("hT", [128, KT, N]); combT = sb("combT", [NE, N])
        small = pb("small", [128, 512])
        lg = small[0:P, 0:J * NE].rearrange("p (j e) -> p j e", e=NE)
        ranks = small[0:P, 64:64 + J * NE].rearrange("p (j e) -> p j e", e=NE)
        big = pb("big", [128, 4, 512])
        ctp = pb("ctp", [NE, 2, 512])
        router_loaded, up_loaded, down_loaded = (c.sem(f"{tag}_{n}_loaded") for n in ("router", "up", "down"))
        lg_ready, rank_ready = c.sem(f"{tag}_lg_ready"), c.sem(f"{tag}_rank_ready")
        consts, up_ready, gelu_done = c.sem(f"{tag}_consts"), c.sem(f"{tag}_up_ready"), c.sem(f"{tag}_gelu_done")
        ct_ready, ct_copied = c.sem(f"{tag}_ct_ready"), c.sem(f"{tag}_ct_copied")
        spread_ready, scaled = c.sem(f"{tag}_spread_ready"), c.sem(f"{tag}_scaled")
        down_ready, added = c.sem(f"{tag}_down_ready"), c.sem(f"{tag}_added")
        blk = ctx.enter_context(nc.Block())
        marks = []

        @blk.sync
        def _(sp):
            sp.dma_start(wg[:], a[f"{tag}_wg"].rearrange("(k q) e -> q k e", q=128)).then_inc(router_loaded, 16)
            sp.dma_start(bg[:], a[f"{tag}_bg"]).then_inc(router_loaded, 16)
            sp.dma_start(w1[:], a[f"{tag}_w1"].rearrange("(k q) f -> q k f", q=128)).then_inc(up_loaded, 16)
            sp.dma_start(b1[:], a[f"{tag}_b1"]).then_inc(up_loaded, 16)
            sp.dma_start(w2[:], a[f"{tag}_w2"].rearrange("(k q) f -> q k f", q=128)).then_inc(down_loaded, 16)
            sp.dma_start(b2[:], a[f"{tag}_b2"]).then_inc(down_loaded, 16)
            sp.dma_start(spread[:], a["spread"]).then_inc(down_loaded, 16)
            sp.dma_start(earlier[:], a["earlier"]).then_inc(down_loaded, 16)

        @blk.vector
        def _(dve):
            dve.memset(every[:], 1.0).then_inc(consts, 1)
            step = route(c, dve, q, kind, lg, lg_ready, marks, (ranks, rank_ready, CAPACITY))
            q.comb_step = step.n
            for n in range(2 * KT):
                k, (h0, hn) = n // 2, HALVES[n % 2]
                dve.wait_ge(gelu_done, n + 1)
                dve.wait_ge(spread_ready, n + 1)
                dve.tensor_tensor(hT[:, k, h0:h0 + hn], hT[:, k, h0:h0 + hn], big[:, n % 4, 0:hn],
                                  ALU.mult).then_inc(scaled, 1)
            for j in range(J):
                dve.wait_ge(down_ready, j + 1)
                dve.tensor_tensor(c.x[:, j, :], c.x[:, j, :], big[0:P, j % 4, :], ALU.add).then_inc(added, 1)

        @blk.scalar
        def _(act):
            for i, m in enumerate(marks[:]):
                act.wait_ge(q.steps, m)
                act.activation(q.e[:], q.e[:], ACT.Exp).then_inc(q.exps, 1)
            act.wait_ge(up_loaded, 32)
            for n in range(2 * KT):
                k, (h0, hn) = n // 2, HALVES[n % 2]
                act.wait_ge(up_ready, n + 1)
                act.activation(hT[:, k, h0:h0 + hn], big[:, n % 4, 0:hn], gelu, bias=b1[:, k:k + 1]).then_inc(gelu_done, 1)
            for i, (first, n) in enumerate(((0, 4), (4, 1))):
                act.wait_ge(ct_ready, i + 1)
                act.activation(combT[:, first * P:(first + n) * P], ctp[:, i, 0:n * P], ACT.Copy).then_inc(ct_copied, 1)

        @blk.tensor
        def _(pe):
            pe.wait_ge(router_loaded, 32)
            for j in range(J):
                for k in range(KT):
                    pe.matmul(lg[:, j, :], c.xnT[:, k, col(j)], wg[:, k, :], start=(k == 0), stop=False)
                ins = pe.matmul(lg[:, j, :], c.ones[:, 0:P], bg[:], start=False, stop=True)
            ins.then_inc(lg_ready, 1)
            pe.wait_ge(up_loaded, 32)
            for n in range(2 * KT):
                m, (h0, hn) = n // 2, HALVES[n % 2]
                if n >= 4:
                    pe.wait_ge(gelu_done, n - 3)
                for k in range(KT):
                    ins = pe.matmul(big[:, n % 4, 0:hn], w1[:, k, col(m, 128)], c.xnT[:, k, h0:h0 + hn],
                                    start=(k == 0), stop=(k == KT - 1))
                ins.then_inc(up_ready, 1)
            pe.wait_ge(down_loaded, 64)
            if kind == "top2_capacity":
                pe.wait_ge(q.steps, q.mask_step)
                pe.wait_ge(consts, 1)
                for j in range(J):
                    for i in range(j):
                        pe.matmul(ranks[:, j, :], every[:], q.mk[:, i, :], start=(i == 0), stop=False)
                    ins = pe.matmul(ranks[:, j, :], earlier[:], q.mk[:, j, :], start=(j == 0), stop=True)
                ins.then_inc(rank_ready, 1)
            pe.wait_ge(q.steps, q.comb_step)
            for j in range(J):
                ins = pe.transpose(ctp[:, j // 4, col(j % 4)], c.comb[:, j, :], c.ident[0:P, 0:P])
                if j >= 3:
                    ins.then_inc(ct_ready, 1)
            pe.wait_ge(ct_copied, 2)
            for n in range(2 * KT):
                k, (h0, hn) = n // 2, HALVES[n % 2]
                if n < 4:
                    pe.wait_ge(gelu_done, n + 5)
                else:
                    pe.wait_ge(scaled, n - 3)
                pe.matmul(big[:, n % 4, 0:hn], spread[:, col(k, 128)], combT[:, h0:h0 + hn],
                          start=True, stop=True).then_inc(spread_ready, 1)
            pe.wait_ge(scaled, 2 * KT)
            for j in range(J):
                if j >= 4:
                    pe.wait_ge(added, j - 3)
                for k in range(KT):
                    pe.matmul(big[0:P, j % 4, :], hT[:, k, col(j)], w2[:, k, :], start=(k == 0), stop=False)
                pe.matmul(big[0:P, j % 4, :], combT[:, col(j)], b2[:], start=False, stop=True).then_inc(down_ready, 1)


CAPACITY = min(128 * math.ceil(math.ceil(0.3125 * N) / 128), N)


def ffn_large(c):
    nc, a = c.nc, c.a
    FM = 8
    norm(c)
    with ExitStack() as ctx:
        sb = lambda n, s, dt=F32: ctx.enter_context(nc.sbuf_tensor(f"fl_{n}", s, dt))
        pb = lambda n, s: ctx.enter_context(nc.psum_tensor(f"fl_{n}", s, F32))
        q = Router(c, ctx, "fl")
        wg = sb("wg", [128, KT, NE]); bg = sb("bg", [1, NE])
        w1 = sb("w1", [128, KT, 1024]); w3 = sb("w3", [128, KT, 1024])
        w2 = sb("w2", [128, FM, D])
        g = sb("g", [128, 2, 313]); hT = sb("hT", [128, FM, N])
        small = pb("small", [128, 512])
        lg = small[0:P, 0:J * NE].rearrange("p (j e) -> p j e", e=NE)
        up = pb("up", [128, 2, 2, 512])
        down = pb("down", [P, 2, 512])
        router_loaded, up_loaded, down_loaded = c.sem("fl_router_loaded"), c.sem("fl_up_loaded"), c.sem("fl_down_loaded")
        lg_ready, up_ready, gelu_done = c.sem("fl_lg_ready"), c.sem("fl_up_ready"), c.sem("fl_gelu_done")
        h_ready, down_ready, added = c.sem("fl_h_ready"), c.sem("fl_down_ready"), c.sem("fl_added")
        blk = ctx.enter_context(nc.Block())
        marks = []
        NH = 2 * FM

        @blk.sync
        def _(sp):
            sp.dma_start(wg[:], a["fl_wg"].rearrange("(k q) e -> q k e", q=128)).then_inc(router_loaded, 16)
            sp.dma_start(bg[:], a["fl_bg"]).then_inc(router_loaded, 16)
            sp.sem_inc(h_ready, NH)
            sp.sem_inc(down_ready, J)
            w1v = a["fl_w1"].rearrange("e (k q) f -> e q k f", q=128)
            w3v = a["fl_w3"].rearrange("e (k q) f -> e q k f", q=128)
            w2v = a["fl_w2"].rearrange("e (k q) f -> e q k f", q=128)
            with sp.Fori(0, NE) as e:
                sp.wait_ge(h_ready, e * NH + NH)
                sp.dma_start(w1[:], w1v[e]).then_inc(up_loaded, 16)
                sp.dma_start(w3[:], w3v[e]).then_inc(up_loaded, 16)
                sp.wait_ge(down_ready, e * J + J)
                sp.dma_start(w2[:], w2v[e]).then_inc(down_loaded, 16)

        @blk.vector
        def _(dve):
            route(c, dve, q, "sparsemixer", lg, lg_ready, marks)
            with dve.Fori(0, NE) as e:
                for n in range(NH):
                    m, (h0, hn) = n // 2, HALVES[n % 2]
                    if n == 0:
                        dve.wait_ge(down_ready, e * J + J)
                    dve.wait_ge(gelu_done, e * NH + n + 1)
                    dve.tensor_tensor(hT[:, m, h0:h0 + hn], g[:, n % 2, 0:hn], up[:, 1, n % 2, 0:hn],
                                      ALU.mult).then_inc(h_ready, 1)
                for j in range(J):
                    dve.wait_ge(down_ready, e * J + J + j + 1)
                    dve.scalar_tensor_tensor(c.x[:, j, :], down[:, j % 2, :], c.comb[:, j, bass.ds(e, 1)],
                                             c.x[:, j, :], ALU.mult, ALU.add).then_inc(added, 1)

        @blk.scalar
        def _(act):
            for m in marks:
                act.wait_ge(q.steps, m)
                act.activation(q.e[:], q.e[:], ACT.Exp).then_inc(q.exps, 1)
            with act.Fori(0, NE) as e:
                for n in range(NH):
                    m, (h0, hn) = n // 2, HALVES[n % 2]
                    act.wait_ge(up_ready, e * NH + n + 1)
                    act.wait_ge(h_ready, e * NH + NH + n - 1)
                    act.activation(g[:, n % 2, 0:hn], up[:, 0, n % 2, 0:hn], ACT.Gelu).then_inc(gelu_done, 1)

        @blk.tensor
        def _(pe):
            pe.wait_ge(router_loaded, 32)
            for j in range(J):
                for k in range(KT):
                    pe.matmul(lg[:, j, :], c.xnT[:, k, col(j)], wg[:, k, :], start=(k == 0), stop=False)
                ins = pe.matmul(lg[:, j, :], c.ones[:, 0:P], bg[:], start=False, stop=True)
            ins.then_inc(lg_ready, 1)
            pe.sem_inc(added, 2)
            with pe.Fori(0, NE) as e:
                pe.wait_ge(up_loaded, e * 32 + 32)
                for n in range(NH):
                    m, (h0, hn) = n // 2, HALVES[n % 2]
                    pe.wait_ge(h_ready, e * NH + NH + n - 1)
                    for s, w in enumerate((w1, w3)):
                        for k in range(KT):
                            ins = pe.matmul(up[:, s, n % 2, 0:hn], w[:, k, col(m, 128)], c.xnT[:, k, h0:h0 + hn],
                                            start=(k == 0), stop=(k == KT - 1))
                    ins.then_inc(up_ready, 1)
                pe.wait_ge(down_loaded, e * 16 + 16)
                pe.wait_ge(h_ready, e * NH + 2 * NH)
                for j in range(J):
                    pe.wait_ge(added, e * J + j + 1)
                    for m in range(FM):
                        ins = pe.matmul(down[:, j % 2, :], hT[:, m, col(j)], w2[:, m, :], start=(m == 0), stop=(m == FM - 1))
                    ins.then_inc(down_ready, 1)


class Tile:

    def __init__(self, u, off, width):
        self.u, self.off, self.width = u, off, width

    def __add__(self, n):
        return self.u * self.width + (self.off + n)

    def __mul__(self, n):
        return Scaled(self.u * (self.width * n), self.off * n)

    def __floordiv__(self, n):
        return self.u * (self.width // n) + self.off // n


class Scaled:
    def __init__(self, v, off):
        self.v, self.off = v, off

    def __add__(self, n):
        return self.v + (self.off + n)


def rounds(eng, stages, last=4, width=U, tiles=TILES):
    for r in range(last):
        for stage, lag in stages:
            if r >= lag:
                stage(r - lag, (r - lag) % width)
    with eng.Fori(0, (tiles - last) // width) as u:
        for b in range(width):
            for stage, lag in stages:
                stage(Tile(u, last + b - lag, width), (last + b - lag) % width)
    for r in range(last + (tiles - last) // width * width, tiles + last):
        for stage, lag in stages:
            if 0 <= r - lag < tiles:
                stage(r - lag, (r - lag) % width)


def filled(t, b, n=1):
    if isinstance(t, int):
        return (t // U + 1) * 16 * n
    return t.u * (t.width // U * 16 * n) + (t.off // U + 1) * 16 * n


def half(b):
    return slice(64 * (b % 2), 64 * (b % 2) + 64)


def at(t):
    return bass.ds(t + 0, 1)


def mace_nodes(c):
    nc, a = c.nc, c.a
    norm(c)
    with ExitStack() as ctx:
        sb = lambda n, s: ctx.enter_context(nc.sbuf_tensor(f"mn_{n}", s, F32))
        w = sb("w", [128, 2, 128]); vT = sb("vT", [128, 3, N]); stage = sb("stage", [P, J, D])
        tp = ctx.enter_context(nc.psum_tensor("mn_tp", [128, 2, 512], F32))
        ps = ctx.enter_context(nc.psum_tensor("mn_ps", [P, 2, 512], F32))
        loaded, turned, copied = c.sem("mn_loaded"), c.sem("mn_turned"), c.sem("mn_copied")
        product, staged, stored = c.sem("mn_product"), c.sem("mn_staged"), c.sem("mn_stored")
        blk = ctx.enter_context(nc.Block())

        @blk.sync
        def _(sp):
            sp.dma_start(w[:, 0], a["W_up0"]).then_inc(loaded, 16)
            sp.dma_start(w[:, 1], a["W_up1"]).then_inc(loaded, 16)
            sp.wait_ge(staged, J)
            sp.dma_start(c.s0_table.rearrange("(j p) f -> p j f", p=P), stage[:, :, 0:128]).then_inc(stored, 16)
            sp.dma_start(c.s1_table.rearrange("(j p) f -> p j f", p=P), stage[:, :, 128:512]).then_inc(stored, 16)
            sp.wait_ge(stored, 32)

        @blk.tensor
        def _(pe):
            for j in range(J):
                if j >= 2:
                    pe.wait_ge(copied, j - 1)
                v = c.xn[:, j, 128:512].rearrange("p (u m) -> p m u", m=3)
                for m in range(3):
                    ins = pe.transpose(tp[:, j % 2, col(m)], v[:, m, :], c.ident[0:P, 0:P])
                ins.then_inc(turned, 1)
            pe.wait_ge(loaded, 32)
            for j in range(J):
                pe.wait_ge(copied, j + 1)
                if j >= 2:
                    pe.wait_ge(staged, j - 1)
                pe.matmul(ps[:, j % 2, 0:128], c.xnT[:, 0, col(j)], w[:, 0], start=True, stop=True)
                for m in range(3):
                    ins = pe.matmul(ps[:, j % 2, col(m + 1, 128)], vT[:, m, col(j)], w[:, 1], start=True, stop=True)
                ins.then_inc(product, 1)

        @blk.scalar
        def _(act):
            for j in range(J):
                act.wait_ge(turned, j + 1)
                act.activation(vT[:, :, col(j)], tp[:, j % 2, 0:3 * P].rearrange("q (m p) -> q m p", m=3),
                               ACT.Copy).then_inc(copied, 1)

        @blk.vector
        def _(dve):
            for j in range(J):
                dve.wait_ge(product, j + 1)
                dve.tensor_scalar(stage[:, j, :], ps[:, j % 2, :], 128.0 ** -0.5, None, ALU.mult).then_inc(staged, 1)


def mace_mlp(c, h3T):
    nc, a = c.nc, c.a
    CH = U * P
    G = E // 2 // CH // 2
    with ExitStack() as ctx:
        sb = lambda n, s: ctx.enter_context(nc.sbuf_tensor(f"mm_{n}", s, F32))
        f = sb("f", [16, 2, CH]); w1 = sb("w1", [16, 128]); w2 = sb("w2", [128, 128]); w3 = sb("w3", [128, 128])
        h = sb("h", [128, 2, 2, CH])
        ps = ctx.enter_context(nc.psum_tensor("mm_ps", [128, 2, 3, 512], F32))
        cleared, w_loaded, f_loaded = c.sem("mm_cleared"), c.sem("mm_w_loaded"), [c.sem(f"mm_f_loaded{i}") for i in range(2)]
        product, active = [[c.sem(f"mm_{n}{i}") for i in range(2)] for n in ("product", "active")]
        blk = ctx.enter_context(nc.Block())

        @blk.vector
        def _(dve):
            for t in (w1, w2, w3):
                dve.memset(t[:], 0.0).then_inc(cleared, 1)

        @blk.sync
        def _(sp):
            sp.wait_ge(cleared, 3)
            for t, n, k in ((w1, "W_mlp1", 8), (w2, "W_mlp2", 64), (w3, "W_mlp3", 64)):
                for i in range(2):
                    sp.dma_start(t[i * k:(i + 1) * k, col(i, 64)], a[n]).then_inc(w_loaded, 16)
            for i in range(2):
                sp.sem_inc(product[i], 3)
            with sp.Fori(0, G) as g:
                for i in range(2):
                    sp.wait_ge(product[i], g * 3 + 1)
                    sp.dma_start(f[:, i, :], a["ea8T"][:, bass.ds(g * (2 * CH) + i * CH, CH)]).then_inc(f_loaded[i], 16)

        @blk.tensor
        def _(pe):
            pe.wait_ge(w_loaded, 96)
            for i in range(2):
                pe.sem_inc(active[i], 3)
            with pe.Fori(0, G) as g:
                for n, w in enumerate((w1, w2, w3)):
                    for i in range(2):
                        if n == 0:
                            pe.wait_ge(f_loaded[i], g * 16 + 16)
                        pe.wait_ge(active[i], g * 3 + 3 + n)
                        rhs = f[:, i, :] if n == 0 else h[:, i, n - 1, :]
                        pe.matmul(ps[:, i, n, 0:CH], w[:], rhs, start=True, stop=True).then_inc(product[i], 1)

        @blk.scalar
        def _(act):
            with act.Fori(0, G) as g:
                for n in range(3):
                    for i in range(2):
                        act.wait_ge(product[i], g * 3 + 4 + n)
                        out = h[:, i, n, :] if n < 2 else h3T[:, bass.ds(g * (2 * CH) + i * CH, CH)]
                        scale = 8.0 ** -0.5 if n == 0 else SILU_2MOM / 8.0
                        act.activation(out, ps[:, i, n, 0:CH], ACT.Silu, scale=scale).then_inc(active[i], 1)


def mace_edges(c, h3T, vector, agg):
    nc, a = c.nc, c.a
    FR = mybir.dt.float32r
    tag = "mv" if vector else "ms"
    W = 384 if vector else 128
    table = c.s1_table if vector else c.s0_table
    K = SILU_2MOM / 8.0
    with ExitStack() as ctx:
        sb = lambda n, s, dt=F32: ctx.enter_context(nc.sbuf_tensor(f"{tag}_{n}", s, dt))
        ix = sb("ix", [P, U], I32); rows = sb("rows", [P, U, W]); hs = sb("hs", [128, U, P])
        w4 = sb("w4", [128, 256]); ea = sb("ea", [P, TILES, 4])
        hot = sb("hot", [P, U, N], FR); part = sb("part", [P, U, 256])
        msg = sb("msg", [P, U, D]); high = sb("high", [P, U, D], FR); low = sb("low", [P, U, D], FR)
        acc = ctx.enter_context(nc.psum_tensor(f"{tag}_acc", [P, J, 512], F32))
        tpw = ctx.enter_context(nc.psum_tensor(f"{tag}_tpw", [P, 2, 512], F32))
        loaded, indexed, go, h_staged = (c.sem(f"{tag}_{n}") for n in ("loaded", "indexed", "go", "h_staged"))
        gathered, before = c.gathered, c.gathers(1)
        w_ready, hot_ready, msg_ready, high_ready, low_ready, scattered, inner, copied = (
            c.sem(f"{tag}_{n}") for n in ("w_ready", "hot_ready", "msg_ready", "high_ready", "low_ready",
                                          "scattered", "inner", "copied"))
        blk = ctx.enter_context(nc.Block())

        @blk.sync
        def _(sp):
            for i in range(2):
                sp.dma_start(w4[col(i, 64)], a["W_mlp4"][:, 256:512] if vector else a["W_mlp4"][:, 0:256]).then_inc(loaded, 16)
            sp.dma_start(ea[:], a["ea4"]).then_inc(loaded, 16)

        @blk.gpsimd
        def _(pool):
            pool.sem_inc(msg_ready, 2 * U)

            def fetch(t, b):
                pool.wait_ge(msg_ready, t * 2 + 2)
                pool.tensor_copy(ix[:, b:b + 1], c.src_i[:, at(t)]).then_inc(indexed, 1)
                pool.wait_ge(indexed, t + 1)
                pool.sem_inc(go, 1)
                pool.indirect_dma_start(rows[:, b, :], None, table, bass.IndirectOffsetOnAxis(
                    ap=ix[:, b:b + 1], axis=0)).then_inc(gathered[b], 16)
            rounds(pool, [(fetch, 0)])

        @blk.tensor
        def _(pe):
            def weights(t, b):
                pe.wait_ge(h_staged, t + 1)
                pe.wait_ge(msg_ready, t * 2 + (2 * U - 2))
                pe.matmul(tpw[:, b % 2, 0:256], hs[half(b), b, :], w4[half(b), :], start=True, stop=True).then_inc(w_ready, 1)

            def scatter(narrow):
                def stage(t, b):
                    pe.wait_ge(hot_ready, t + 1)
                    pe.wait_ge(high_ready, t + 1)
                    pe.wait_ge(low_ready, t + 1)
                    add_targets(pe, c, acc, hot[:, b, :], [high[:, b, :], low[:, b, :]], t, narrow).then_inc(scattered, 1)
                return stage

            pe.sem_inc(scattered, U)
            pe.sem_inc(w_ready, U)
            open_accumulators(pe, c, acc)
            pe.wait_ge(loaded, 48)
            for_width(pe, c, lambda narrow: rounds(pe, [(weights, 0), (scatter(narrow), 3)]))
            close_accumulators(pe, c, acc).then_inc(scattered, 1)

        @blk.vector
        def _(dve):
            def gathered_rows(t, b):
                dve.wait_ge(scattered, t + 1)
                dve.wait_ge(gathered[b], filled(t, b) + before)
                dve.wait_ge(w_ready, t + (1 + U))

            def scalar_messages(narrow):
                def stage(t, b):
                    gathered_rows(t, b)
                    v = part[:, b, :].rearrange("p (g f) -> p g f", g=2)
                    dve.scalar_tensor_tensor(v, tpw[:, b % 2, 0:256].rearrange("p (g f) -> p g f", g=2), K,
                                             rows[:, b, :].unsqueeze(1).broadcast_to([P, 2, 128]),
                                             ALU.mult, ALU.mult).then_inc(inner, 1)
                    target_hot(dve, c, hot[:, b, :], t, narrow).then_inc(hot_ready, 1)
                    dve.wait_ge(inner, t + 1)
                    dve.tensor_scalar(msg[:, b, 0:128], v[:, 0, :], ea[:, at(t), 0], None, ALU.mult).then_inc(msg_ready, 1)
                    dve.tensor_tensor(msg[:, b, 128:512].rearrange("p (m f) -> p m f", m=3),
                                      v[:, 1:2, :].broadcast_to([P, 3, 128]),
                                      ea[:, at(t), 1:4].rearrange("p a m -> p (a m)").unsqueeze(2).broadcast_to([P, 3, 128]),
                                      ALU.mult).then_inc(msg_ready, 1)
                return stage

            def vector_messages(narrow):
                def stage(t, b):
                    gathered_rows(t, b)
                    s1 = rows[:, b, :].rearrange("p (m f) -> p m f", m=3)
                    dot, w3y = part[:, b, 0:128], part[:, b, 128:256]
                    dve.tensor_scalar(dot, s1[:, 0, :], ea[:, at(t), 1], None, ALU.mult).then_inc(inner, 1)
                    dve.tensor_scalar(w3y, tpw[:, b % 2, 0:128], ea[:, at(t), 0], K, ALU.mult, ALU.mult).then_inc(inner, 1)
                    target_hot(dve, c, hot[:, b, :], t, narrow).then_inc(hot_ready, 1)
                    dve.wait_ge(inner, t * 4 + 1)
                    dve.scalar_tensor_tensor(dot, s1[:, 1, :], ea[:, at(t), 2], dot, ALU.mult, ALU.add).then_inc(inner, 1)
                    dve.wait_ge(inner, t * 4 + 2)
                    dve.tensor_tensor(msg[:, b, 128:512].rearrange("p (m f) -> p m f", m=3), s1,
                                      w3y.unsqueeze(1).broadcast_to([P, 3, 128]), ALU.mult).then_inc(msg_ready, 1)
                    dve.wait_ge(inner, t * 4 + 3)
                    dve.scalar_tensor_tensor(dot, s1[:, 2, :], ea[:, at(t), 3], dot, ALU.mult, ALU.add).then_inc(inner, 1)
                    dve.wait_ge(inner, t * 4 + 4)
                    dve.scalar_tensor_tensor(msg[:, b, 0:128], tpw[:, b % 2, 128:256], K * 3.0 ** -0.5, dot,
                                             ALU.mult, ALU.mult).then_inc(msg_ready, 1)
                return stage

            def split_low(t, b):
                dve.wait_ge(high_ready, t + 1)
                dve.tensor_tensor(low[:, b, :], msg[:, b, :], high[:, b, :].bitcast(F32), ALU.subtract).then_inc(low_ready, 1)

            dve.wait_ge(loaded, 48)
            messages = vector_messages if vector else scalar_messages
            for_width(dve, c, lambda narrow: rounds(dve, [(messages(narrow), 1), (split_low, 2)]))

        @blk.scalar
        def _(act):
            def stage_hidden(t, b):
                pair = t // 2
                act.wait_ge(w_ready, t + 1)
                act.activation(hs[half(b), b, :], h3T.rearrange("q (t p) -> q t p", p=P)[half(b), at(pair), :].rearrange(
                    "q a p -> q (a p)"), ACT.Copy).then_inc(h_staged, 1)

            def split_high(t, b):
                act.wait_ge(msg_ready, t * 2 + (2 + 2 * U))
                act.activation(high[:, b, :], msg[:, b, :], ACT.Copy).then_inc(high_ready, 1)
            rounds(act, [(stage_hidden, 0), (split_high, 2)])
            act.wait_ge(scattered, U + TILES + 1)
            for j in range(J):
                act.activation(agg[:, j, :], acc[:, j, :], ACT.Copy).then_inc(copied, 1)


def mace_out(c, agg_s, agg_v):
    nc, a = c.nc, c.a
    with ExitStack() as ctx:
        sb = lambda n, s: ctx.enter_context(nc.sbuf_tensor(f"mo_{n}", s, F32))
        w = sb("w", [128, 2, 2, 128])
        aT = sb("aT", [128, 2, 4, N])
        tp = ctx.enter_context(nc.psum_tensor("mo_tp", [128, 2, 512], F32))
        ps = ctx.enter_context(nc.psum_tensor("mo_ps", [P, 2, 512], F32))
        loaded, turned, copied, product, added = (c.sem(f"mo_{n}") for n in (
            "loaded", "turned", "copied", "product", "added"))
        blk = ctx.enter_context(nc.Block())

        @blk.sync
        def _(sp):
            for i in range(2):
                sp.dma_start(w[:, i], a[f"W_out{i}"].rearrange("(h q) f -> q h f", q=128)).then_inc(loaded, 16)

        @blk.tensor
        def _(pe):
            for n in range(2 * J):
                j, agg = n // 2, (agg_s, agg_v)[n % 2]
                if n >= 2:
                    pe.wait_ge(copied, n - 1)
                for g in range(4):
                    ins = pe.transpose(tp[:, n % 2, col(g)], agg[:, j, col(g, 128)], c.ident[0:P, 0:P])
                ins.then_inc(turned, 1)
            pe.wait_ge(loaded, 32)
            for j in range(J):
                pe.wait_ge(copied, 2 * j + 2)
                if j >= 2:
                    pe.wait_ge(added, 2 * (j - 1))
                for g in range(4):
                    for h in range(2):
                        ins = pe.matmul(ps[:, j % 2, col(g, 128)], aT[:, h, g, col(j)], w[:, min(g, 1), h],
                                        start=(h == 0), stop=(h == 1))
                ins.then_inc(product, 1)

        @blk.scalar
        def _(act):
            for n in range(2 * J):
                act.wait_ge(turned, n + 1)
                act.activation(aT[:, n % 2, :, col(n // 2)], tp[:, n % 2, 0:4 * P].rearrange("q (g p) -> q g p", g=4),
                               ACT.Copy).then_inc(copied, 1)

        @blk.vector
        def _(dve):
            for j in range(J):
                dve.wait_ge(product, j + 1)
                dve.scalar_tensor_tensor(c.x[:, j, 0:128], ps[:, j % 2, 0:128], 1 / 160, c.x[:, j, 0:128],
                                         ALU.mult, ALU.add).then_inc(added, 1)
                v = c.x[:, j, 128:512].rearrange("p (v m) -> p m v", m=3)
                dve.scalar_tensor_tensor(v, ps[:, j % 2, 128:512].rearrange("p (m v) -> p m v", m=3), 1 / 160, v,
                                         ALU.mult, ALU.add).then_inc(added, 1)


def adjacency(c, degree):
    nc = c.nc
    BF = mybir.dt.bfloat16
    with ExitStack() as ctx:
        sb = lambda n, s, dt=F32: ctx.enter_context(nc.sbuf_tensor(f"ad_{n}", s, dt))
        src_hot = sb("src_hot", [P, U, N], BF); dst_hot = sb("dst_hot", [P, U, N], BF); counts = sb("counts", [P, J, N])
        acc = ctx.enter_context(nc.psum_tensor("ad_acc", [P, 7 * 512], F32))
        hot_ready, counted, copied, turned, done = (c.sem(f"ad_{n}") for n in (
            "hot_ready", "counted", "copied", "turned", "done"))
        blk = ctx.enter_context(nc.Block())
        LAST = J * 512

        @blk.vector
        def _(dve):
            def hots(narrow):
                def stage(t, b):
                    dve.wait_ge(counted, t + 1)
                    dve.tensor_scalar(src_hot[:, b, :], c.iota[:], c.src_f[:, at(t)], None, ALU.is_equal)
                    target_hot(dve, c, dst_hot[:, b, :], t, narrow).then_inc(hot_ready, 1)
                return stage
            for_width(dve, c, lambda narrow: rounds(dve, [(hots(narrow), 0)]))
            dve.wait_ge(copied, J + 2)
            dve.tensor_reduce(degree[:], counts[:], X, ALU.add).then_inc(done, 1)
            dve.wait_ge(done, 1)
            dve.tensor_scalar(degree[:], degree[:], 1.0, None, ALU.max).then_inc(done, 1)
            dve.wait_ge(done, 2)
            dve.reciprocal(degree[:], degree[:]).then_inc(done, 1)

        @blk.tensor
        def _(pe):
            def count(narrow):
                def stage(t, b):
                    pe.wait_ge(hot_ready, t + 1)
                    if narrow:
                        first = pe.value_load(c.first_i[0:1, at(t)], min_val=0, max_val=J - 2)
                    for n in range(2 if narrow else J):
                        bank = first * 512 + n * 512 if narrow else n * 512
                        fifth = first * 128 + (LAST + n * 128) if narrow else LAST + n * 128
                        pe.matmul(acc[:, bass.ds(bank, 4 * P)], dst_hot[:, b, col(n)], src_hot[:, b, 0:4 * P],
                                  start=False, stop=False)
                        ins = pe.matmul(acc[:, bass.ds(fifth, P)], dst_hot[:, b, col(n)], src_hot[:, b, 4 * P:N],
                                        start=False, stop=False)
                    ins.then_inc(counted, 1)
                return stage

            pe.sem_inc(counted, U)
            for k in range(7):
                pe.matmul(acc[:, col(k, 512)], c.zeros[:, 0:P], c.zeros[:], start=True, stop=False)
            for_width(pe, c, lambda narrow: rounds(pe, [(count(narrow), 0)]))
            for k in range(7):
                ins = pe.matmul(acc[:, col(k, 512)], c.zeros[:, 0:P], c.zeros[:], start=False, stop=True)
            ins.then_inc(counted, 1)
            pe.wait_ge(copied, J + 2)
            for unit in range(J * J):
                i, n, place = unit // J, unit % J, unit // 4 * 512 + unit % 4 * P
                ins = pe.transpose(acc[:, place:place + P], counts[:, n, col(i)], c.ident[0:P, 0:P])
                if unit % 4 == 3 or unit == J * J - 1:
                    ins.then_inc(turned, 1)

        @blk.scalar
        def _(act):
            act.wait_ge(counted, U + TILES + 1)
            for n in range(J):
                act.activation(counts[:, n, 0:4 * P], acc[:, n * 512:n * 512 + 4 * P], ACT.Copy).then_inc(copied, 1)
            act.activation(counts[:, 0:4, 4 * P:N], acc[:, LAST:LAST + 512].rearrange("p (n f) -> p n f", f=128)[:, :, 0:P],
                           ACT.Copy).then_inc(copied, 1)
            act.activation(counts[:, 4, 4 * P:N], acc[:, LAST + 512:LAST + 512 + P], ACT.Copy).then_inc(copied, 1)
            flat = c.adjT[:].rearrange("p i n -> p (i n)")
            for k in range(7):
                width = min(4 * P, J * N - k * 4 * P)
                act.wait_ge(turned, k + 1)
                act.activation(flat[:, k * 4 * P:k * 4 * P + width], acc[:, k * 512:k * 512 + width], ACT.Copy)


def sage_layer(c, l, h, degree, final):
    nc, a = c.nc, c.a
    tag = f"sg{l}"
    with ExitStack() as ctx:
        sb = lambda n, s: ctx.enter_context(nc.sbuf_tensor(f"{tag}_{n}", s, F32))
        wl = sb("wl", [128, KT, D]); wr = sb("wr", [128, KT, D]); bl = sb("bl", [1, D])
        gain = sb("gain", [P, D]); bias = sb("bias", [P, D]); slope = sb("slope", [P, 1])
        agg = sb("agg", [P, J, D]); aggT = sb("aggT", [128, KT, N]); hT = sb("hT", [128, KT, N])
        y = sb("y", [P, J, D]); st = sb("st", [P, J, 6]); mv = sb("mv", [P, J, 2])
        acc = ctx.enter_context(nc.psum_tensor(f"{tag}_acc", [P, J, 512], F32))
        tp = ctx.enter_context(nc.psum_tensor(f"{tag}_tp", [128, 3, 512], F32))
        w_loaded, n_loaded = c.sem(f"{tag}_w_loaded"), c.sem(f"{tag}_n_loaded")
        summed, averaged, turned, copied, product = (c.sem(f"{tag}_{n}") for n in (
            "summed", "averaged", "turned", "copied", "product"))
        steps, var_ready, rooted = c.sem(f"{tag}_steps"), c.sem(f"{tag}_var_ready"), c.sem(f"{tag}_rooted")
        blk = ctx.enter_context(nc.Block())

        @blk.sync
        def _(sp):
            sp.dma_start(wl[:], a[f"Wl{l}"].rearrange("(k q) f -> q k f", q=128)).then_inc(w_loaded, 16)
            sp.dma_start(wr[:], a[f"Wr{l}"].rearrange("(k q) f -> q k f", q=128)).then_inc(w_loaded, 16)
            sp.dma_start(bl[:], a[f"bl{l}"]).then_inc(w_loaded, 16)
            sp.dma_start(gain[:], a[f"g{l}"].partition_broadcast(P)).then_inc(n_loaded, 16)
            sp.dma_start(bias[:], a[f"b{l}"].partition_broadcast(P)).then_inc(n_loaded, 16)
            sp.dma_start(slope[:], a["a_prelu"].partition_broadcast(P)).then_inc(n_loaded, 16)

        @blk.tensor
        def _(pe):
            for j in range(J):
                for i in range(J):
                    ins = pe.matmul(acc[:, j, :], c.adjT[:, i, col(j)], h[:, i, :], start=(i == 0), stop=(i == J - 1))
                ins.then_inc(summed, 1)
            for n in range(2 * J):
                j, s = n % J, (h, agg)[n // J]
                if n >= 3:
                    pe.wait_ge(copied, n - 2)
                if n >= J:
                    pe.wait_ge(averaged, j + 1)
                for k in range(KT):
                    ins = pe.transpose(tp[:, n % 3, col(k)], s[:, j, col(k, 128)], c.ident[0:P, 0:P])
                ins.then_inc(turned, 1)
            pe.wait_ge(w_loaded, 48)
            for j in range(J):
                pe.wait_ge(averaged, j + 1)
                pe.wait_ge(copied, J + j + 1)
                for k in range(KT):
                    pe.matmul(acc[:, j, :], hT[:, k, col(j)], wr[:, k, :], start=(k == 0), stop=False)
                for k in range(KT):
                    pe.matmul(acc[:, j, :], aggT[:, k, col(j)], wl[:, k, :], start=False, stop=False)
                pe.matmul(acc[:, j, :], c.ones[:, 0:P], bl[:], start=False, stop=True).then_inc(product, 1)

        @blk.scalar
        def _(act):
            for n in range(2 * J):
                act.wait_ge(turned, n + 1)
                act.activation((hT, aggT)[n // J][:, :, col(n % J)],
                               tp[:, n % 3, 0:KT * P].rearrange("q (k p) -> q k p", k=KT), ACT.Copy).then_inc(copied, 1)
            act.wait_ge(var_ready, 1)
            act.activation(mv[:, :, 1], mv[:, :, 1], ACT.Sqrt).then_inc(rooted, 1)

        @blk.vector
        def _(dve):
            step = Chain(dve, steps)
            for j in range(J):
                dve.wait_ge(summed, j + 1)
                dve.tensor_scalar(agg[:, j, :], acc[:, j, :], degree[:, j:j + 1], None, ALU.mult).then_inc(averaged, 1)
            for j in range(J):
                dve.wait_ge(product, j + 1)
                if l == 0:
                    step(dve.tensor_copy(y[:, j, :], acc[:, j, :]))
                else:
                    step(dve.tensor_tensor(y[:, j, :], acc[:, j, :], h[:, j, :], ALU.add))
                step(dve.bn_stats(st[:, j, :], y[:, j, :]))
                step(dve.bn_aggr(mv[:, j, :], st[:, j, :]))
            dve.tensor_scalar(mv[:, :, 1], mv[:, :, 1], EPS, None, ALU.add).then_inc(var_ready, 1)
            dve.wait_ge(rooted, 1)
            step(dve.reciprocal(mv[:, :, 1], mv[:, :, 1]))
            dve.wait_ge(n_loaded, 48)
            for j in range(J):
                step(dve.tensor_scalar(y[:, j, :], y[:, j, :], mv[:, j, 0:1], mv[:, j, 1:2], ALU.subtract, ALU.mult))
                step(dve.tensor_tensor(y[:, j, :], y[:, j, :], gain[:], ALU.mult))
                step(dve.tensor_tensor(y[:, j, :], y[:, j, :], bias[:], ALU.add))
                step(dve.tensor_scalar(agg[:, j, :], y[:, j, :], 0.0, slope[:], ALU.min, ALU.mult))
                step(dve.scalar_tensor_tensor(h[:, j, :], y[:, j, :], 0.0, agg[:, j, :], ALU.max, ALU.add))
                if final:
                    step(dve.tensor_tensor(c.x[:, j, :], c.x[:, j, :], h[:, j, :], ALU.add))


def edge_nodes(c):
    nc, a = c.nc, c.a
    norm(c)
    with ExitStack() as ctx:
        sb = lambda n, s: ctx.enter_context(nc.sbuf_tensor(f"en_{n}", s, F32))
        w = sb("w", [128, 2, KT, D]); b = sb("b", [1, D]); stage = sb("stage", [P, 2, J, D])
        ps = ctx.enter_context(nc.psum_tensor("en_ps", [P, 4, 512], F32))
        loaded, product, staged, stored = (c.sem(f"en_{n}") for n in ("loaded", "product", "staged", "stored"))
        blk = ctx.enter_context(nc.Block())

        @blk.sync
        def _(sp):
            for s in range(2):
                sp.dma_start(w[:, s], a["E_W1"][s * D:(s + 1) * D].rearrange("(k q) f -> q k f", q=128)).then_inc(loaded, 16)
            sp.dma_start(b[:], a["E_b1"]).then_inc(loaded, 16)
            for s, table in enumerate((c.xs_table, c.xd_table)):
                sp.wait_ge(staged, (s + 1) * J)
                sp.dma_start(table.rearrange("(j p) f -> p j f", p=P), stage[:, s]).then_inc(stored, 16)
            sp.wait_ge(stored, 32)

        @blk.tensor
        def _(pe):
            pe.wait_ge(loaded, 48)
            for n in range(2 * J):
                s, j = n // J, n % J
                if n >= 4:
                    pe.wait_ge(staged, n - 3)
                for k in range(KT):
                    ins = pe.matmul(ps[:, n % 4, :], c.xnT[:, k, col(j)], w[:, s, k, :], start=(k == 0),
                                    stop=(k == KT - 1 and s == 0))
                if s == 1:
                    ins = pe.matmul(ps[:, n % 4, :], c.ones[:, 0:P], b[:], start=False, stop=True)
                ins.then_inc(product, 1)

        @blk.scalar
        def _(act):
            for n in range(2 * J):
                act.wait_ge(product, n + 1)
                act.activation(stage[:, n // J, n % J, :], ps[:, n % 4, :], ACT.Copy).then_inc(staged, 1)


def edge_messages(c, agg):
    nc, a = c.nc, c.a
    FR = mybir.dt.float32r
    W = 2 * U
    SECOND = 3
    with ExitStack() as ctx:
        sb = lambda n, s, dt=F32: ctx.enter_context(nc.sbuf_tensor(f"em_{n}", s, dt))
        ix = sb("ix", [P, U, 2], I32); rows = sb("rows", [P, U, 2, D])
        ea = sb("ea", [128, 2, U * P]); ea_high = sb("ea_high", [128, 2, U * P], FR); ea_both = sb("ea_both", [128, 2, U * P], FR)
        w1 = sb("w1", [128, D]); w1_high = sb("w1_high", [128, D], FR); w1_low = sb("w1_low", [64, D], FR)
        w2 = sb("w2", [128, KT, D]); w2_high = sb("w2_high", [128, KT, D], FR); w2_low = sb("w2_low", [128, KT, D], FR)
        b2 = sb("b2", [P, D])
        z1 = sb("z1", [P, W, D]); q1 = sb("q1", [P, W, D]); h = sb("h", [P, 2, D])
        hT_high = sb("hT_high", [128, 2, KT * P], FR); hT_low = sb("hT_low", [128, 2, KT * P], FR)
        z2 = sb("z2", [P, W, D]); q2 = sb("q2", [P, W, D]); msg = sb("msg", [P, 2, D]); hot = sb("hot", [P, 2, N])
        acc = ctx.enter_context(nc.psum_tensor("em_acc", [P, J, 512], F32))
        z1p = ctx.enter_context(nc.psum_tensor("em_z1p", [P, 512], F32))
        z2p = ctx.enter_context(nc.psum_tensor("em_z2p", [P, 512], F32))
        tp = ctx.enter_context(nc.psum_tensor("em_tp", [128, 512], F32))
        (w_loaded, w_high_ready, w_ready, ea_high_ready, ea_ready, indexed, go, edge_product, z1_partial, z1_ready,
         q1_ready, h_ready, turned, high_ready, hT_ready, product, z2_ready, q2_ready, msg_ready, hot_ready, scattered,
         copied, angles1, angles2) = (c.sem(f"em_{n}") for n in (
            "w_loaded", "w_high_ready", "w_ready", "ea_high_ready", "ea_ready", "indexed", "go", "edge_product",
            "z1_partial", "z1_ready", "q1_ready", "h_ready", "turned", "high_ready", "hT_ready", "product", "z2_ready",
            "q2_ready", "msg_ready", "hot_ready", "scattered", "copied", "angles1", "angles2"))
        gathered, before = c.gathered, c.gathers(2)
        ea_loaded = [c.sem(f"em_ea_loaded{b}") for b in range(2)]
        blk = ctx.enter_context(nc.Block())
        EDGE, FIRST, HIDDEN, TURN, COPY, PRODUCT, OUTPUT = 0, 1, W, W + 1, W + 2, W + 3, W + 4
        MESSAGE, SCATTER, ROUNDS = OUTPUT + W - 1, OUTPUT + W, 3 * W
        tile_rounds = lambda eng, stages: rounds(eng, stages, ROUNDS, W)

        @blk.sync
        def _(sp):
            for i in range(2):
                sp.dma_start(w1[col(i, 64)], a["E_W1"][2 * D:2 * D + 64]).then_inc(w_loaded, 16)
            sp.dma_start(w2[:], a["E_W2"].rearrange("(k q) f -> q k f", q=128)).then_inc(w_loaded, 16)
            sp.dma_start(b2[:], a["E_b2"].partition_broadcast(P)).then_inc(w_loaded, 16)
            sp.sem_inc(ea_ready, 2)
            with sp.Fori(0, TURNS // 2) as u:
                for i in range(2):
                    sp.wait_ge(ea_ready, u * 2 + i + 1)
                    for half_rows in range(2):
                        sp.dma_start(ea[col(half_rows, 64), i, :],
                                     a["ea64T"][:, bass.ds(u * (W * P) + i * (U * P), U * P)]).then_inc(ea_loaded[i], 16)

        @blk.gpsimd
        def _(pool):
            pool.sem_inc(z1_ready, U)

            def fetch(t, b):
                b = b % U
                pool.wait_ge(z1_ready, t + 1)
                pool.tensor_copy(ix[:, b, 0:1], c.src_i[:, at(t)]).then_inc(indexed, 1)
                pool.tensor_copy(ix[:, b, 1:2], c.dst_i[:, at(t)]).then_inc(indexed, 1)
                pool.wait_ge(indexed, t * 2 + 2)
                pool.sem_inc(go, 1)
                for n, table in enumerate((c.xs_table, c.xd_table)):
                    pool.indirect_dma_start(rows[:, b, n, :], None, table, bass.IndirectOffsetOnAxis(
                        ap=ix[:, b, n:n + 1], axis=0)).then_inc(gathered[b], 16)
            rounds(pool, [(fetch, 0)])

        @blk.tensor
        def _(pe):
            def edge_part(t, b):
                g = b // U % 2
                pe.wait_ge(ea_ready, t // U + 3)
                pe.wait_ge(z1_partial, t + 1)
                place = col(b % U)
                pe.matmul(z1p[0:P, :], ea_both[:, g, place], w1_high[:], start=True, stop=False)
                pe.matmul(z1p[0:P, :], ea_both[0:64, g, place], w1_low[:], start=False, stop=True).then_inc(edge_product, 1)

            def turn_h(t, b):
                pe.wait_ge(h_ready, t + (1 + W))
                pe.wait_ge(hT_ready, t + 1)
                for k in range(KT):
                    ins = pe.transpose(tp[:, col(k)], h[:, b % 2, col(k, 128)], c.ident[0:P, 0:P])
                ins.then_inc(turned, 1)

            def second(t, b):
                pe.wait_ge(hT_ready, t + 2)
                pe.wait_ge(z2_ready, t + 1)
                terms = [(x, y, k) for k in range(KT) for x, y in
                         ((hT_high, w2_high), (hT_low, w2_high), (hT_high, w2_low))]
                for n, (x, y, k) in enumerate(terms):
                    ins = pe.matmul(z2p[0:P, :], x[:, b % 2, col(k)], y[:, k, :], start=(n == 0), stop=(n == len(terms) - 1))
                ins.then_inc(product, 1)

            def scatter(narrow):
                def stage(t, b):
                    pe.wait_ge(msg_ready, t + (1 + W))
                    pe.wait_ge(hot_ready, t + 1)
                    add_targets(pe, c, acc, hot[:, b % 2, :], [msg[:, b % 2, :]], t, narrow).then_inc(scattered, 1)
                return stage

            pe.sem_inc(z1_partial, 1)
            pe.sem_inc(z2_ready, 1)
            pe.sem_inc(hT_ready, 1)
            for freed in (scattered, turned, product):
                pe.sem_inc(freed, 2)
            for freed in (h_ready, msg_ready, edge_product):
                pe.sem_inc(freed, W)
            open_accumulators(pe, c, acc)
            pe.wait_ge(w_ready, 2)
            for_width(pe, c, lambda narrow: tile_rounds(
                pe, [(scatter(narrow), SCATTER), (second, PRODUCT), (edge_part, EDGE), (turn_h, TURN)]))
            close_accumulators(pe, c, acc).then_inc(scattered, 1)

        @blk.vector
        def _(dve):
            def split_features(t, b):
                if b % U:
                    return
                g = b // U % 2
                dve.wait_ge(ea_high_ready, t // U + 1)
                dve.tensor_tensor(ea_both[64:128, g, :], ea[64:128, g, :], ea_high[64:128, g, :].bitcast(F32),
                                  ALU.subtract).then_inc(ea_ready, 1)

            def first(t, b):
                dve.wait_ge(edge_product, t + (1 + W))
                dve.wait_ge(gathered[b % U], filled(t, b, 2) + before)
                dve.wait_ge(h_ready, t + 1)
                dve.tensor_tensor(z1[:, b, :], z1p[0:P, :], rows[:, b % U, 0, :], ALU.add).then_inc(z1_partial, 1)
                dve.wait_ge(z1_partial, t + 2)
                dve.tensor_tensor(z1[:, b, :], z1[:, b, :], rows[:, b % U, 1, :], ALU.add).then_inc(z1_ready, 1)

            def hidden(t, b):
                dve.wait_ge(q1_ready, t // U + 1)
                dve.wait_ge(turned, t + 1)
                dve.tensor_tensor(h[:, b % 2, :], z1[:, b, :], q1[:, b, :], ALU.mult).then_inc(h_ready, 1)

            def copy_turned(t, b):
                dve.wait_ge(turned, t + 3)
                dve.wait_ge(product, t + 1)
                dve.tensor_copy(hT_high[:, b % 2, :], tp[:, 0:KT * P]).then_inc(high_ready, 1)
                dve.wait_ge(high_ready, t + 1)
                dve.tensor_tensor(hT_low[:, b % 2, :], tp[:, 0:KT * P], hT_high[:, b % 2, :].bitcast(F32),
                                  ALU.subtract).then_inc(hT_ready, 1)

            def output(t, b):
                dve.wait_ge(product, t + 3)
                dve.wait_ge(msg_ready, t + 1)
                dve.tensor_tensor(z2[:, b, :], z2p[0:P, :], b2[:], ALU.add).then_inc(z2_ready, 1)

            def message(narrow):
                def stage(t, b):
                    dve.wait_ge(scattered, t + 1)
                    target_hot(dve, c, hot[:, b % 2, :], t, narrow).then_inc(hot_ready, 1)
                    dve.wait_ge(q2_ready, t // U + 1)
                    dve.tensor_tensor(msg[:, b % 2, :], z2[:, b, :], q2[:, b, :], ALU.mult).then_inc(msg_ready, 1)
                return stage

            dve.wait_ge(w_high_ready, 2)
            dve.tensor_tensor(w2_low[:], w2[:], w2_high[:].bitcast(F32), ALU.subtract).then_inc(w_ready, 1)
            dve.tensor_tensor(w1_low[:], w1[0:64, :], w1_high[0:64, :].bitcast(F32), ALU.subtract).then_inc(w_ready, 1)
            for_width(dve, c, lambda narrow: tile_rounds(
                dve, [(output, OUTPUT), (split_features, EDGE), (first, FIRST), (copy_turned, COPY),
                      (message(narrow), MESSAGE), (hidden, HIDDEN)]))

        @blk.scalar
        def _(act):
            def features(G, p):
                act.wait_ge(ea_loaded[p], G // 2 * 32 + 32 if isinstance(G, int) else G.u * 32 + (G.off // 2 * 32 + 32))
                act.wait_ge(ea_ready, G + 1)
                act.wait_ge(edge_product, G * U + (2 * U - U))
                act.activation(ea_high[64:128, p, :], ea[64:128, p, :], ACT.Copy)
                act.activation(ea_both[0:64, p, :], ea[0:64, p, :], ACT.Copy).then_inc(ea_high_ready, 1)

            def angle(z, q, sums, credits, angles):
                def stage(G, p):
                    slots = slice(p * U, (p + 1) * U)
                    act.wait_ge(sums, G * U + (U + credits))
                    act.activation(q[:, slots, :], z[:, slots, :], ACT.Sigmoid, scale=-1.0).then_inc(angles, 1)
                    act.wait_ge(angles, G * 2 + 1)
                    act.activation(q[:, slots, :], q[:, slots, :], ACT.Arctan).then_inc(angles, 1)
                return stage

            def factor(q, angles, done):
                def stage(G, p):
                    slots = slice(p * U, (p + 1) * U)
                    act.wait_ge(angles, G * 2 + 2)
                    act.activation(q[:, slots, :], q[:, slots, :], ACT.Sin, scale=-2.0, bias=c.half_pi[:]).then_inc(done, 1)
                return stage

            act.wait_ge(w_loaded, 64)
            act.activation(w2_high[:], w2[:], ACT.Copy).then_inc(w_high_ready, 1)
            act.activation(w1_high[:], w1[:], ACT.Copy).then_inc(w_high_ready, 1)
            rounds(act, [(features, 0), (angle(z2, q2, z2_ready, 1, angles2), 1 + SECOND), (angle(z1, q1, z1_ready, U, angles1), 1),
                         (factor(q2, angles2, q2_ready), 1 + SECOND), (factor(q1, angles1, q1_ready), 1)],
                   4, 2, TURNS)
            act.wait_ge(scattered, 2 + TILES + 1)
            for j in range(J):
                act.activation(agg[:, j, :], acc[:, j, :], ACT.Copy).then_inc(copied, 1)


def edge_out(c, agg):
    nc, a = c.nc, c.a
    with ExitStack() as ctx:
        sb = lambda n, s: ctx.enter_context(nc.sbuf_tensor(f"eo_{n}", s, F32))
        w3 = sb("w3", [128, 2 * KT, D]); w4 = sb("w4", [128, KT, D]); b3 = sb("b3", [1, D]); b4 = sb("b4", [1, D])
        gain = sb("gain", [P, D]); bias = sb("bias", [P, D])
        aggT = sb("aggT", [128, KT, N]); uT = sb("uT", [128, KT, N])
        z = sb("z", [P, J, D]); q = sb("q", [P, J, D]); y = sb("y", [P, J, D])
        st = sb("st", [P, J, 6]); mv = sb("mv", [P, J, 2])
        acc = ctx.enter_context(nc.psum_tensor("eo_acc", [P, J, 512], F32))
        tp = ctx.enter_context(nc.psum_tensor("eo_tp", [128, 3, 512], F32))
        (w_loaded, n_loaded, turned, copied, product, taken, squared, q_ready, u_ready, out_ready, steps, var_ready,
         rooted) = (c.sem(f"eo_{n}") for n in (
            "w_loaded", "n_loaded", "turned", "copied", "product", "taken", "squared", "q_ready", "u_ready",
            "out_ready", "steps", "var_ready", "rooted"))
        blk = ctx.enter_context(nc.Block())

        @blk.sync
        def _(sp):
            sp.dma_start(w3[:], a["E_W3"].rearrange("(k q) f -> q k f", q=128)).then_inc(w_loaded, 16)
            sp.dma_start(b3[:], a["E_b3"]).then_inc(w_loaded, 16)
            sp.dma_start(w4[:], a["E_W4"].rearrange("(k q) f -> q k f", q=128)).then_inc(w_loaded, 16)
            sp.dma_start(b4[:], a["E_b4"]).then_inc(w_loaded, 16)
            sp.dma_start(gain[:], a["E_gamma"].partition_broadcast(P)).then_inc(n_loaded, 16)
            sp.dma_start(bias[:], a["E_beta"].partition_broadcast(P)).then_inc(n_loaded, 16)

        @blk.tensor
        def _(pe):
            for n in range(J):
                if n >= 3:
                    pe.wait_ge(copied, n - 2)
                for k in range(KT):
                    ins = pe.transpose(tp[:, n % 3, col(k)], agg[:, n, col(k, 128)], c.ident[0:P, 0:P])
                ins.then_inc(turned, 1)
            pe.wait_ge(w_loaded, 64)
            for j in range(J):
                pe.wait_ge(copied, j + 1)
                for k in range(2 * KT):
                    lhs = c.xnT[:, k, col(j)] if k < KT else aggT[:, k - KT, col(j)]
                    pe.matmul(acc[:, j, :], lhs, w3[:, k, :], start=(k == 0), stop=False)
                pe.matmul(acc[:, j, :], c.ones[:, 0:P], b3[:], start=False, stop=True).then_inc(product, 1)
            for j in range(J):
                pe.wait_ge(u_ready, j + 1)
                pe.wait_ge(copied, J if j < 1 else J + j - 1)
                for k in range(KT):
                    ins = pe.transpose(tp[:, j % 3, col(k)], y[:, j, col(k, 128)], c.ident[0:P, 0:P])
                ins.then_inc(turned, 1)
            for j in range(J):
                pe.wait_ge(copied, J + j + 1)
                for k in range(KT):
                    pe.matmul(acc[:, j, :], uT[:, k, col(j)], w4[:, k, :], start=(k == 0), stop=False)
                pe.matmul(acc[:, j, :], c.ones[:, 0:P], b4[:], start=False, stop=True).then_inc(out_ready, 1)

        @blk.scalar
        def _(act):
            def copy(n, dst):
                act.wait_ge(turned, n + 1)
                act.activation(dst[:, :, col(n % J)], tp[:, n % J % 3, 0:KT * P].rearrange("q (k p) -> q k p", k=KT),
                               ACT.Copy).then_inc(copied, 1)
            for n in range(J):
                copy(n, aggT)
            for j in range(J):
                act.wait_ge(taken, j + 1)
                act.activation(q[:, j, :], z[:, j, :], ACT.Sigmoid, scale=-1.0).then_inc(squared, 1)
                act.wait_ge(squared, 2 * j + 1)
                act.activation(q[:, j, :], q[:, j, :], ACT.Arctan).then_inc(squared, 1)
            for j in range(J):
                act.wait_ge(squared, 2 * j + 2)
                act.activation(q[:, j, :], q[:, j, :], ACT.Sin, scale=-2.0, bias=c.half_pi[:]).then_inc(q_ready, 1)
            for n in range(J, 2 * J):
                copy(n, uT)
            act.wait_ge(var_ready, 1)
            act.activation(mv[:, :, 1], mv[:, :, 1], ACT.Sqrt).then_inc(rooted, 1)

        @blk.vector
        def _(dve):
            step = Chain(dve, steps)
            for j in range(J):
                dve.wait_ge(product, j + 1)
                dve.tensor_copy(z[:, j, :], acc[:, j, :]).then_inc(taken, 1)
            for j in range(J):
                dve.wait_ge(q_ready, j + 1)
                dve.tensor_tensor(y[:, j, :], z[:, j, :], q[:, j, :], ALU.mult).then_inc(u_ready, 1)
            dve.wait_ge(copied, 2 * J)
            for j in range(J):
                dve.wait_ge(out_ready, j + 1)
                step(dve.tensor_tensor(y[:, j, :], acc[:, j, :], c.xn[:, j, :], ALU.add))
                step(dve.bn_stats(st[:, j, :], y[:, j, :]))
                step(dve.bn_aggr(mv[:, j, :], st[:, j, :]))
            dve.tensor_scalar(mv[:, :, 1], mv[:, :, 1], EPS, None, ALU.add).then_inc(var_ready, 1)
            dve.wait_ge(rooted, 1)
            step(dve.reciprocal(mv[:, :, 1], mv[:, :, 1]))
            dve.wait_ge(n_loaded, 32)
            for j in range(J):
                step(dve.tensor_scalar(y[:, j, :], y[:, j, :], mv[:, j, 0:1], mv[:, j, 1:2], ALU.subtract, ALU.mult))
                step(dve.tensor_tensor(y[:, j, :], y[:, j, :], gain[:], ALU.mult))
                step(dve.tensor_tensor(y[:, j, :], y[:, j, :], bias[:], ALU.add))
                step(dve.tensor_tensor(c.x[:, j, :], c.x[:, j, :], y[:, j, :], ALU.add))


def store(c):
    with ExitStack() as ctx:
        stored = c.sem("out_stored")
        blk = ctx.enter_context(c.nc.Block())

        @blk.sync
        def _(sp):
            sp.dma_start(c.a["out"].rearrange("(j p) d -> p j d", p=P), c.x[:]).then_inc(stored, 16)
            sp.wait_ge(stored, 16)


def program(nc, a):
    ctx = ExitStack()
    with ctx:
        c = Core(nc, ctx, a)
        buf = lambda s, name, shape: s.enter_context(nc.sbuf_tensor(name, shape, F32))
        setup(c)
        if STAGES >= 1:
            norm(c)
            with ExitStack() as s:
                h_self = buf(s, "h_self", [P, J, D])
                rel_tables(c, h_self)
                rel_edges(c, h_self)
        c.recycle()
        if STAGES >= 2:
            ffn_large(c)
        if STAGES >= 3:
            mace_nodes(c)
            with ExitStack() as s:
                agg_s, agg_v = buf(s, "agg_s", [P, J, D]), buf(s, "agg_v", [P, J, D])
                with ExitStack() as s2:
                    h3T = buf(s2, "h3T", [128, E // 2])
                    mace_mlp(c, h3T)
                    mace_edges(c, h3T, False, agg_s)
                    mace_edges(c, h3T, True, agg_v)
                mace_out(c, agg_s, agg_v)
        c.recycle()
        if STAGES >= 4:
            ffn_small(c, "f1", "switch", ACT.Gelu)
        c.recycle()
        if STAGES >= 5:
            with ExitStack() as s:
                degree = buf(s, "degree", [P, J])
                adjacency(c, degree)
                norm(c)
                for l in range(3):
                    sage_layer(c, l, c.xn, degree, l == 2)
        if STAGES >= 6:
            ffn_small(c, "f2", "top2_capacity", ACT.Gelu_apprx_tanh)
        c.recycle()
        if STAGES >= 7:
            edge_nodes(c)
            with ExitStack() as s:
                agg = buf(s, "agg_e", [P, J, D])
                edge_messages(c, agg)
                edge_out(c, agg)
        if STAGES >= 8:
            ffn_small(c, "f3", "top2_scores", ACT.Gelu)
        store(c)


STAGES = 8


def kernel(**v):
    import numpy as np
    import concourse.bacc as bacc
    from concourse.bass_utils import run_bass_kernel_spmd as run

    v = {k: np.asarray(x) for k, x in v.items()}
    cut = lambda x: x.reshape(2, TILES // 2, P, -1).transpose(1, 0, 2, 3).reshape(TILES, P, -1)
    tiles = lambda x: cut(x)[:, :, 0].T
    row = lambda x: x.reshape(1, -1)
    arrays = {
        "x": v["x"], "src": tiles(v["src"]), "dst": tiles(v["dst"]), "rel": tiles(v["edge_type_8"]),
        "dst_by_tile": v["dst"].reshape(2, TILES // 2, P).transpose(1, 0, 2),
        "ea4": cut(v["edge_attr_4"]).transpose(1, 0, 2),
        "ea8T": v["edge_attr_8"].reshape(2, E // 2, 8).transpose(0, 2, 1).reshape(16, E // 2),
        "ea64T": cut(v["edge_attr_64"]).reshape(E, 64).T,
        "iota": np.arange(N, dtype=np.float32), "ident": np.eye(128, dtype=np.float32),
        "spread": np.repeat(np.eye(NE, dtype=np.float32), 64, axis=1),
        "earlier": np.triu(np.ones((P, P), dtype=np.float32), 1),
        "W_rel": np.concatenate([v["L0_gnn_W_rel"], v["L0_gnn_W_self"][None]]).transpose(0, 2, 1).reshape(-1, D),
        "b_rel": np.concatenate([v["L0_gnn_b_rel"], v["L0_gnn_b_self"][None]]),
        "fl_wg": v["L0_ffn_wg"], "fl_bg": row(v["L0_ffn_bg"]), "fl_w1": v["L0_ffn_w1"], "fl_w3": v["L0_ffn_w3"],
        "fl_w2": v["L0_ffn_w2"], "a_prelu": v["L2_gnn_a_prelu"],
    }
    for n in ("W_up0", "W_up1", "W_mlp1", "W_mlp2", "W_mlp3", "W_mlp4", "W_out0", "W_out1"):
        arrays[n] = v["L1_gnn_" + n]
    for l in range(3):
        arrays[f"Wl{l}"], arrays[f"Wr{l}"] = v[f"L2_gnn_Wl{l}"].T, v[f"L2_gnn_Wr{l}"].T
        arrays[f"bl{l}"], arrays[f"g{l}"], arrays[f"b{l}"] = row(v[f"L2_gnn_bl{l}"]), v[f"L2_gnn_g{l}"], v[f"L2_gnn_b{l}"]
    for n in ("W1", "W2", "W3", "W4", "gamma", "beta", "b2"):
        arrays["E_" + n] = v["L3_gnn_" + n]
    for n in ("b1", "b3", "b4"):
        arrays["E_" + n] = row(v["L3_gnn_" + n])
    zero_bias = np.zeros((1, NE), np.float32)
    for tag, wg, bg, m in (("f1", "L1_ffn_Ws", "L1_ffn_bs", ("W1", "b1", "W2", "b2")),
                           ("f2", "L2_ffn_router_w", None, ("w1", "b1", "w2", "b2")),
                           ("f3", "L3_ffn_Wg", "L3_ffn_bg", ("W1", "b1", "W2", "b2"))):
        w1, b1, w2, b2 = (v[wg[:7] + n] for n in m)
        arrays[tag + "_wg"], arrays[tag + "_bg"] = v[wg], row(v[bg]) if bg else zero_bias
        arrays[tag + "_w1"] = w1.transpose(1, 0, 2).reshape(D, D)
        arrays[tag + "_b1"] = b1.reshape(KT, 128).T
        arrays[tag + "_w2"], arrays[tag + "_b2"] = w2.reshape(D, D), b2
    arrays = {k: np.ascontiguousarray(x) for k, x in arrays.items()}
    nc = bacc.Bacc("TRN2", target_bir_lowering=False, num_devices=1)
    a = {k: nc.dram_tensor("in_" + k, x.shape, mybir.dt.from_np(x.dtype), kind="ExternalInput").ap()
         for k, x in arrays.items()}
    a["out"] = nc.dram_tensor("out", (N, D), F32, kind="ExternalOutput").ap()
    program(nc, a)
    r = run(nc, [{"in_" + k: x for k, x in arrays.items()}], core_ids=[0])
    return r.results[0]["out"]
```

```python
import concourse.bass as bass
from concourse import mybir
from contextlib import ExitStack
import math

F32 = mybir.dt.float32
I32 = mybir.dt.int32
ACT = mybir.ActivationFunctionType
ALU = mybir.AluOpType
X = mybir.AxisListType.X

N, D, E = 625, 512, 20000
P, J = 125, 5
TILES = E // P
U = 4
TURNS = TILES // U
KT = D // 128
R = 8
NE = 8
HALVES = ((0, 313), (313, 312))
EPS = 1e-5
BIG = 3.0e38
SILU_2MOM = 1.679177


class Chain:

    def __init__(self, eng, sem, start=0):
        self.eng, self.sem, self.n = eng, sem, start

    def __call__(self, ins):
        self.n += 1
        ins.then_inc(self.sem, 1)
        self.eng.wait_ge(self.sem, self.n)


class Core:

    def __init__(self, nc, ctx, a):
        self.nc, self.ctx, self.a = nc, ctx, a
        sb = lambda name, shape, dt=F32: ctx.enter_context(nc.sbuf_tensor(name, shape, dt))
        self.x = sb("x", [P, J, D])
        self.ident = sb("ident", [128, 128])
        self.iota = sb("iota", [P, N])
        self.dst_f = sb("dst_f", [P, TILES])
        self.src_f = sb("src_f", [P, TILES])
        self.src_i = sb("src_i", [P, TILES], I32)
        self.dst_i = sb("dst_i", [P, TILES], I32)
        self.first_i = sb("first_i", [1, TILES], I32)
        self.narrow_i = sb("narrow_i", [1, 1], I32)
        self.dst_w = sb("dst_w", [P, TILES])
        self.ones = sb("ones", [1, 128])
        self.zeros = sb("zeros", [1, D])
        self.comb = sb("comb", [P, J, NE])
        self.half_pi = sb("half_pi", [P, 1])
        self.tail_row = sb("tail_row", [P, TILES], I32)
        self.head_row = sb("head_row", [P, TILES], I32)
        self.rel_table = nc.dram_tensor("rel_table", (2 * R * N, D), F32).ap()
        self.s0_table = nc.dram_tensor("s0_table", (N, 128), F32).ap()
        self.s1_table = nc.dram_tensor("s1_table", (N, 384), F32).ap()
        self.xs_table = nc.dram_tensor("xs_table", (N, D), F32).ap()
        self.xd_table = nc.dram_tensor("xd_table", (N, D), F32).ap()
        self.xnT_table = nc.dram_tensor("xnT_table", (128, KT * N), F32).ap()
        self.norm_uses = self.norm_rooms = 0
        self.gathered = [ctx.enter_context(nc.semaphore(f"gathered{b}")) for b in range(U)]
        self.gather_count = 0
        self.used = []
        self.nsem = {k: ctx.enter_context(nc.semaphore("norm_" + k)) for k in
                     ("stats", "var", "root", "rows_ready", "transposed", "evacuated")}

    def sem(self, name):
        self.used.append(self.nc.alloc_semaphore(name=name))
        return self.used[-1]

    def norm_room(self, ctx):
        v = self.norm_rooms = self.norm_rooms + 1
        self.xn = ctx.enter_context(self.nc.sbuf_tensor(f"xn{v}", [P, J, D], F32))
        self.xnT = ctx.enter_context(self.nc.sbuf_tensor(f"xnT{v}", [128, KT, N], F32))

    def gathers(self, n):
        before = self.gather_count
        self.gather_count += TURNS * n * 16
        return before

    def recycle(self):
        blk = self.nc.Block()
        with blk:
            @blk.gpsimd
            def _(pool):
                for s in self.used:
                    pool.sem_clear(s)
        for s in self.used:
            self.nc.release_semaphore(s)
        self.used = []


def col(j, w=P):
    return slice(j * w, (j + 1) * w)


def setup(c):
    nc, a = c.nc, c.a
    with ExitStack() as ctx:
        rel_i = ctx.enter_context(nc.sbuf_tensor("rel_i", [P, TILES], I32))
        rel_f = ctx.enter_context(nc.sbuf_tensor("rel_f", [P, TILES], F32))
        T2 = TILES // 2
        sb = lambda n, s, dt=F32: ctx.enter_context(nc.sbuf_tensor(n, s, dt))
        by_tile, by_tile_f = sb("by_tile", [T2, 2, P], I32), sb("by_tile_f", [T2, 2, P])
        span, tile_of = sb("span", [T2, 2, 2]), sb("tile_of", [T2, 2, 2])
        diag, ones80, widest = sb("diag", [T2, 2, T2, 2]), sb("ones80", [T2, P]), sb("widest", [1, 1])
        spread_out = ctx.enter_context(nc.psum_tensor("spread_out", [P, 2, TILES], F32))
        loaded, ready = c.sem("setup_loaded"), c.sem("setup_steps")
        spans_ready, spread = c.sem("spans_ready"), c.sem("spread")
        blk = ctx.enter_context(nc.Block())

        @blk.sync
        def _(sp):
            sp.dma_start(c.src_i[:], a["src"]).then_inc(loaded, 16)
            sp.dma_start(c.dst_i[:], a["dst"]).then_inc(loaded, 16)
            sp.dma_start(rel_i[:], a["rel"]).then_inc(loaded, 16)
            sp.dma_start(c.x[:], a["x"].rearrange("(j p) d -> p j d", p=P)).then_inc(loaded, 16)
            sp.dma_start(c.iota[:], a["iota"].partition_broadcast(P)).then_inc(loaded, 16)
            sp.dma_start(c.ident[:], a["ident"]).then_inc(loaded, 16)
            sp.dma_start(by_tile[:], a["dst_by_tile"]).then_inc(loaded, 16)

        @blk.tensor
        def _(pe):
            pe.wait_ge(spans_ready, 1)
            pe.matmul(spread_out[:, 0, :], ones80[:], diag[:, 0].rearrange("t i h -> t (i h)"), start=True, stop=True)
            pe.matmul(spread_out[:, 1, :], ones80[:], diag[:, 1].rearrange("t i h -> t (i h)"), start=True,
                      stop=True).then_inc(spread, 1)

        @blk.vector
        def _(dve):
            step = Chain(dve, ready)
            step(dve.memset(ones80[:], 1.0))
            step(dve.memset(c.ones[:], 1.0))
            step(dve.memset(c.zeros[:], 0.0))
            step(dve.memset(c.half_pi[:], math.pi / 2))
            dve.wait_ge(loaded, 7 * 16)
            step(dve.tensor_copy(by_tile_f[:], by_tile[:]))
            step(dve.tensor_reduce(span[:, 0, :], by_tile_f[:], X, ALU.min))
            step(dve.tensor_reduce(span[:, 1, :], by_tile_f[:], X, ALU.max))
            step(dve.tensor_scalar(tile_of[:], span[:], float(P), None, ALU.is_ge))
            for k in range(2, J):
                step(dve.scalar_tensor_tensor(tile_of[:], span[:], float(k * P), tile_of[:], ALU.is_ge, ALU.add))
            step(dve.tensor_scalar(tile_of[:, 0, :], tile_of[:, 0, :], float(J - 2), None, ALU.min))
            step(dve.tensor_tensor(tile_of[:, 1, :], tile_of[:, 1, :], tile_of[:, 0, :], ALU.subtract))
            for r in range(2):
                step(dve.tensor_tensor(diag[:, r], c.ident[0:T2, 0:T2].unsqueeze(2).broadcast_to([T2, T2, 2]),
                                       tile_of[:, r, :].unsqueeze(1).broadcast_to([T2, T2, 2]), ALU.mult))
            dve.sem_inc(spans_ready, 1)
            dve.wait_ge(spread, 1)
            step(dve.tensor_copy(c.first_i[:], spread_out[0:1, 0, :]))
            step(dve.tensor_reduce(widest[:], spread_out[0:1, 1, :], X, ALU.max))
            step(dve.tensor_scalar(widest[:], widest[:], 1.0, None, ALU.is_le))
            step(dve.tensor_copy(c.narrow_i[:], widest[:]))
            step(dve.tensor_copy(c.src_f[:], c.src_i[:]))
            step(dve.tensor_copy(c.dst_f[:], c.dst_i[:]))
            step(dve.scalar_tensor_tensor(c.dst_w[:], spread_out[:, 0, :], -float(P), c.dst_f[:], ALU.mult, ALU.add))
            step(dve.tensor_copy(rel_f[:], rel_i[:]))
            step(dve.scalar_tensor_tensor(c.tail_row[:], rel_f[:], float(N), c.dst_f[:], ALU.mult, ALU.add))
            step(dve.scalar_tensor_tensor(rel_f[:], rel_f[:], float(N), c.src_f[:], ALU.mult, ALU.add))
            step(dve.tensor_scalar(c.head_row[:], rel_f[:], float(R * N), None, ALU.add))


def norm(c):
    nc, s = c.nc, c.nsem
    v = c.norm_uses
    c.norm_uses += 1
    with ExitStack() as ctx:
        st = ctx.enter_context(nc.sbuf_tensor(f"bn_st{v}", [P, J, 6], F32))
        mv = ctx.enter_context(nc.sbuf_tensor(f"bn_mv{v}", [P, J, 2], F32))
        tp = ctx.enter_context(nc.psum_tensor(f"norm_tp{v}", [128, J, 512], F32))
        blk = ctx.enter_context(nc.Block())

        @blk.vector
        def _(dve):
            for j in range(J):
                dve.bn_stats(st[:, j, :], c.x[:, j, :]).then_inc(s["stats"], 1)
            for j in range(J):
                dve.wait_ge(s["stats"], (v * J + j + 1))
                dve.bn_aggr(mv[:, j, :], st[:, j, :]).then_inc(s["var"], 1)
            dve.wait_ge(s["var"], v * 7 + 5)
            dve.tensor_scalar(mv[:, :, 1], mv[:, :, 1], EPS, None, ALU.add).then_inc(s["var"], 1)
            dve.wait_ge(s["root"], v + 1)
            dve.reciprocal(mv[:, :, 1], mv[:, :, 1]).then_inc(s["var"], 1)
            dve.wait_ge(s["var"], v * 7 + 7)
            for j in range(J):
                dve.tensor_scalar(c.xn[:, j, :], c.x[:, j, :], mv[:, j, 0:1], mv[:, j, 1:2],
                                  ALU.subtract, ALU.mult).then_inc(s["rows_ready"], 1)

        @blk.scalar
        def _(act):
            act.wait_ge(s["var"], v * 7 + 6)
            act.activation(mv[:, :, 1], mv[:, :, 1], ACT.Sqrt).then_inc(s["root"], 1)
            for j in range(J):
                act.wait_ge(s["transposed"], v * J + j + 1)
                act.activation(c.xnT[:, :, col(j)], tp[:, j, 0:KT * P].rearrange("q (k p) -> q k p", k=KT),
                               ACT.Copy).then_inc(s["evacuated"], 1)

        @blk.tensor
        def _(pe):
            for j in range(J):
                pe.wait_ge(s["rows_ready"], v * J + j + 1)
                for k in range(KT):
                    ins = pe.transpose(tp[:, j, col(k)], c.xn[:, j, col(k, 128)], c.ident[0:P, 0:P])
                ins.then_inc(s["transposed"], 1)


def open_accumulators(pe, c, acc):
    for j in range(J):
        pe.matmul(acc[:, j, :], c.zeros[:, 0:P], c.zeros[:], start=True, stop=False)


def target_hot(dve, c, out, t, narrow):
    if narrow:
        return dve.tensor_scalar(out[:, 0:2 * P], c.iota[:, 0:2 * P], c.dst_w[:, at(t)], None, ALU.is_equal)
    return dve.tensor_scalar(out, c.iota[:], c.dst_f[:, at(t)], None, ALU.is_equal)


def add_targets(pe, c, acc, hot, parts, t, narrow):
    if narrow:
        first = pe.value_load(c.first_i[0:1, at(t)], min_val=0, max_val=J - 2)
        for n in range(2):
            for part in parts:
                ins = pe.matmul(acc[:, bass.ds(first + n, 1), :].rearrange("p a f -> p (a f)"), hot[:, col(n)], part,
                                start=False, stop=False)
        return ins
    for n in range(J):
        for part in parts:
            ins = pe.matmul(acc[:, n, :], hot[:, col(n)], part, start=False, stop=False)
    return ins


def for_width(eng, c, body):
    narrow = eng.value_load(c.narrow_i[0:1, 0:1], min_val=0, max_val=1)
    with eng.If(narrow == 1):
        body(True)
    with eng.Else():
        body(False)


def close_accumulators(pe, c, acc):
    for j in range(J):
        ins = pe.matmul(acc[:, j, :], c.zeros[:, 0:P], c.zeros[:], start=False, stop=True)
    return ins


def rel_tables(c, h_self):
    nc, a = c.nc, c.a
    G = 2 * R // 2
    FR = mybir.dt.float32r
    with ExitStack() as ctx:
        sb = lambda n, s, dt=F32: ctx.enter_context(nc.sbuf_tensor(f"rel_{n}", s, dt))
        w = sb("w", [128, 2, KT, D]); w_high = sb("w_high", [128, 2, KT, D], FR); w_low = sb("w_low", [128, 2, KT, D], FR)
        x_high = sb("x_high", [128, KT, N], FR); x_low = sb("x_low", [128, KT, N], FR)
        bias = sb("bias", [P, 2, D]); stage = sb("stage", [P, 2, J, D])
        ps = ctx.enter_context(nc.psum_tensor("rel_ps", [P, J, 512], F32))
        w_loaded = [c.sem(f"rel_w_loaded{i}") for i in range(2)]
        bias_loaded = [c.sem(f"rel_bias_loaded{i}") for i in range(2)]
        stored = [c.sem(f"rel_stored{i}") for i in range(2)]
        x_high_ready, x_low_ready, high_ready, low_ready, product, evacuated = (c.sem(f"rel_{n}") for n in (
            "x_high_ready", "x_low_ready", "high_ready", "low_ready", "product", "evacuated"))
        blk = ctx.enter_context(nc.Block())
        wv = a["W_rel"].rearrange("(r k q) o -> r q k o", k=KT, q=128)
        table = c.rel_table.rearrange("(g t j p) o -> g t p j o", t=2, j=J, p=P)

        @blk.sync
        def _(sp):
            def load(r, g, i):
                sp.wait_ge(low_ready, r + 1)
                sp.dma_start(w[:, i], wv[r]).then_inc(w_loaded[i], 16)
                sp.wait_ge(evacuated, r * J + J)
                sp.dma_start(bias[:, i], a["b_rel"][r].partition_broadcast(P)).then_inc(bias_loaded[i], 16)

            sp.sem_inc(low_ready, 2)
            sp.sem_inc(evacuated, 2 * J)
            with sp.Fori(0, G) as g:
                for i in range(2):
                    load(g * 2 + i, g, i)
            load(2 * G, G, 0)

        @blk.scalar
        def _(act):
            def split_high(r, g, i):
                act.wait_ge(w_loaded[i], g * 16 + 16)
                act.wait_ge(product, r * J + J)
                act.activation(w_high[:, i], w[:, i], ACT.Copy).then_inc(high_ready, 1)

            act.sem_inc(product, 2 * J)
            act.activation(x_high[:], c.xnT[:], ACT.Copy).then_inc(x_high_ready, 1)
            split_high(0, 0, 0)
            with act.Fori(0, G) as g:
                for i in range(2):
                    split_high(g * 2 + i + 1, g + i, 1 - i)
                    act.wait_ge(evacuated, g * (2 * J) + (i + 3) * J)
                    act.dma_start(table[g, i], stage[:, i]).then_inc(stored[i], 16)
            for i in range(2):
                act.wait_ge(stored[i], 16 * (G + 1))

        @blk.vector
        def _(dve):
            def split_low(r, i):
                dve.wait_ge(high_ready, r + 1)
                dve.wait_ge(product, r * J + J)
                dve.tensor_tensor(w_low[:, i], w[:, i], w_high[:, i].bitcast(F32), ALU.subtract).then_inc(low_ready, 1)

            def evacuate(r, g, i, out):
                dve.wait_ge(bias_loaded[i], g * 16 + 16)
                for j in range(J):
                    dve.wait_ge(product, r * J + (2 * J + j + 1))
                    dve.tensor_tensor(out[:, j, :], ps[:, j, :], bias[:, i, :], ALU.add).then_inc(evacuated, 1)

            for i in range(2):
                dve.sem_inc(stored[i], 16)
            dve.wait_ge(x_high_ready, 1)
            dve.tensor_tensor(x_low[:], c.xnT[:], x_high[:].bitcast(F32), ALU.subtract).then_inc(x_low_ready, 1)
            split_low(0, 0)
            with dve.Fori(0, G) as g:
                for i in range(2):
                    split_low(g * 2 + i + 1, 1 - i)
                    dve.wait_ge(stored[i], g * 16 + 16)
                    evacuate(g * 2 + i, g, i, stage[:, i])
            evacuate(2 * G, G, 0, h_self)

        @blk.tensor
        def _(pe):
            def products(r, i):
                pe.wait_ge(low_ready, r + 3)
                terms = [(x, y, k) for k in range(KT) for x, y in
                         ((x_high, w_high), (x_low, w_high), (x_high, w_low))]
                for j in range(J):
                    pe.wait_ge(evacuated, r * J + (J + j + 1))
                    for n, (x, y, k) in enumerate(terms):
                        ins = pe.matmul(ps[:, j, :], x[:, k, col(j)], y[:, i, k, :], start=(n == 0),
                                        stop=(n == len(terms) - 1))
                    ins.then_inc(product, 1)

            pe.wait_ge(x_low_ready, 1)
            with pe.Fori(0, G) as g:
                for i in range(2):
                    products(g * 2 + i, i)
            products(2 * G, 0)


def rel_edges(c, h_self):
    nc = c.nc
    FR = mybir.dt.float32r
    with ExitStack() as ctx:
        sb = lambda n, s, dt=F32: ctx.enter_context(nc.sbuf_tensor(f"re_{n}", s, dt))
        ix = sb("ix", [P, U, 2], I32); rows = sb("rows", [P, U, 2, D])
        high = sb("high", [P, 2, 2, D], FR); low = sb("low", [P, 2, 2, D], FR)
        src_hot = sb("src_hot", [P, 2, N], FR); dst_hot = sb("dst_hot", [P, 2, N], FR)
        acc = ctx.enter_context(nc.psum_tensor("re_acc", [P, J, 512], F32))
        indexed, go = c.sem("re_indexed"), c.sem("re_go")
        gathered, before = c.gathered, c.gathers(2)
        hot_ready, high_ready, low_ready, scattered, steps = (c.sem(f"re_{n}") for n in (
            "hot_ready", "high_ready", "low_ready", "scattered", "steps"))
        blk = ctx.enter_context(nc.Block())

        @blk.gpsimd
        def _(pool):
            pool.sem_inc(low_ready, U)

            def fetch(t, b):
                pool.wait_ge(low_ready, t + 1)
                pool.tensor_copy(ix[:, b, 0:1], c.tail_row[:, at(t)]).then_inc(indexed, 1)
                pool.tensor_copy(ix[:, b, 1:2], c.head_row[:, at(t)]).then_inc(indexed, 1)
                pool.wait_ge(indexed, t * 2 + 2)
                pool.sem_inc(go, 1)
                for h in range(2):
                    pool.indirect_dma_start(rows[:, b, h, :], None, c.rel_table, bass.IndirectOffsetOnAxis(
                        ap=ix[:, b, h:h + 1], axis=0)).then_inc(gathered[b], 16)
            rounds(pool, [(fetch, 0)])

        @blk.scalar
        def _(act):
            def split_high(t, b):
                act.wait_ge(gathered[b], filled(t, b, 2) + before)
                act.wait_ge(scattered, t + 1)
                act.activation(high[:, b % 2], rows[:, b], ACT.Copy).then_inc(high_ready, 1)
            rounds(act, [(split_high, 0)])

        @blk.vector
        def _(dve):
            def hots(narrow):
                def stage(t, b):
                    dve.wait_ge(scattered, t + 1)
                    dve.tensor_scalar(src_hot[:, b % 2, :], c.iota[:], c.src_f[:, at(t)], None,
                                      ALU.is_equal).then_inc(hot_ready, 1)
                    target_hot(dve, c, dst_hot[:, b % 2, :], t, narrow).then_inc(hot_ready, 1)
                return stage

            def split_low(t, b):
                dve.wait_ge(high_ready, t + 1)
                dve.tensor_tensor(low[:, b % 2], rows[:, b], high[:, b % 2].bitcast(F32), ALU.subtract).then_inc(low_ready, 1)

            for_width(dve, c, lambda narrow: rounds(dve, [(hots(narrow), 0), (split_low, 0)]))
            dve.wait_ge(scattered, TILES + 2 + 1)
            step = Chain(dve, steps)
            for j in range(J):
                step(dve.tensor_tensor(h_self[:, j, :], h_self[:, j, :], acc[:, j, :], ALU.add))
                dve.scalar_tensor_tensor(c.x[:, j, :], h_self[:, j, :], 0.0, c.x[:, j, :], ALU.max, ALU.add)

        @blk.tensor
        def _(pe):
            def scatter(narrow):
                def stage(t, b):
                    p = b % 2
                    pe.wait_ge(hot_ready, t * 2 + 2)
                    pe.wait_ge(high_ready, t + 1)
                    pe.wait_ge(low_ready, t + U + 1)
                    for j in range(J):
                        for part in (high, low):
                            pe.matmul(acc[:, j, :], src_hot[:, p, col(j)], part[:, p, 0, :], start=False, stop=False)
                    add_targets(pe, c, acc, dst_hot[:, p, :], [high[:, p, 1, :], low[:, p, 1, :]], t,
                                narrow).then_inc(scattered, 1)
                return stage

            pe.sem_inc(scattered, 2)
            open_accumulators(pe, c, acc)
            for_width(pe, c, lambda narrow: rounds(pe, [(scatter(narrow), 0)]))
            close_accumulators(pe, c, acc).then_inc(scattered, 1)


class Router:

    def __init__(self, c, ctx, tag):
        sb = lambda n, shape: ctx.enter_context(c.nc.sbuf_tensor(f"{tag}_{n}", shape, F32))
        self.c = c
        self.s = sb("s", [P, J, NE])
        self.e = sb("e", [P, J, NE])
        self.t = sb("t", [P, J, NE])
        self.mk = sb("mk", [P, J, NE])
        self.kp = sb("kp", [P, J, NE])
        self.oh1 = sb("oh1", [P, J, NE])
        self.oh2 = sb("oh2", [P, J, NE])
        self.m1, self.m2 = sb("m1", [P, J]), sb("m2", [P, J])
        self.r = sb("r", [P, J])
        self.ids = c.iota[:, 0:NE].unsqueeze(1).broadcast_to([P, J, NE])
        self.steps = c.sem(f"{tag}_steps")
        self.exps = c.sem(f"{tag}_exps")

    def wide(self, m):
        return m[:].unsqueeze(2).broadcast_to([P, J, NE])

    def first_max(self, dve, step, s, m, oh):
        t = self.t
        step(dve.tensor_reduce(m[:], s[:], X, ALU.max))
        step(dve.tensor_tensor(t[:], s[:], self.wide(m), ALU.is_equal))
        step(dve.scalar_tensor_tensor(t[:], t[:], -float(NE), self.ids, ALU.mult, ALU.add))
        step(dve.tensor_reduce(self.r[:], t[:], X, ALU.min))
        step(dve.tensor_tensor(oh[:], t[:], self.wide(self.r), ALU.is_equal))

    def exp_of(self, dve, step, s, m, n):
        step(dve.tensor_tensor(self.e[:], s[:], self.wide(m), ALU.subtract))
        dve.wait_ge(self.exps, n)

    def normalise(self, dve, step, out):
        step(dve.tensor_reduce(self.r[:], self.e[:], X, ALU.add))
        step(dve.reciprocal(self.r[:], self.r[:]))
        step(dve.tensor_tensor(out[:], self.e[:], self.wide(self.r), ALU.mult))


def route(c, dve, q, kind, logits, lg_ready, marks, capacity=None):
    step = Chain(dve, q.steps)
    dve.wait_ge(lg_ready, 1)
    step(dve.tensor_copy(q.s[:], logits))
    n_exp = [0]

    def exponential(s, m):
        step(dve.tensor_tensor(q.e[:], s[:], q.wide(m), ALU.subtract))
        marks.append(step.n)
        n_exp[0] += 1
        dve.wait_ge(q.exps, n_exp[0])

    def softmax():
        step(dve.tensor_reduce(q.m1[:], q.s[:], X, ALU.max))
        exponential(q.s, q.m1)
        q.normalise(dve, step, q.s)

    def second_max():
        step(dve.scalar_tensor_tensor(q.mk[:], q.oh1[:], -BIG, q.s[:], ALU.mult, ALU.add))
        q.first_max(dve, step, q.mk, q.m2, q.oh2)

    def keep_near(m):
        step(dve.tensor_tensor(q.t[:], q.s[:], q.wide(m), ALU.max))
        step(dve.reciprocal(q.t[:], q.t[:]))
        step(dve.tensor_tensor(q.kp[:], q.wide(m), q.s[:], ALU.subtract))
        step(dve.tensor_tensor(q.kp[:], q.kp[:], q.t[:], ALU.mult))
        step(dve.tensor_scalar(q.kp[:], q.kp[:], 0.02, None, ALU.is_le))

    def masked_share(oh, m):
        exponential(q.s, m)
        step(dve.tensor_tensor(q.e[:], q.e[:], q.kp[:], ALU.mult))
        step(dve.tensor_reduce(q.r[:], q.e[:], X, ALU.add))
        step(dve.reciprocal(q.r[:], q.r[:]))
        step(dve.tensor_tensor(q.e[:], q.e[:], oh[:], ALU.mult))
        step(dve.tensor_tensor(q.e[:], q.e[:], q.wide(q.r), ALU.mult))

    if kind == "sparsemixer":
        softmax()
        q.first_max(dve, step, q.s, q.m1, q.oh1)
        keep_near(q.m1)
        masked_share(q.oh1, q.m1)
        step(dve.tensor_copy(c.comb[:], q.e[:]))
        second_max()
        keep_near(q.m2)
        step(dve.scalar_tensor_tensor(q.t[:], q.oh1[:], 0.0, q.kp[:], ALU.is_equal, ALU.mult))
        step(dve.tensor_copy(q.kp[:], q.t[:]))
        masked_share(q.oh2, q.m2)
        step(dve.tensor_tensor(c.comb[:], c.comb[:], q.e[:], ALU.add))
    elif kind == "switch":
        softmax()
        q.first_max(dve, step, q.s, q.m1, q.oh1)
        step(dve.tensor_tensor(c.comb[:], q.s[:], q.oh1[:], ALU.mult))
    elif kind == "top2_scores":
        softmax()
        q.first_max(dve, step, q.s, q.m1, q.oh1)
        second_max()
        step(dve.tensor_tensor(q.t[:], q.oh1[:], q.oh2[:], ALU.add))
        step(dve.tensor_tensor(q.e[:], q.s[:], q.t[:], ALU.mult))
        q.normalise(dve, step, c.comb)
    elif kind == "top2_capacity":
        q.first_max(dve, step, q.s, q.m1, q.oh1)
        second_max()
        step(dve.tensor_tensor(q.mk[:], q.oh1[:], q.oh2[:], ALU.add))
        q.mask_step = step.n
        exponential(q.s, q.m1)
        step(dve.tensor_tensor(q.e[:], q.e[:], q.mk[:], ALU.mult))
        q.normalise(dve, step, c.comb)
        ranks, rank_ready, cap = capacity
        dve.wait_ge(rank_ready, 1)
        step(dve.scalar_tensor_tensor(c.comb[:], ranks, float(cap), c.comb[:], ALU.is_lt, ALU.mult))
    return step


class Weights:

    def __init__(self, c, ctx, tag, tiles):
        self.tiles, self.sources, self.loaded = {}, [], c.sem(f"{tag}_loaded")
        for name, shape, source in tiles:
            tile = ctx.enter_context(c.nc.sbuf_tensor(f"{tag}_{name}", shape, F32))
            self.tiles[name] = tile
            self.sources.append((tile, source))

    def __getitem__(self, name):
        return self.tiles[name]

    def load(self, queue):
        for tile, source in self.sources:
            queue.dma_start(tile[:], source).then_inc(self.loaded, 16)
        queue.wait_ge(self.loaded, 16 * len(self.sources))


def chunks(w):
    return w.rearrange("(k q) f -> q k f", q=128)


def small_weights(c, ctx, tag):
    a = c.a
    return Weights(c, ctx, tag, [
        ("wg", [128, KT, NE], chunks(a[f"{tag}_wg"])), ("bg", [1, NE], a[f"{tag}_bg"]),
        ("w1", [128, KT, D], chunks(a[f"{tag}_w1"])), ("b1", [128, KT], a[f"{tag}_b1"]),
        ("w2", [128, KT, D], chunks(a[f"{tag}_w2"])), ("b2", [NE, D], a[f"{tag}_b2"]),
        ("spread", [NE, D], a["spread"]), ("earlier", [P, P], a["earlier"])])


def ffn_small(c, tag, kind, gelu, wts):
    nc = c.nc
    norm(c)
    with ExitStack() as ctx:
        sb = lambda n, s, dt=F32: ctx.enter_context(nc.sbuf_tensor(f"{tag}_{n}", s, dt))
        pb = lambda n, s: ctx.enter_context(nc.psum_tensor(f"{tag}_{n}", s, F32))
        q = Router(c, ctx, tag)
        wg, bg, w1, b1, w2, b2, spread, earlier = (wts[n] for n in ("wg", "bg", "w1", "b1", "w2", "b2", "spread", "earlier"))
        every = sb("every", [P, P])
        hT = sb("hT", [128, KT, N]); combT = sb("combT", [NE, N])
        small = pb("small", [128, 512])
        lg = small[0:P, 0:J * NE].rearrange("p (j e) -> p j e", e=NE)
        ranks = small[0:P, 64:64 + J * NE].rearrange("p (j e) -> p j e", e=NE)
        big = pb("big", [128, 4, 512])
        ctp = pb("ctp", [NE, 2, 512])
        lg_ready, rank_ready = c.sem(f"{tag}_lg_ready"), c.sem(f"{tag}_rank_ready")
        consts, up_ready, gelu_done = c.sem(f"{tag}_consts"), c.sem(f"{tag}_up_ready"), c.sem(f"{tag}_gelu_done")
        ct_ready, ct_copied = c.sem(f"{tag}_ct_ready"), c.sem(f"{tag}_ct_copied")
        spread_ready, scaled = c.sem(f"{tag}_spread_ready"), c.sem(f"{tag}_scaled")
        down_ready, added = c.sem(f"{tag}_down_ready"), c.sem(f"{tag}_added")
        blk = ctx.enter_context(nc.Block())
        marks = []

        @blk.vector
        def _(dve):
            dve.memset(every[:], 1.0).then_inc(consts, 1)
            step = route(c, dve, q, kind, lg, lg_ready, marks, (ranks, rank_ready, CAPACITY))
            q.comb_step = step.n
            for n in range(2 * KT):
                k, (h0, hn) = n // 2, HALVES[n % 2]
                dve.wait_ge(gelu_done, n + 1)
                dve.wait_ge(spread_ready, n + 1)
                dve.tensor_tensor(hT[:, k, h0:h0 + hn], hT[:, k, h0:h0 + hn], big[:, n % 4, 0:hn],
                                  ALU.mult).then_inc(scaled, 1)
            for j in range(J):
                dve.wait_ge(down_ready, j + 1)
                dve.tensor_tensor(c.x[:, j, :], c.x[:, j, :], big[0:P, j % 4, :], ALU.add).then_inc(added, 1)

        @blk.scalar
        def _(act):
            for i, m in enumerate(marks[:]):
                act.wait_ge(q.steps, m)
                act.activation(q.e[:], q.e[:], ACT.Exp).then_inc(q.exps, 1)
            for n in range(2 * KT):
                k, (h0, hn) = n // 2, HALVES[n % 2]
                act.wait_ge(up_ready, n + 1)
                act.activation(hT[:, k, h0:h0 + hn], big[:, n % 4, 0:hn], gelu, bias=b1[:, k:k + 1]).then_inc(gelu_done, 1)
            for i, (first, n) in enumerate(((0, 4), (4, 1))):
                act.wait_ge(ct_ready, i + 1)
                act.activation(combT[:, first * P:(first + n) * P], ctp[:, i, 0:n * P], ACT.Copy).then_inc(ct_copied, 1)

        @blk.tensor
        def _(pe):
            for j in range(J):
                for k in range(KT):
                    pe.matmul(lg[:, j, :], c.xnT[:, k, col(j)], wg[:, k, :], start=(k == 0), stop=False)
                ins = pe.matmul(lg[:, j, :], c.ones[:, 0:P], bg[:], start=False, stop=True)
            ins.then_inc(lg_ready, 1)
            for n in range(2 * KT):
                m, (h0, hn) = n // 2, HALVES[n % 2]
                if n >= 4:
                    pe.wait_ge(gelu_done, n - 3)
                for k in range(KT):
                    ins = pe.matmul(big[:, n % 4, 0:hn], w1[:, k, col(m, 128)], c.xnT[:, k, h0:h0 + hn],
                                    start=(k == 0), stop=(k == KT - 1))
                ins.then_inc(up_ready, 1)
            if kind == "top2_capacity":
                pe.wait_ge(q.steps, q.mask_step)
                pe.wait_ge(consts, 1)
                for j in range(J):
                    for i in range(j):
                        pe.matmul(ranks[:, j, :], every[:], q.mk[:, i, :], start=(i == 0), stop=False)
                    ins = pe.matmul(ranks[:, j, :], earlier[:], q.mk[:, j, :], start=(j == 0), stop=True)
                ins.then_inc(rank_ready, 1)
            pe.wait_ge(q.steps, q.comb_step)
            for j in range(J):
                ins = pe.transpose(ctp[:, j // 4, col(j % 4)], c.comb[:, j, :], c.ident[0:P, 0:P])
                if j >= 3:
                    ins.then_inc(ct_ready, 1)
            pe.wait_ge(ct_copied, 2)
            for n in range(2 * KT):
                k, (h0, hn) = n // 2, HALVES[n % 2]
                if n < 4:
                    pe.wait_ge(gelu_done, n + 5)
                else:
                    pe.wait_ge(scaled, n - 3)
                pe.matmul(big[:, n % 4, 0:hn], spread[:, col(k, 128)], combT[:, h0:h0 + hn],
                          start=True, stop=True).then_inc(spread_ready, 1)
            pe.wait_ge(scaled, 2 * KT)
            for j in range(J):
                if j >= 4:
                    pe.wait_ge(added, j - 3)
                for k in range(KT):
                    pe.matmul(big[0:P, j % 4, :], hT[:, k, col(j)], w2[:, k, :], start=(k == 0), stop=False)
                pe.matmul(big[0:P, j % 4, :], combT[:, col(j)], b2[:], start=False, stop=True).then_inc(down_ready, 1)


CAPACITY = min(128 * math.ceil(math.ceil(0.3125 * N) / 128), N)


def ffn_large(c):
    FR = mybir.dt.float32r
    with ExitStack() as ctx:
        sb = lambda n, s, dt=F32: ctx.enter_context(c.nc.sbuf_tensor(f"fl_{n}", s, dt))
        slot, fits = sb("slot", [P, J, NE]), sb("fits", [1, 1], I32)
        with ExitStack() as parts:
            x_high = parts.enter_context(c.nc.sbuf_tensor("fl_x_high", [P, J, D], FR))
            x_low = parts.enter_context(c.nc.sbuf_tensor("fl_x_low", [P, J, D], FR))
            with ExitStack() as room:
                c.norm_room(room)
                norm(c)
                route_large(c, slot, fits, x_high, x_low)
            experts_sparse(c, slot, fits, x_high, x_low)
        c.norm_room(ctx)
        experts_dense(c, fits)


SLOTS = 2 * P
RING = 4


def route_large(c, slot, fits, x_high, x_low):
    nc, a = c.nc, c.a
    with ExitStack() as ctx:
        sb = lambda n, s, dt=F32: ctx.enter_context(nc.sbuf_tensor(f"fr_{n}", s, dt))
        q = Router(c, ctx, "fr")
        wg = sb("wg", [128, KT, NE]); bg = sb("bg", [1, NE])
        earlier = sb("earlier", [P, P]); every = sb("every", [P, P]); most = sb("most", [1, 1])
        small = ctx.enter_context(nc.psum_tensor("fr_small", [P, 512], F32))
        lg = small[:, 0:J * NE].rearrange("p (j e) -> p j e", e=NE)
        ranks = small[:, 64:64 + J * NE].rearrange("p (j e) -> p j e", e=NE)
        totals = small[:, 128:128 + NE]
        loaded, saved, consts, lg_ready, masked, ranked, split = (c.sem(f"fr_{n}") for n in (
            "loaded", "saved", "consts", "lg_ready", "masked", "ranked", "split"))
        blk = ctx.enter_context(nc.Block())
        marks = []

        @blk.sync
        def _(sp):
            sp.dma_start(wg[:], a["fl_wg"].rearrange("(k q) e -> q k e", q=128)).then_inc(loaded, 16)
            sp.dma_start(bg[:], a["fl_bg"]).then_inc(loaded, 16)
            sp.dma_start(earlier[:], a["earlier"]).then_inc(loaded, 16)
            sp.dma_start(c.xnT_table, c.xnT[:].rearrange("q k n -> q (k n)")).then_inc(saved, 16)
            sp.wait_ge(saved, 16)

        @blk.vector
        def _(dve):
            dve.memset(every[:], 1.0).then_inc(consts, 1)
            dve.wait_ge(split, 1)
            dve.tensor_tensor(x_low[:], c.xn[:], x_high[:].bitcast(F32), ALU.subtract).then_inc(split, 1)
            step = route(c, dve, q, "sparsemixer", lg, lg_ready, marks)
            step(dve.tensor_tensor(q.mk[:], q.oh1[:], q.oh2[:], ALU.add))
            dve.sem_inc(masked, 1)
            dve.wait_ge(ranked, 1)
            step(dve.scalar_tensor_tensor(slot[:], ranks, 1.0, q.mk[:], ALU.add, ALU.mult))
            step(dve.tensor_scalar(slot[:], slot[:], -1.0, None, ALU.add))
            step(dve.tensor_reduce(most[:], totals[0:1, :], X, ALU.max))
            step(dve.tensor_scalar(most[:], most[:], float(SLOTS), None, ALU.is_le))
            step(dve.tensor_copy(fits[:], most[:]))

        @blk.scalar
        def _(act):
            act.activation(x_high[:], c.xn[:], ACT.Copy).then_inc(split, 1)
            for m in marks:
                act.wait_ge(q.steps, m)
                act.activation(q.e[:], q.e[:], ACT.Exp).then_inc(q.exps, 1)

        @blk.tensor
        def _(pe):
            pe.wait_ge(loaded, 48)
            for j in range(J):
                for k in range(KT):
                    pe.matmul(lg[:, j, :], c.xnT[:, k, col(j)], wg[:, k, :], start=(k == 0), stop=False)
                ins = pe.matmul(lg[:, j, :], c.ones[:, 0:P], bg[:], start=False, stop=True)
            ins.then_inc(lg_ready, 1)
            pe.wait_ge(consts, 1)
            pe.wait_ge(masked, 1)
            for j in range(J):
                for i in range(j):
                    pe.matmul(ranks[:, j, :], every[:], q.mk[:, i, :], start=(i == 0), stop=False)
                pe.matmul(ranks[:, j, :], earlier[:], q.mk[:, j, :], start=(j == 0), stop=True)
            for i in range(J):
                ins = pe.matmul(totals, every[:], q.mk[:, i, :], start=(i == 0), stop=(i == J - 1))
            ins.then_inc(ranked, 1)


def experts_sparse(c, slot, fits, x_high, x_low):
    nc, a = c.nc, c.a
    FR = mybir.dt.float32r
    FM = 8
    with ExitStack() as ctx:
        sb = lambda n, s, dt=F32: ctx.enter_context(nc.sbuf_tensor(f"fs_{n}", s, dt))
        pb = lambda n, s: ctx.enter_context(nc.psum_tensor(f"fs_{n}", s, F32))
        raw = sb("raw", [128, RING, 2, 512])
        up_low = sb("up_low", [128, 2, 2, KT, 512], FR); up_high = sb("up_high", [128, 2, 2, KT, 512], FR)
        down_low = sb("down_low", [128, FM, D], FR); down_high = sb("down_high", [128, FM, D], FR)
        sel = sb("sel", [P, J, SLOTS], FR); back = sb("back", [P, 2, N], FR)
        number = sb("number", [P, J, 2]); number_r = sb("number_r", [P, J, 2], FR); token = sb("token", [P, 2])
        t_high = sb("t_high", [128, KT, SLOTS], FR); t_low = sb("t_low", [128, KT, SLOTS], FR)
        g = sb("g", [128, 2, SLOTS]); h = sb("h", [128, 2, SLOTS])
        h_high = sb("h_high", [128, FM, SLOTS], FR); h_low = sb("h_low", [128, FM, SLOTS], FR)
        y_high = sb("y_high", [P, 2, D], FR); y_low = sb("y_low", [P, 2, D], FR)
        wide = pb("wide", [128, 2, 512])
        up = pb("up", [128, 2, 2, 512])
        out = pb("out", [P, 2, 512])
        raw_loaded = [c.sem(f"fs_raw_loaded{i}") for i in range(RING)]
        number_loaded, high_ready, low_ready = (c.sem(f"fs_{n}") for n in ("number_loaded", "high_ready", "low_ready"))
        number_ready, sel_ready, gathered, t_high_ready, t_low_ready, token_ready, back_ready = (
            c.sem(f"fs_{n}") for n in ("number_ready", "sel_ready", "gathered", "t_high_ready",
                                       "t_low_ready", "token_ready", "back_ready"))
        up_done, gelu_done, h_ready, h_high_ready, h_low_ready, down_done, y_high_ready, y_low_ready = (
            c.sem(f"fs_{n}") for n in ("up_done", "gelu_done", "h_ready", "h_high_ready", "h_low_ready", "down_done",
                                       "y_high_ready", "y_low_ready"))
        scattered, added = c.sem("fs_scattered"), c.sem("fs_added")
        blk = ctx.enter_context(nc.Block())
        numbers = wide[0:P, 1, 500:504]

        def place(up, down, n):
            if n < 8:
                return up[:, n // 4, n % 4 // 2, n % 2 * 2:n % 2 * 2 + 2, :]
            return down[:, 2 * (n - 8):2 * (n - 8) + 2, :]

        def when_fits(eng):
            return eng.If(eng.value_load(fits[0:1, 0:1], min_val=0, max_val=1) == 1)

        @blk.sync
        def _(sp):
            up_views = [a[n].rearrange("e (k q) (h f) -> e h q k f", q=128, h=2) for n in ("fl_w1", "fl_w3")]
            down_view = a["fl_w2"].rearrange("e (k q) f -> e q k f", q=128)
            with when_fits(sp):
                sp.dma_start(number[:], a["number"]).then_inc(number_loaded, 16)
                sp.sem_inc(low_ready, RING)
                with sp.Fori(0, NE) as e:
                    for n in range(12):
                        if n < 8:
                            piece = up_views[n % 4 // 2][e, n // 4][:, n % 2 * 2:n % 2 * 2 + 2, :]
                        else:
                            piece = down_view[e][:, 2 * (n - 8):2 * (n - 8) + 2, :]
                        sp.wait_ge(low_ready, e * 12 + (n + 1))
                        sp.dma_start(raw[:, n % RING], piece).then_inc(raw_loaded[n % RING], 16)

        @blk.scalar
        def _(act):
            def high(e, n):
                act.wait_ge(raw_loaded[n % RING], e * (12 // RING * 16) + (n // RING + 1) * 16)
                act.activation(place(up_high, down_high, n), raw[:, n % RING], ACT.Copy).then_inc(high_ready, 1)

            def first_half(e):
                for n in range(4):
                    high(e, n)

            def tokens(e):
                act.wait_ge(gathered, e + 1)
                act.activation(t_high[:].rearrange("q (b k) s -> q b (k s)", b=2), wide[:, :, 0:2 * SLOTS],
                               ACT.Copy).then_inc(t_high_ready, 1)

            def expert(e, last):
                for m in range(FM + 1):
                    if m < FM:
                        act.wait_ge(up_done, e * FM + m + 1)
                        act.wait_ge(h_ready, e * FM + (m + 1))
                        act.activation(g[:, m % 2, :], up[:, 0, m % 2, 0:SLOTS], ACT.Gelu).then_inc(gelu_done, 1)
                    if m == 1:
                        act.wait_ge(down_done, e * 2 + 2)
                    if m:
                        act.wait_ge(h_ready, e * FM + (m + 2))
                        act.activation(h_high[:, m - 1, :], h[:, (m - 1) % 2, :], ACT.Copy).then_inc(h_high_ready, 1)
                    if m < FM:
                        high(e, 4 + m)
                if not last:
                    tokens(e + 1)
                    first_half(e + 1)
                for s in range(2):
                    act.wait_ge(down_done, e * 2 + (s + 3))
                    act.activation(y_high[:, s, :], out[:, s, :], ACT.Copy).then_inc(y_high_ready, 1)

            with when_fits(act):
                act.wait_ge(number_loaded, 16)
                act.activation(number_r[:], number[:], ACT.Copy).then_inc(number_ready, 1)
                tokens(0)
                first_half(0)
                with act.Fori(0, NE - 1) as e:
                    expert(e, False)
                expert(NE - 1, True)

        @blk.vector
        def _(dve):
            def low(e, n):
                dve.wait_ge(high_ready, e * 12 + (n + 1))
                dve.tensor_tensor(place(up_low, down_low, n), raw[:, n % RING], place(up_high, down_high, n).bitcast(F32),
                                  ALU.subtract).then_inc(low_ready, 1)

            def first_half(e):
                for n in range(4):
                    low(e, n)

            def select(e):
                for j in range(J):
                    ins = dve.tensor_scalar(sel[:, j, :], c.iota[:, 0:SLOTS], slot[:, j, bass.ds(e + 0, 1)], None, ALU.is_equal)
                ins.then_inc(sel_ready, 1)

            def tokens(e):
                dve.wait_ge(t_high_ready, e + 1)
                dve.tensor_tensor(t_low[:].rearrange("q (b k) s -> q b (k s)", b=2), wide[:, :, 0:2 * SLOTS],
                                  t_high[:].bitcast(F32).rearrange("q (b k) s -> q b (k s)", b=2),
                                  ALU.subtract).then_inc(t_low_ready, 1)
                dve.tensor_scalar(token[:], numbers.rearrange("p (s i) -> p s i", i=2)[:, :, 0], -1.0, None,
                                  ALU.add).then_inc(token_ready, 1)

            def expert(e, last):
                dve.wait_ge(token_ready, e + 1)
                for s in range(2):
                    ins = dve.tensor_scalar(back[:, s, :], c.iota[:], token[:, s:s + 1], None, ALU.is_equal)
                ins.then_inc(back_ready, 1)
                for m in range(FM + 1):
                    if m < FM:
                        dve.wait_ge(gelu_done, e * FM + m + 1)
                        dve.wait_ge(h_low_ready, e * FM + (m + 1))
                        dve.tensor_tensor(h[:, m % 2, :], g[:, m % 2, :], up[:, 1, m % 2, 0:SLOTS], ALU.mult).then_inc(h_ready, 1)
                    if m:
                        dve.wait_ge(h_high_ready, e * FM + m)
                        dve.tensor_tensor(h_low[:, m - 1, :], h[:, (m - 1) % 2, :], h_high[:, m - 1, :].bitcast(F32),
                                          ALU.subtract).then_inc(h_low_ready, 1)
                    if m < FM:
                        low(e, 4 + m)
                    if m == 5 and not last:
                        dve.wait_ge(gathered, e + 1)
                        select(e + 1)
                if not last:
                    dve.wait_ge(back_ready, e + 1)
                    tokens(e + 1)
                    first_half(e + 1)
                for s in range(2):
                    dve.wait_ge(y_high_ready, e * 2 + s + 1)
                    dve.tensor_tensor(y_low[:, s, :], out[:, s, :], y_high[:, s, :].bitcast(F32),
                                      ALU.subtract).then_inc(y_low_ready, 1)
                for j in range(J):
                    dve.wait_ge(scattered, e * J + j + 1)
                    dve.scalar_tensor_tensor(c.x[:, j, :], wide[0:P, j % 2, :], c.comb[:, j, bass.ds(e + 0, 1)], c.x[:, j, :],
                                             ALU.mult, ALU.add).then_inc(added, 1)

            with when_fits(dve):
                select(0)
                tokens(0)
                first_half(0)
                with dve.Fori(0, NE - 1) as e:
                    expert(e, False)
                expert(NE - 1, True)

        @blk.tensor
        def _(pe):
            def summed(place, terms, lhs, rhs):
                for n, term in enumerate(terms):
                    ins = pe.matmul(place, lhs(*term), rhs(*term), start=(n == 0), stop=(n == len(terms) - 1))
                return ins

            def gather(e):
                pe.wait_ge(sel_ready, e + 1)
                for k in range(KT):
                    summed(wide[:, k // 2, k % 2 * SLOTS:(k % 2 + 1) * SLOTS],
                           [(j, x) for j in range(J) for x in (x_high, x_low)],
                           lambda j, x: x[:, j, col(k, 128)], lambda j, x: sel[:, j, :])
                for s in range(2):
                    ins = summed(numbers[:, 2 * s:2 * s + 2], [(j,) for j in range(J)],
                                 lambda j: sel[:, j, col(s)], lambda j: number_r[:, j, :])
                ins.then_inc(gathered, 1)

            def expert(e, last):
                products = [(0, 0), (1, 0), (0, 1)]
                pe.wait_ge(t_low_ready, e + 1)
                for m in range(FM):
                    if m % 4 == 0:
                        pe.wait_ge(low_ready, e * 12 + (RING + 4 + m))
                    pe.wait_ge(h_ready, e * FM + (m + 1))
                    for i in range(2):
                        ins = summed(up[:, i, m % 2, 0:SLOTS], [(k, *p) for k in range(KT) for p in products],
                                     lambda k, wl, tl: (up_high, up_low)[wl][:, m // 4, i, k, col(m % 4, 128)],
                                     lambda k, wl, tl: (t_high, t_low)[tl][:, k, :])
                    ins.then_inc(up_done, 1)
                if not last:
                    pe.wait_ge(added, e * J + 1)
                    gather(e + 1)
                pe.wait_ge(low_ready, e * 12 + (RING + 12))
                pe.wait_ge(h_low_ready, e * FM + (FM + 2))
                for s in range(2):
                    summed(out[:, s, :], [(m, *p) for m in range(FM) for p in products],
                           lambda m, wl, tl: (h_high, h_low)[tl][:, m, col(s)],
                           lambda m, wl, tl: (down_high, down_low)[wl][:, m, :]).then_inc(down_done, 1)
                pe.wait_ge(back_ready, e + 1)
                pe.wait_ge(y_low_ready, e * 2 + 2)
                if last:
                    pe.wait_ge(added, e * J + 1)
                else:
                    pe.wait_ge(token_ready, e + 2)
                for j in range(J):
                    if j >= 2:
                        pe.wait_ge(added, e * J + j)
                    summed(wide[0:P, j % 2, :], [(s, y) for s in range(2) for y in (y_high, y_low)],
                           lambda s, y: back[:, s, col(j)], lambda s, y: y[:, s, :]).then_inc(scattered, 1)

            with when_fits(pe):
                for freed, n in ((h_ready, 2), (h_low_ready, 2), (down_done, 2), (added, 1)):
                    pe.sem_inc(freed, n)
                pe.wait_ge(number_ready, 1)
                gather(0)
                with pe.Fori(0, NE - 1) as e:
                    expert(e, False)
                expert(NE - 1, True)


def experts_dense(c, fits):
    nc, a = c.nc, c.a
    FM = 8
    with ExitStack() as ctx:
        sb = lambda n, s, dt=F32: ctx.enter_context(nc.sbuf_tensor(f"fl_{n}", s, dt))
        pb = lambda n, s: ctx.enter_context(nc.psum_tensor(f"fl_{n}", s, F32))
        w1 = sb("w1", [128, KT, 1024]); w3 = sb("w3", [128, KT, 1024])
        w2 = sb("w2", [128, FM, D])
        g = sb("g", [128, 2, 313]); hT = sb("hT", [128, FM, N])
        up = pb("up", [128, 2, 2, 512])
        down = pb("down", [P, 2, 512])
        x_loaded, up_loaded, down_loaded = c.sem("fl_x_loaded"), c.sem("fl_up_loaded"), c.sem("fl_down_loaded")
        up_ready, gelu_done = c.sem("fl_up_ready"), c.sem("fl_gelu_done")
        h_ready, down_ready, added = c.sem("fl_h_ready"), c.sem("fl_down_ready"), c.sem("fl_added")
        blk = ctx.enter_context(nc.Block())
        NH = 2 * FM

        @blk.sync
        def _(sp):
            with sp.If(sp.value_load(fits[0:1, 0:1], min_val=0, max_val=1) == 0):
                sp.dma_start(c.xnT[:].rearrange("q k n -> q (k n)"), c.xnT_table).then_inc(x_loaded, 16)
                sp.sem_inc(h_ready, NH)
                sp.sem_inc(down_ready, J)
                w1v = a["fl_w1"].rearrange("e (k q) f -> e q k f", q=128)
                w3v = a["fl_w3"].rearrange("e (k q) f -> e q k f", q=128)
                w2v = a["fl_w2"].rearrange("e (k q) f -> e q k f", q=128)
                with sp.Fori(0, NE) as e:
                    sp.wait_ge(h_ready, e * NH + NH)
                    sp.dma_start(w1[:], w1v[e]).then_inc(up_loaded, 16)
                    sp.dma_start(w3[:], w3v[e]).then_inc(up_loaded, 16)
                    sp.wait_ge(down_ready, e * J + J)
                    sp.dma_start(w2[:], w2v[e]).then_inc(down_loaded, 16)

        @blk.vector
        def _(dve):
            with dve.If(dve.value_load(fits[0:1, 0:1], min_val=0, max_val=1) == 0):
                with dve.Fori(0, NE) as e:
                    for n in range(NH):
                        m, (h0, hn) = n // 2, HALVES[n % 2]
                        if n == 0:
                            dve.wait_ge(down_ready, e * J + J)
                        dve.wait_ge(gelu_done, e * NH + n + 1)
                        dve.tensor_tensor(hT[:, m, h0:h0 + hn], g[:, n % 2, 0:hn], up[:, 1, n % 2, 0:hn],
                                          ALU.mult).then_inc(h_ready, 1)
                    for j in range(J):
                        dve.wait_ge(down_ready, e * J + J + j + 1)
                        dve.scalar_tensor_tensor(c.x[:, j, :], down[:, j % 2, :], c.comb[:, j, bass.ds(e, 1)],
                                                 c.x[:, j, :], ALU.mult, ALU.add).then_inc(added, 1)

        @blk.scalar
        def _(act):
            with act.If(act.value_load(fits[0:1, 0:1], min_val=0, max_val=1) == 0):
                with act.Fori(0, NE) as e:
                    for n in range(NH):
                        m, (h0, hn) = n // 2, HALVES[n % 2]
                        act.wait_ge(up_ready, e * NH + n + 1)
                        act.wait_ge(h_ready, e * NH + NH + n - 1)
                        act.activation(g[:, n % 2, 0:hn], up[:, 0, n % 2, 0:hn], ACT.Gelu).then_inc(gelu_done, 1)

        @blk.tensor
        def _(pe):
            with pe.If(pe.value_load(fits[0:1, 0:1], min_val=0, max_val=1) == 0):
                pe.wait_ge(x_loaded, 16)
                pe.sem_inc(added, 2)
                with pe.Fori(0, NE) as e:
                    pe.wait_ge(up_loaded, e * 32 + 32)
                    for n in range(NH):
                        m, (h0, hn) = n // 2, HALVES[n % 2]
                        pe.wait_ge(h_ready, e * NH + NH + n - 1)
                        for s, w in enumerate((w1, w3)):
                            for k in range(KT):
                                ins = pe.matmul(up[:, s, n % 2, 0:hn], w[:, k, col(m, 128)], c.xnT[:, k, h0:h0 + hn],
                                                start=(k == 0), stop=(k == KT - 1))
                        ins.then_inc(up_ready, 1)
                    pe.wait_ge(down_loaded, e * 16 + 16)
                    pe.wait_ge(h_ready, e * NH + 2 * NH)
                    for j in range(J):
                        pe.wait_ge(added, e * J + j + 1)
                        for m in range(FM):
                            ins = pe.matmul(down[:, j % 2, :], hT[:, m, col(j)], w2[:, m, :], start=(m == 0), stop=(m == FM - 1))
                        ins.then_inc(down_ready, 1)


class Tile:

    def __init__(self, u, off, width):
        self.u, self.off, self.width = u, off, width

    def __add__(self, n):
        return self.u * self.width + (self.off + n)

    def __mul__(self, n):
        return Scaled(self.u * (self.width * n), self.off * n)

    def __floordiv__(self, n):
        return self.u * (self.width // n) + self.off // n


class Scaled:
    def __init__(self, v, off):
        self.v, self.off = v, off

    def __add__(self, n):
        return self.v + (self.off + n)


def rounds(eng, stages, last=4, width=U, tiles=TILES):
    for r in range(last):
        for stage, lag in stages:
            if r >= lag:
                stage(r - lag, (r - lag) % width)
    with eng.Fori(0, (tiles - last) // width) as u:
        for b in range(width):
            for stage, lag in stages:
                stage(Tile(u, last + b - lag, width), (last + b - lag) % width)
    for r in range(last + (tiles - last) // width * width, tiles + last):
        for stage, lag in stages:
            if 0 <= r - lag < tiles:
                stage(r - lag, (r - lag) % width)


def filled(t, b, n=1):
    if isinstance(t, int):
        return (t // U + 1) * 16 * n
    return t.u * (t.width // U * 16 * n) + (t.off // U + 1) * 16 * n


def half(b):
    return slice(64 * (b % 2), 64 * (b % 2) + 64)


def at(t):
    return bass.ds(t + 0, 1)


def mace_nodes(c):
    nc, a = c.nc, c.a
    norm(c)
    with ExitStack() as ctx:
        sb = lambda n, s: ctx.enter_context(nc.sbuf_tensor(f"mn_{n}", s, F32))
        w = sb("w", [128, 2, 128]); vT = sb("vT", [128, 3, N]); stage = sb("stage", [P, J, D])
        tp = ctx.enter_context(nc.psum_tensor("mn_tp", [128, 2, 512], F32))
        ps = ctx.enter_context(nc.psum_tensor("mn_ps", [P, 2, 512], F32))
        loaded, turned, copied = c.sem("mn_loaded"), c.sem("mn_turned"), c.sem("mn_copied")
        product, staged, stored = c.sem("mn_product"), c.sem("mn_staged"), c.sem("mn_stored")
        blk = ctx.enter_context(nc.Block())

        @blk.sync
        def _(sp):
            sp.dma_start(w[:, 0], a["W_up0"]).then_inc(loaded, 16)
            sp.dma_start(w[:, 1], a["W_up1"]).then_inc(loaded, 16)
            sp.wait_ge(staged, J)
            sp.dma_start(c.s0_table.rearrange("(j p) f -> p j f", p=P), stage[:, :, 0:128]).then_inc(stored, 16)
            sp.dma_start(c.s1_table.rearrange("(j p) f -> p j f", p=P), stage[:, :, 128:512]).then_inc(stored, 16)
            sp.wait_ge(stored, 32)

        @blk.tensor
        def _(pe):
            for j in range(J):
                if j >= 2:
                    pe.wait_ge(copied, j - 1)
                v = c.xn[:, j, 128:512].rearrange("p (u m) -> p m u", m=3)
                for m in range(3):
                    ins = pe.transpose(tp[:, j % 2, col(m)], v[:, m, :], c.ident[0:P, 0:P])
                ins.then_inc(turned, 1)
            pe.wait_ge(loaded, 32)
            for j in range(J):
                pe.wait_ge(copied, j + 1)
                if j >= 2:
                    pe.wait_ge(staged, j - 1)
                pe.matmul(ps[:, j % 2, 0:128], c.xnT[:, 0, col(j)], w[:, 0], start=True, stop=True)
                for m in range(3):
                    ins = pe.matmul(ps[:, j % 2, col(m + 1, 128)], vT[:, m, col(j)], w[:, 1], start=True, stop=True)
                ins.then_inc(product, 1)

        @blk.scalar
        def _(act):
            for j in range(J):
                act.wait_ge(turned, j + 1)
                act.activation(vT[:, :, col(j)], tp[:, j % 2, 0:3 * P].rearrange("q (m p) -> q m p", m=3),
                               ACT.Copy).then_inc(copied, 1)

        @blk.vector
        def _(dve):
            for j in range(J):
                dve.wait_ge(product, j + 1)
                dve.tensor_scalar(stage[:, j, :], ps[:, j % 2, :], 128.0 ** -0.5, None, ALU.mult).then_inc(staged, 1)


def mace_mlp(c, h3T):
    nc, a = c.nc, c.a
    CH = U * P
    G = E // 2 // CH // 2
    with ExitStack() as ctx:
        sb = lambda n, s: ctx.enter_context(nc.sbuf_tensor(f"mm_{n}", s, F32))
        f = sb("f", [16, 2, CH]); w1 = sb("w1", [16, 128]); w2 = sb("w2", [128, 128]); w3 = sb("w3", [128, 128])
        h = sb("h", [128, 2, 2, CH])
        ps = ctx.enter_context(nc.psum_tensor("mm_ps", [128, 2, 3, 512], F32))
        cleared, w_loaded, f_loaded = c.sem("mm_cleared"), c.sem("mm_w_loaded"), [c.sem(f"mm_f_loaded{i}") for i in range(2)]
        product, active = [[c.sem(f"mm_{n}{i}") for i in range(2)] for n in ("product", "active")]
        blk = ctx.enter_context(nc.Block())

        @blk.vector
        def _(dve):
            for t in (w1, w2, w3):
                dve.memset(t[:], 0.0).then_inc(cleared, 1)

        @blk.sync
        def _(sp):
            sp.wait_ge(cleared, 3)
            for t, n, k in ((w1, "W_mlp1", 8), (w2, "W_mlp2", 64), (w3, "W_mlp3", 64)):
                for i in range(2):
                    sp.dma_start(t[i * k:(i + 1) * k, col(i, 64)], a[n]).then_inc(w_loaded, 16)
            for i in range(2):
                sp.sem_inc(product[i], 3)
            with sp.Fori(0, G) as g:
                for i in range(2):
                    sp.wait_ge(product[i], g * 3 + 1)
                    sp.dma_start(f[:, i, :], a["ea8T"][:, bass.ds(g * (2 * CH) + i * CH, CH)]).then_inc(f_loaded[i], 16)

        @blk.tensor
        def _(pe):
            pe.wait_ge(w_loaded, 96)
            for i in range(2):
                pe.sem_inc(active[i], 3)
            with pe.Fori(0, G) as g:
                for n, w in enumerate((w1, w2, w3)):
                    for i in range(2):
                        if n == 0:
                            pe.wait_ge(f_loaded[i], g * 16 + 16)
                        pe.wait_ge(active[i], g * 3 + 3 + n)
                        rhs = f[:, i, :] if n == 0 else h[:, i, n - 1, :]
                        pe.matmul(ps[:, i, n, 0:CH], w[:], rhs, start=True, stop=True).then_inc(product[i], 1)

        @blk.scalar
        def _(act):
            with act.Fori(0, G) as g:
                for n in range(3):
                    for i in range(2):
                        act.wait_ge(product[i], g * 3 + 4 + n)
                        out = h[:, i, n, :] if n < 2 else h3T[:, bass.ds(g * (2 * CH) + i * CH, CH)]
                        scale = 8.0 ** -0.5 if n == 0 else SILU_2MOM / 8.0
                        act.activation(out, ps[:, i, n, 0:CH], ACT.Silu, scale=scale).then_inc(active[i], 1)


def mace_edges(c, h3T, vector, agg, ahead=None):
    nc, a = c.nc, c.a
    FR = mybir.dt.float32r
    tag = "mv" if vector else "ms"
    W = 384 if vector else 128
    table = c.s1_table if vector else c.s0_table
    K = SILU_2MOM / 8.0
    with ExitStack() as ctx:
        sb = lambda n, s, dt=F32: ctx.enter_context(nc.sbuf_tensor(f"{tag}_{n}", s, dt))
        ix = sb("ix", [P, U], I32); rows = sb("rows", [P, U, W]); hs = sb("hs", [128, U, P])
        w4 = sb("w4", [128, 256]); ea = sb("ea", [P, TILES, 4])
        hot = sb("hot", [P, U, N], FR); part = sb("part", [P, U, 256])
        msg = sb("msg", [P, U, D]); high = sb("high", [P, U, D], FR); low = sb("low", [P, U, D], FR)
        acc = ctx.enter_context(nc.psum_tensor(f"{tag}_acc", [P, J, 512], F32))
        tpw = ctx.enter_context(nc.psum_tensor(f"{tag}_tpw", [P, 2, 512], F32))
        loaded, indexed, go, h_staged = (c.sem(f"{tag}_{n}") for n in ("loaded", "indexed", "go", "h_staged"))
        gathered, before = c.gathered, c.gathers(1)
        w_ready, hot_ready, msg_ready, high_ready, low_ready, scattered, inner, copied = (
            c.sem(f"{tag}_{n}") for n in ("w_ready", "hot_ready", "msg_ready", "high_ready", "low_ready",
                                          "scattered", "inner", "copied"))
        blk = ctx.enter_context(nc.Block())

        @blk.sync
        def _(sp):
            for i in range(2):
                sp.dma_start(w4[col(i, 64)], a["W_mlp4"][:, 256:512] if vector else a["W_mlp4"][:, 0:256]).then_inc(loaded, 16)
            sp.dma_start(ea[:], a["ea4"]).then_inc(loaded, 16)
            if ahead:
                ahead.load(sp)

        @blk.gpsimd
        def _(pool):
            pool.sem_inc(msg_ready, 2 * U)

            def fetch(t, b):
                pool.wait_ge(msg_ready, t * 2 + 2)
                pool.tensor_copy(ix[:, b:b + 1], c.src_i[:, at(t)]).then_inc(indexed, 1)
                pool.wait_ge(indexed, t + 1)
                pool.sem_inc(go, 1)
                pool.indirect_dma_start(rows[:, b, :], None, table, bass.IndirectOffsetOnAxis(
                    ap=ix[:, b:b + 1], axis=0)).then_inc(gathered[b], 16)
            rounds(pool, [(fetch, 0)])

        @blk.tensor
        def _(pe):
            def weights(t, b):
                pe.wait_ge(h_staged, t + 1)
                pe.wait_ge(msg_ready, t * 2 + (2 * U - 2))
                pe.matmul(tpw[:, b % 2, 0:256], hs[half(b), b, :], w4[half(b), :], start=True, stop=True).then_inc(w_ready, 1)

            def scatter(narrow):
                def stage(t, b):
                    pe.wait_ge(hot_ready, t + 1)
                    pe.wait_ge(high_ready, t + 1)
                    pe.wait_ge(low_ready, t + 1)
                    add_targets(pe, c, acc, hot[:, b, :], [high[:, b, :], low[:, b, :]], t, narrow).then_inc(scattered, 1)
                return stage

            pe.sem_inc(scattered, U)
            pe.sem_inc(w_ready, U)
            open_accumulators(pe, c, acc)
            pe.wait_ge(loaded, 48)
            for_width(pe, c, lambda narrow: rounds(pe, [(weights, 0), (scatter(narrow), 3)]))
            close_accumulators(pe, c, acc).then_inc(scattered, 1)

        @blk.vector
        def _(dve):
            def gathered_rows(t, b):
                dve.wait_ge(scattered, t + 1)
                dve.wait_ge(gathered[b], filled(t, b) + before)
                dve.wait_ge(w_ready, t + (1 + U))

            def scalar_messages(narrow):
                def stage(t, b):
                    gathered_rows(t, b)
                    v = part[:, b, :].rearrange("p (g f) -> p g f", g=2)
                    dve.scalar_tensor_tensor(v, tpw[:, b % 2, 0:256].rearrange("p (g f) -> p g f", g=2), K,
                                             rows[:, b, :].unsqueeze(1).broadcast_to([P, 2, 128]),
                                             ALU.mult, ALU.mult).then_inc(inner, 1)
                    target_hot(dve, c, hot[:, b, :], t, narrow).then_inc(hot_ready, 1)
                    dve.wait_ge(inner, t + 1)
                    dve.tensor_scalar(msg[:, b, 0:128], v[:, 0, :], ea[:, at(t), 0], None, ALU.mult).then_inc(msg_ready, 1)
                    dve.tensor_tensor(msg[:, b, 128:512].rearrange("p (m f) -> p m f", m=3),
                                      v[:, 1:2, :].broadcast_to([P, 3, 128]),
                                      ea[:, at(t), 1:4].rearrange("p a m -> p (a m)").unsqueeze(2).broadcast_to([P, 3, 128]),
                                      ALU.mult).then_inc(msg_ready, 1)
                return stage

            def vector_messages(narrow):
                def stage(t, b):
                    gathered_rows(t, b)
                    s1 = rows[:, b, :].rearrange("p (m f) -> p m f", m=3)
                    dot, w3y = part[:, b, 0:128], part[:, b, 128:256]
                    dve.tensor_scalar(dot, s1[:, 0, :], ea[:, at(t), 1], None, ALU.mult).then_inc(inner, 1)
                    dve.tensor_scalar(w3y, tpw[:, b % 2, 0:128], ea[:, at(t), 0], K, ALU.mult, ALU.mult).then_inc(inner, 1)
                    target_hot(dve, c, hot[:, b, :], t, narrow).then_inc(hot_ready, 1)
                    dve.wait_ge(inner, t * 4 + 1)
                    dve.scalar_tensor_tensor(dot, s1[:, 1, :], ea[:, at(t), 2], dot, ALU.mult, ALU.add).then_inc(inner, 1)
                    dve.wait_ge(inner, t * 4 + 2)
                    dve.tensor_tensor(msg[:, b, 128:512].rearrange("p (m f) -> p m f", m=3), s1,
                                      w3y.unsqueeze(1).broadcast_to([P, 3, 128]), ALU.mult).then_inc(msg_ready, 1)
                    dve.wait_ge(inner, t * 4 + 3)
                    dve.scalar_tensor_tensor(dot, s1[:, 2, :], ea[:, at(t), 3], dot, ALU.mult, ALU.add).then_inc(inner, 1)
                    dve.wait_ge(inner, t * 4 + 4)
                    dve.scalar_tensor_tensor(msg[:, b, 0:128], tpw[:, b % 2, 128:256], K * 3.0 ** -0.5, dot,
                                             ALU.mult, ALU.mult).then_inc(msg_ready, 1)
                return stage

            def split_low(t, b):
                dve.wait_ge(high_ready, t + 1)
                dve.tensor_tensor(low[:, b, :], msg[:, b, :], high[:, b, :].bitcast(F32), ALU.subtract).then_inc(low_ready, 1)

            dve.wait_ge(loaded, 48)
            messages = vector_messages if vector else scalar_messages
            for_width(dve, c, lambda narrow: rounds(dve, [(messages(narrow), 1), (split_low, 2)]))

        @blk.scalar
        def _(act):
            def stage_hidden(t, b):
                pair = t // 2
                act.wait_ge(w_ready, t + 1)
                act.activation(hs[half(b), b, :], h3T.rearrange("q (t p) -> q t p", p=P)[half(b), at(pair), :].rearrange(
                    "q a p -> q (a p)"), ACT.Copy).then_inc(h_staged, 1)

            def split_high(t, b):
                act.wait_ge(msg_ready, t * 2 + (2 + 2 * U))
                act.activation(high[:, b, :], msg[:, b, :], ACT.Copy).then_inc(high_ready, 1)
            rounds(act, [(stage_hidden, 0), (split_high, 2)])
            act.wait_ge(scattered, U + TILES + 1)
            for j in range(J):
                act.activation(agg[:, j, :], acc[:, j, :], ACT.Copy).then_inc(copied, 1)


def mace_out(c, agg_s, agg_v):
    nc, a = c.nc, c.a
    with ExitStack() as ctx:
        sb = lambda n, s: ctx.enter_context(nc.sbuf_tensor(f"mo_{n}", s, F32))
        w = sb("w", [128, 2, 2, 128])
        aT = sb("aT", [128, 2, 4, N])
        tp = ctx.enter_context(nc.psum_tensor("mo_tp", [128, 2, 512], F32))
        ps = ctx.enter_context(nc.psum_tensor("mo_ps", [P, 2, 512], F32))
        loaded, turned, copied, product, added = (c.sem(f"mo_{n}") for n in (
            "loaded", "turned", "copied", "product", "added"))
        blk = ctx.enter_context(nc.Block())

        @blk.sync
        def _(sp):
            for i in range(2):
                sp.dma_start(w[:, i], a[f"W_out{i}"].rearrange("(h q) f -> q h f", q=128)).then_inc(loaded, 16)

        @blk.tensor
        def _(pe):
            for n in range(2 * J):
                j, agg = n // 2, (agg_s, agg_v)[n % 2]
                if n >= 2:
                    pe.wait_ge(copied, n - 1)
                for g in range(4):
                    ins = pe.transpose(tp[:, n % 2, col(g)], agg[:, j, col(g, 128)], c.ident[0:P, 0:P])
                ins.then_inc(turned, 1)
            pe.wait_ge(loaded, 32)
            for j in range(J):
                pe.wait_ge(copied, 2 * j + 2)
                if j >= 2:
                    pe.wait_ge(added, 2 * (j - 1))
                for g in range(4):
                    for h in range(2):
                        ins = pe.matmul(ps[:, j % 2, col(g, 128)], aT[:, h, g, col(j)], w[:, min(g, 1), h],
                                        start=(h == 0), stop=(h == 1))
                ins.then_inc(product, 1)

        @blk.scalar
        def _(act):
            for n in range(2 * J):
                act.wait_ge(turned, n + 1)
                act.activation(aT[:, n % 2, :, col(n // 2)], tp[:, n % 2, 0:4 * P].rearrange("q (g p) -> q g p", g=4),
                               ACT.Copy).then_inc(copied, 1)

        @blk.vector
        def _(dve):
            for j in range(J):
                dve.wait_ge(product, j + 1)
                dve.scalar_tensor_tensor(c.x[:, j, 0:128], ps[:, j % 2, 0:128], 1 / 160, c.x[:, j, 0:128],
                                         ALU.mult, ALU.add).then_inc(added, 1)
                v = c.x[:, j, 128:512].rearrange("p (v m) -> p m v", m=3)
                dve.scalar_tensor_tensor(v, ps[:, j % 2, 128:512].rearrange("p (m v) -> p m v", m=3), 1 / 160, v,
                                         ALU.mult, ALU.add).then_inc(added, 1)


def adjacency(c, degree, ahead):
    nc = c.nc
    BF = mybir.dt.bfloat16
    with ExitStack() as ctx:
        sb = lambda n, s, dt=F32: ctx.enter_context(nc.sbuf_tensor(f"ad_{n}", s, dt))
        src_hot = sb("src_hot", [P, U, N], BF); dst_hot = sb("dst_hot", [P, U, N], BF); counts = sb("counts", [P, J, N])
        acc = ctx.enter_context(nc.psum_tensor("ad_acc", [P, 7 * 512], F32))
        hot_ready, counted, copied, turned, done = (c.sem(f"ad_{n}") for n in (
            "hot_ready", "counted", "copied", "turned", "done"))
        blk = ctx.enter_context(nc.Block())
        LAST = J * 512

        @blk.sync
        def _(sp):
            for weights in ahead:
                weights.load(sp)

        @blk.vector
        def _(dve):
            def hots(narrow):
                def stage(t, b):
                    dve.wait_ge(counted, t + 1)
                    dve.tensor_scalar(src_hot[:, b, :], c.iota[:], c.src_f[:, at(t)], None, ALU.is_equal)
                    target_hot(dve, c, dst_hot[:, b, :], t, narrow).then_inc(hot_ready, 1)
                return stage
            for_width(dve, c, lambda narrow: rounds(dve, [(hots(narrow), 0)]))
            dve.wait_ge(copied, J + 2)
            dve.tensor_reduce(degree[:], counts[:], X, ALU.add).then_inc(done, 1)
            dve.wait_ge(done, 1)
            dve.tensor_scalar(degree[:], degree[:], 1.0, None, ALU.max).then_inc(done, 1)
            dve.wait_ge(done, 2)
            dve.reciprocal(degree[:], degree[:]).then_inc(done, 1)

        @blk.tensor
        def _(pe):
            def count(narrow):
                def stage(t, b):
                    pe.wait_ge(hot_ready, t + 1)
                    if narrow:
                        first = pe.value_load(c.first_i[0:1, at(t)], min_val=0, max_val=J - 2)
                    for n in range(2 if narrow else J):
                        bank = first * 512 + n * 512 if narrow else n * 512
                        fifth = first * 128 + (LAST + n * 128) if narrow else LAST + n * 128
                        pe.matmul(acc[:, bass.ds(bank, 4 * P)], dst_hot[:, b, col(n)], src_hot[:, b, 0:4 * P],
                                  start=False, stop=False)
                        ins = pe.matmul(acc[:, bass.ds(fifth, P)], dst_hot[:, b, col(n)], src_hot[:, b, 4 * P:N],
                                        start=False, stop=False)
                    ins.then_inc(counted, 1)
                return stage

            pe.sem_inc(counted, U)
            for k in range(7):
                pe.matmul(acc[:, col(k, 512)], c.zeros[:, 0:P], c.zeros[:], start=True, stop=False)
            for_width(pe, c, lambda narrow: rounds(pe, [(count(narrow), 0)]))
            for k in range(7):
                ins = pe.matmul(acc[:, col(k, 512)], c.zeros[:, 0:P], c.zeros[:], start=False, stop=True)
            ins.then_inc(counted, 1)
            pe.wait_ge(copied, J + 2)
            for unit in range(J * J):
                i, n, place = unit // J, unit % J, unit // 4 * 512 + unit % 4 * P
                ins = pe.transpose(acc[:, place:place + P], counts[:, n, col(i)], c.ident[0:P, 0:P])
                if unit % 4 == 3 or unit == J * J - 1:
                    ins.then_inc(turned, 1)

        @blk.scalar
        def _(act):
            act.wait_ge(counted, U + TILES + 1)
            for n in range(J):
                act.activation(counts[:, n, 0:4 * P], acc[:, n * 512:n * 512 + 4 * P], ACT.Copy).then_inc(copied, 1)
            act.activation(counts[:, 0:4, 4 * P:N], acc[:, LAST:LAST + 512].rearrange("p (n f) -> p n f", f=128)[:, :, 0:P],
                           ACT.Copy).then_inc(copied, 1)
            act.activation(counts[:, 4, 4 * P:N], acc[:, LAST + 512:LAST + 512 + P], ACT.Copy).then_inc(copied, 1)
            flat = c.adjT[:].rearrange("p i n -> p (i n)")
            for k in range(7):
                width = min(4 * P, J * N - k * 4 * P)
                act.wait_ge(turned, k + 1)
                act.activation(flat[:, k * 4 * P:k * 4 * P + width], acc[:, k * 512:k * 512 + width], ACT.Copy)


def sage_weights(c, ctx, l):
    a = c.a
    wide = lambda n: a[n].partition_broadcast(P)
    return Weights(c, ctx, f"sw{l}", [
        ("wl", [128, KT, D], chunks(a[f"Wl{l}"])), ("wr", [128, KT, D], chunks(a[f"Wr{l}"])), ("bl", [P, D], wide(f"bl{l}")),
        ("gain", [P, D], wide(f"g{l}")), ("bias", [P, D], wide(f"b{l}")), ("slope", [P, 1], wide("a_prelu"))])


def sage_layer(c, l, h, degree, final, wts):
    nc = c.nc
    tag = f"sg{l}"
    with ExitStack() as ctx:
        sb = lambda n, s: ctx.enter_context(nc.sbuf_tensor(f"{tag}_{n}", s, F32))
        wl, wr, bl, gain, bias, slope = (wts[n] for n in ("wl", "wr", "bl", "gain", "bias", "slope"))
        agg = sb("agg", [P, J, D]); aggT = sb("aggT", [128, KT, N]); hT = sb("hT", [128, KT, N])
        y = sb("y", [P, J, D]); st = sb("st", [P, J, 6]); mv = sb("mv", [P, J, 2])
        acc = ctx.enter_context(nc.psum_tensor(f"{tag}_acc", [P, J, 512], F32))
        tp = ctx.enter_context(nc.psum_tensor(f"{tag}_tp", [128, 3, 512], F32))
        summed, averaged, turned, copied, product = (c.sem(f"{tag}_{n}") for n in (
            "summed", "averaged", "turned", "copied", "product"))
        steps, var_ready, rooted = c.sem(f"{tag}_steps"), c.sem(f"{tag}_var_ready"), c.sem(f"{tag}_rooted")
        blk = ctx.enter_context(nc.Block())

        @blk.tensor
        def _(pe):
            for j in range(J):
                for i in range(J):
                    ins = pe.matmul(acc[:, j, :], c.adjT[:, i, col(j)], h[:, i, :], start=(i == 0), stop=(i == J - 1))
                ins.then_inc(summed, 1)
            for n in range(2 * J):
                j, s = n % J, (h, agg)[n // J]
                if n >= 3:
                    pe.wait_ge(copied, n - 2)
                if n >= J:
                    pe.wait_ge(averaged, j + 1)
                for k in range(KT):
                    ins = pe.transpose(tp[:, n % 3, col(k)], s[:, j, col(k, 128)], c.ident[0:P, 0:P])
                ins.then_inc(turned, 1)
            for j in range(J):
                pe.wait_ge(averaged, j + 1)
                pe.wait_ge(copied, J + j + 1)
                for k in range(KT):
                    pe.matmul(acc[:, j, :], hT[:, k, col(j)], wr[:, k, :], start=(k == 0), stop=False)
                for k in range(KT):
                    ins = pe.matmul(acc[:, j, :], aggT[:, k, col(j)], wl[:, k, :], start=False, stop=(k == KT - 1))
                ins.then_inc(product, 1)

        @blk.scalar
        def _(act):
            for n in range(2 * J):
                act.wait_ge(turned, n + 1)
                act.activation((hT, aggT)[n // J][:, :, col(n % J)],
                               tp[:, n % 3, 0:KT * P].rearrange("q (k p) -> q k p", k=KT), ACT.Copy).then_inc(copied, 1)
            act.wait_ge(var_ready, 1)
            act.activation(mv[:, :, 1], mv[:, :, 1], ACT.Sqrt).then_inc(rooted, 1)

        @blk.vector
        def _(dve):
            step = Chain(dve, steps)
            for j in range(J):
                dve.wait_ge(summed, j + 1)
                dve.tensor_scalar(agg[:, j, :], acc[:, j, :], degree[:, j:j + 1], None, ALU.mult).then_inc(averaged, 1)
            for j in range(J):
                dve.wait_ge(product, j + 1)
                step(dve.tensor_tensor(y[:, j, :], acc[:, j, :], bl[:], ALU.add))
                if l > 0:
                    step(dve.tensor_tensor(y[:, j, :], y[:, j, :], h[:, j, :], ALU.add))
                step(dve.bn_stats(st[:, j, :], y[:, j, :]))
                step(dve.bn_aggr(mv[:, j, :], st[:, j, :]))
            dve.tensor_scalar(mv[:, :, 1], mv[:, :, 1], EPS, None, ALU.add).then_inc(var_ready, 1)
            dve.wait_ge(rooted, 1)
            step(dve.reciprocal(mv[:, :, 1], mv[:, :, 1]))
            for j in range(J):
                step(dve.tensor_scalar(y[:, j, :], y[:, j, :], mv[:, j, 0:1], mv[:, j, 1:2], ALU.subtract, ALU.mult))
                step(dve.tensor_tensor(y[:, j, :], y[:, j, :], gain[:], ALU.mult))
                step(dve.tensor_tensor(y[:, j, :], y[:, j, :], bias[:], ALU.add))
                step(dve.tensor_scalar(agg[:, j, :], y[:, j, :], 0.0, slope[:], ALU.min, ALU.mult))
                step(dve.scalar_tensor_tensor(h[:, j, :], y[:, j, :], 0.0, agg[:, j, :], ALU.max, ALU.add))
                if final:
                    step(dve.tensor_tensor(c.x[:, j, :], c.x[:, j, :], h[:, j, :], ALU.add))


def edge_node_weights(c, ctx):
    a = c.a
    return Weights(c, ctx, "enw", [("source", [128, KT, D], chunks(a["E_W1"][0:D])),
                                   ("target", [128, KT, D], chunks(a["E_W1"][D:2 * D])), ("b", [1, D], a["E_b1"])])


def edge_nodes(c, wts):
    nc = c.nc
    norm(c)
    with ExitStack() as ctx:
        sb = lambda n, s: ctx.enter_context(nc.sbuf_tensor(f"en_{n}", s, F32))
        w = (wts["source"], wts["target"]); b = wts["b"]; stage = sb("stage", [P, 2, J, D])
        ps = ctx.enter_context(nc.psum_tensor("en_ps", [P, 4, 512], F32))
        product, staged, stored = (c.sem(f"en_{n}") for n in ("product", "staged", "stored"))
        blk = ctx.enter_context(nc.Block())

        @blk.sync
        def _(sp):
            for s, table in enumerate((c.xs_table, c.xd_table)):
                sp.wait_ge(staged, (s + 1) * J)
                sp.dma_start(table.rearrange("(j p) f -> p j f", p=P), stage[:, s]).then_inc(stored, 16)
            sp.wait_ge(stored, 32)

        @blk.tensor
        def _(pe):
            for n in range(2 * J):
                s, j = n // J, n % J
                if n >= 4:
                    pe.wait_ge(staged, n - 3)
                for k in range(KT):
                    ins = pe.matmul(ps[:, n % 4, :], c.xnT[:, k, col(j)], w[s][:, k, :], start=(k == 0),
                                    stop=(k == KT - 1 and s == 0))
                if s == 1:
                    ins = pe.matmul(ps[:, n % 4, :], c.ones[:, 0:P], b[:], start=False, stop=True)
                ins.then_inc(product, 1)

        @blk.scalar
        def _(act):
            for n in range(2 * J):
                act.wait_ge(product, n + 1)
                act.activation(stage[:, n // J, n % J, :], ps[:, n % 4, :], ACT.Copy).then_inc(staged, 1)


def edge_messages(c, agg):
    nc, a = c.nc, c.a
    FR = mybir.dt.float32r
    W = 2 * U
    SECOND = 3
    with ExitStack() as ctx:
        sb = lambda n, s, dt=F32: ctx.enter_context(nc.sbuf_tensor(f"em_{n}", s, dt))
        ix = sb("ix", [P, U, 2], I32); rows = sb("rows", [P, U, 2, D])
        ea = sb("ea", [128, 2, U * P]); ea_high = sb("ea_high", [128, 2, U * P], FR); ea_both = sb("ea_both", [128, 2, U * P], FR)
        w1 = sb("w1", [128, D]); w1_high = sb("w1_high", [128, D], FR); w1_low = sb("w1_low", [64, D], FR)
        w2 = sb("w2", [128, KT, D]); w2_high = sb("w2_high", [128, KT, D], FR); w2_low = sb("w2_low", [128, KT, D], FR)
        b2 = sb("b2", [P, D])
        z1 = sb("z1", [P, W, D]); q1 = sb("q1", [P, W, D]); h = sb("h", [P, 2, D])
        hT_high = sb("hT_high", [128, 2, KT * P], FR); hT_low = sb("hT_low", [128, 2, KT * P], FR)
        z2 = sb("z2", [P, W, D]); q2 = sb("q2", [P, W, D]); msg = sb("msg", [P, 2, D]); hot = sb("hot", [P, 2, N])
        acc = ctx.enter_context(nc.psum_tensor("em_acc", [P, J, 512], F32))
        z1p = ctx.enter_context(nc.psum_tensor("em_z1p", [P, 512], F32))
        z2p = ctx.enter_context(nc.psum_tensor("em_z2p", [P, 512], F32))
        tp = ctx.enter_context(nc.psum_tensor("em_tp", [128, 512], F32))
        (w_loaded, w_high_ready, w_ready, ea_high_ready, ea_ready, indexed, go, edge_product, z1_partial, z1_ready,
         q1_ready, h_ready, turned, high_ready, hT_ready, product, z2_ready, q2_ready, msg_ready, hot_ready, scattered,
         copied, angles1, angles2) = (c.sem(f"em_{n}") for n in (
            "w_loaded", "w_high_ready", "w_ready", "ea_high_ready", "ea_ready", "indexed", "go", "edge_product",
            "z1_partial", "z1_ready", "q1_ready", "h_ready", "turned", "high_ready", "hT_ready", "product", "z2_ready",
            "q2_ready", "msg_ready", "hot_ready", "scattered", "copied", "angles1", "angles2"))
        gathered, before = c.gathered, c.gathers(2)
        ea_loaded = [c.sem(f"em_ea_loaded{b}") for b in range(2)]
        blk = ctx.enter_context(nc.Block())
        EDGE, FIRST, HIDDEN, TURN, COPY, PRODUCT, OUTPUT = 0, 1, W, W + 1, W + 2, W + 3, W + 4
        MESSAGE, SCATTER, ROUNDS = OUTPUT + W - 1, OUTPUT + W, 3 * W
        tile_rounds = lambda eng, stages: rounds(eng, stages, ROUNDS, W)

        @blk.sync
        def _(sp):
            for i in range(2):
                sp.dma_start(w1[col(i, 64)], a["E_W1"][2 * D:2 * D + 64]).then_inc(w_loaded, 16)
            sp.dma_start(w2[:], a["E_W2"].rearrange("(k q) f -> q k f", q=128)).then_inc(w_loaded, 16)
            sp.dma_start(b2[:], a["E_b2"].partition_broadcast(P)).then_inc(w_loaded, 16)
            sp.sem_inc(ea_ready, 2)
            with sp.Fori(0, TURNS // 2) as u:
                for i in range(2):
                    sp.wait_ge(ea_ready, u * 2 + i + 1)
                    for half_rows in range(2):
                        sp.dma_start(ea[col(half_rows, 64), i, :],
                                     a["ea64T"][:, bass.ds(u * (W * P) + i * (U * P), U * P)]).then_inc(ea_loaded[i], 16)

        @blk.gpsimd
        def _(pool):
            pool.sem_inc(z1_ready, U)

            def fetch(t, b):
                b = b % U
                pool.wait_ge(z1_ready, t + 1)
                pool.tensor_copy(ix[:, b, 0:1], c.src_i[:, at(t)]).then_inc(indexed, 1)
                pool.tensor_copy(ix[:, b, 1:2], c.dst_i[:, at(t)]).then_inc(indexed, 1)
                pool.wait_ge(indexed, t * 2 + 2)
                pool.sem_inc(go, 1)
                for n, table in enumerate((c.xs_table, c.xd_table)):
                    pool.indirect_dma_start(rows[:, b, n, :], None, table, bass.IndirectOffsetOnAxis(
                        ap=ix[:, b, n:n + 1], axis=0)).then_inc(gathered[b], 16)
            rounds(pool, [(fetch, 0)])

        @blk.tensor
        def _(pe):
            def edge_part(t, b):
                g = b // U % 2
                pe.wait_ge(ea_ready, t // U + 3)
                pe.wait_ge(z1_partial, t + 1)
                place = col(b % U)
                pe.matmul(z1p[0:P, :], ea_both[:, g, place], w1_high[:], start=True, stop=False)
                pe.matmul(z1p[0:P, :], ea_both[0:64, g, place], w1_low[:], start=False, stop=True).then_inc(edge_product, 1)

            def turn_h(t, b):
                pe.wait_ge(h_ready, t + (1 + W))
                pe.wait_ge(hT_ready, t + 1)
                for k in range(KT):
                    ins = pe.transpose(tp[:, col(k)], h[:, b % 2, col(k, 128)], c.ident[0:P, 0:P])
                ins.then_inc(turned, 1)

            def second(t, b):
                pe.wait_ge(hT_ready, t + 2)
                pe.wait_ge(z2_ready, t + 1)
                terms = [(x, y, k) for k in range(KT) for x, y in
                         ((hT_high, w2_high), (hT_low, w2_high), (hT_high, w2_low))]
                for n, (x, y, k) in enumerate(terms):
                    ins = pe.matmul(z2p[0:P, :], x[:, b % 2, col(k)], y[:, k, :], start=(n == 0), stop=(n == len(terms) - 1))
                ins.then_inc(product, 1)

            def scatter(narrow):
                def stage(t, b):
                    pe.wait_ge(msg_ready, t + (1 + W))
                    pe.wait_ge(hot_ready, t + 1)
                    add_targets(pe, c, acc, hot[:, b % 2, :], [msg[:, b % 2, :]], t, narrow).then_inc(scattered, 1)
                return stage

            pe.sem_inc(z1_partial, 1)
            pe.sem_inc(z2_ready, 1)
            pe.sem_inc(hT_ready, 1)
            for freed in (scattered, turned, product):
                pe.sem_inc(freed, 2)
            for freed in (h_ready, msg_ready, edge_product):
                pe.sem_inc(freed, W)
            open_accumulators(pe, c, acc)
            pe.wait_ge(w_ready, 2)
            for_width(pe, c, lambda narrow: tile_rounds(
                pe, [(scatter(narrow), SCATTER), (second, PRODUCT), (edge_part, EDGE), (turn_h, TURN)]))
            close_accumulators(pe, c, acc).then_inc(scattered, 1)

        @blk.vector
        def _(dve):
            def split_features(t, b):
                if b % U:
                    return
                g = b // U % 2
                dve.wait_ge(ea_high_ready, t // U + 1)
                dve.tensor_tensor(ea_both[64:128, g, :], ea[64:128, g, :], ea_high[64:128, g, :].bitcast(F32),
                                  ALU.subtract).then_inc(ea_ready, 1)

            def first(t, b):
                dve.wait_ge(edge_product, t + (1 + W))
                dve.wait_ge(gathered[b % U], filled(t, b, 2) + before)
                dve.wait_ge(h_ready, t + 1)
                dve.tensor_tensor(z1[:, b, :], z1p[0:P, :], rows[:, b % U, 0, :], ALU.add).then_inc(z1_partial, 1)
                dve.wait_ge(z1_partial, t + 2)
                dve.tensor_tensor(z1[:, b, :], z1[:, b, :], rows[:, b % U, 1, :], ALU.add).then_inc(z1_ready, 1)

            def hidden(t, b):
                dve.wait_ge(q1_ready, t // U + 1)
                dve.wait_ge(turned, t + 1)
                dve.tensor_tensor(h[:, b % 2, :], z1[:, b, :], q1[:, b, :], ALU.mult).then_inc(h_ready, 1)

            def copy_turned(t, b):
                dve.wait_ge(turned, t + 3)
                dve.wait_ge(product, t + 1)
                dve.tensor_copy(hT_high[:, b % 2, :], tp[:, 0:KT * P]).then_inc(high_ready, 1)
                dve.wait_ge(high_ready, t + 1)
                dve.tensor_tensor(hT_low[:, b % 2, :], tp[:, 0:KT * P], hT_high[:, b % 2, :].bitcast(F32),
                                  ALU.subtract).then_inc(hT_ready, 1)

            def output(t, b):
                dve.wait_ge(product, t + 3)
                dve.wait_ge(msg_ready, t + 1)
                dve.tensor_tensor(z2[:, b, :], z2p[0:P, :], b2[:], ALU.add).then_inc(z2_ready, 1)

            def message(narrow):
                def stage(t, b):
                    dve.wait_ge(scattered, t + 1)
                    target_hot(dve, c, hot[:, b % 2, :], t, narrow).then_inc(hot_ready, 1)
                    dve.wait_ge(q2_ready, t // U + 1)
                    dve.tensor_tensor(msg[:, b % 2, :], z2[:, b, :], q2[:, b, :], ALU.mult).then_inc(msg_ready, 1)
                return stage

            dve.wait_ge(w_high_ready, 2)
            dve.tensor_tensor(w2_low[:], w2[:], w2_high[:].bitcast(F32), ALU.subtract).then_inc(w_ready, 1)
            dve.tensor_tensor(w1_low[:], w1[0:64, :], w1_high[0:64, :].bitcast(F32), ALU.subtract).then_inc(w_ready, 1)
            for_width(dve, c, lambda narrow: tile_rounds(
                dve, [(output, OUTPUT), (split_features, EDGE), (first, FIRST), (copy_turned, COPY),
                      (message(narrow), MESSAGE), (hidden, HIDDEN)]))

        @blk.scalar
        def _(act):
            def features(G, p):
                act.wait_ge(ea_loaded[p], G // 2 * 32 + 32 if isinstance(G, int) else G.u * 32 + (G.off // 2 * 32 + 32))
                act.wait_ge(ea_ready, G + 1)
                act.wait_ge(edge_product, G * U + (2 * U - U))
                act.activation(ea_high[64:128, p, :], ea[64:128, p, :], ACT.Copy)
                act.activation(ea_both[0:64, p, :], ea[0:64, p, :], ACT.Copy).then_inc(ea_high_ready, 1)

            def angle(z, q, sums, credits, angles):
                def stage(G, p):
                    slots = slice(p * U, (p + 1) * U)
                    act.wait_ge(sums, G * U + (U + credits))
                    act.activation(q[:, slots, :], z[:, slots, :], ACT.Sigmoid, scale=-1.0).then_inc(angles, 1)
                    act.wait_ge(angles, G * 2 + 1)
                    act.activation(q[:, slots, :], q[:, slots, :], ACT.Arctan).then_inc(angles, 1)
                return stage

            def factor(q, angles, done):
                def stage(G, p):
                    slots = slice(p * U, (p + 1) * U)
                    act.wait_ge(angles, G * 2 + 2)
                    act.activation(q[:, slots, :], q[:, slots, :], ACT.Sin, scale=-2.0, bias=c.half_pi[:]).then_inc(done, 1)
                return stage

            act.wait_ge(w_loaded, 64)
            act.activation(w2_high[:], w2[:], ACT.Copy).then_inc(w_high_ready, 1)
            act.activation(w1_high[:], w1[:], ACT.Copy).then_inc(w_high_ready, 1)
            rounds(act, [(features, 0), (angle(z2, q2, z2_ready, 1, angles2), 1 + SECOND), (angle(z1, q1, z1_ready, U, angles1), 1),
                         (factor(q2, angles2, q2_ready), 1 + SECOND), (factor(q1, angles1, q1_ready), 1)],
                   4, 2, TURNS)
            act.wait_ge(scattered, 2 + TILES + 1)
            for j in range(J):
                act.activation(agg[:, j, :], acc[:, j, :], ACT.Copy).then_inc(copied, 1)


def edge_out(c, agg, ahead):
    nc, a = c.nc, c.a
    with ExitStack() as ctx:
        sb = lambda n, s: ctx.enter_context(nc.sbuf_tensor(f"eo_{n}", s, F32))
        w3 = sb("w3", [128, 2 * KT, D]); w4 = sb("w4", [128, KT, D]); b3 = sb("b3", [P, D]); b4 = sb("b4", [P, D])
        gain = sb("gain", [P, D]); bias = sb("bias", [P, D])
        aggT = sb("aggT", [128, KT, N]); uT = sb("uT", [128, KT, N])
        z = sb("z", [P, J, D]); q = sb("q", [P, J, D]); y = sb("y", [P, J, D])
        st = sb("st", [P, J, 6]); mv = sb("mv", [P, J, 2])
        acc = ctx.enter_context(nc.psum_tensor("eo_acc", [P, J, 512], F32))
        tp = ctx.enter_context(nc.psum_tensor("eo_tp", [128, 3, 512], F32))
        (w_loaded, n_loaded, turned, copied, product, taken, squared, q_ready, u_ready, out_ready, steps, var_ready,
         rooted) = (c.sem(f"eo_{n}") for n in (
            "w_loaded", "n_loaded", "turned", "copied", "product", "taken", "squared", "q_ready", "u_ready",
            "out_ready", "steps", "var_ready", "rooted"))
        blk = ctx.enter_context(nc.Block())

        @blk.sync
        def _(sp):
            sp.dma_start(w3[:], a["E_W3"].rearrange("(k q) f -> q k f", q=128)).then_inc(w_loaded, 16)
            sp.dma_start(b3[:], a["E_b3"].partition_broadcast(P)).then_inc(w_loaded, 16)
            sp.dma_start(w4[:], a["E_W4"].rearrange("(k q) f -> q k f", q=128)).then_inc(w_loaded, 16)
            sp.dma_start(b4[:], a["E_b4"].partition_broadcast(P)).then_inc(w_loaded, 16)
            sp.dma_start(gain[:], a["E_gamma"].partition_broadcast(P)).then_inc(n_loaded, 16)
            sp.dma_start(bias[:], a["E_beta"].partition_broadcast(P)).then_inc(n_loaded, 16)
            ahead.load(sp)

        @blk.tensor
        def _(pe):
            for n in range(J):
                if n >= 3:
                    pe.wait_ge(copied, n - 2)
                for k in range(KT):
                    ins = pe.transpose(tp[:, n % 3, col(k)], agg[:, n, col(k, 128)], c.ident[0:P, 0:P])
                ins.then_inc(turned, 1)
            pe.wait_ge(w_loaded, 64)
            for j in range(J):
                pe.wait_ge(copied, j + 1)
                for k in range(2 * KT):
                    lhs = c.xnT[:, k, col(j)] if k < KT else aggT[:, k - KT, col(j)]
                    ins = pe.matmul(acc[:, j, :], lhs, w3[:, k, :], start=(k == 0), stop=(k == 2 * KT - 1))
                ins.then_inc(product, 1)
            for j in range(J):
                pe.wait_ge(u_ready, j + 1)
                pe.wait_ge(copied, J if j < 1 else J + j - 1)
                for k in range(KT):
                    ins = pe.transpose(tp[:, j % 3, col(k)], y[:, j, col(k, 128)], c.ident[0:P, 0:P])
                ins.then_inc(turned, 1)
            for j in range(J):
                pe.wait_ge(copied, J + j + 1)
                for k in range(KT):
                    ins = pe.matmul(acc[:, j, :], uT[:, k, col(j)], w4[:, k, :], start=(k == 0), stop=(k == KT - 1))
                ins.then_inc(out_ready, 1)

        @blk.scalar
        def _(act):
            def copy(n, dst):
                act.wait_ge(turned, n + 1)
                act.activation(dst[:, :, col(n % J)], tp[:, n % J % 3, 0:KT * P].rearrange("q (k p) -> q k p", k=KT),
                               ACT.Copy).then_inc(copied, 1)
            for n in range(J):
                copy(n, aggT)
            for j in range(J):
                act.wait_ge(taken, j + 1)
                act.activation(q[:, j, :], z[:, j, :], ACT.Sigmoid, scale=-1.0).then_inc(squared, 1)
                act.wait_ge(squared, 2 * j + 1)
                act.activation(q[:, j, :], q[:, j, :], ACT.Arctan).then_inc(squared, 1)
            for j in range(J):
                act.wait_ge(squared, 2 * j + 2)
                act.activation(q[:, j, :], q[:, j, :], ACT.Sin, scale=-2.0, bias=c.half_pi[:]).then_inc(q_ready, 1)
            for n in range(J, 2 * J):
                copy(n, uT)
            act.wait_ge(var_ready, 1)
            act.activation(mv[:, :, 1], mv[:, :, 1], ACT.Sqrt).then_inc(rooted, 1)

        @blk.vector
        def _(dve):
            step = Chain(dve, steps)
            dve.wait_ge(w_loaded, 64)
            for j in range(J):
                dve.wait_ge(product, j + 1)
                dve.tensor_tensor(z[:, j, :], acc[:, j, :], b3[:], ALU.add).then_inc(taken, 1)
            for j in range(J):
                dve.wait_ge(q_ready, j + 1)
                dve.tensor_tensor(y[:, j, :], z[:, j, :], q[:, j, :], ALU.mult).then_inc(u_ready, 1)
            dve.wait_ge(copied, 2 * J)
            for j in range(J):
                dve.wait_ge(out_ready, j + 1)
                step(dve.tensor_tensor(y[:, j, :], acc[:, j, :], c.xn[:, j, :], ALU.add))
                step(dve.tensor_tensor(y[:, j, :], y[:, j, :], b4[:], ALU.add))
                step(dve.bn_stats(st[:, j, :], y[:, j, :]))
                step(dve.bn_aggr(mv[:, j, :], st[:, j, :]))
            dve.tensor_scalar(mv[:, :, 1], mv[:, :, 1], EPS, None, ALU.add).then_inc(var_ready, 1)
            dve.wait_ge(rooted, 1)
            step(dve.reciprocal(mv[:, :, 1], mv[:, :, 1]))
            dve.wait_ge(n_loaded, 32)
            for j in range(J):
                step(dve.tensor_scalar(y[:, j, :], y[:, j, :], mv[:, j, 0:1], mv[:, j, 1:2], ALU.subtract, ALU.mult))
                step(dve.tensor_tensor(y[:, j, :], y[:, j, :], gain[:], ALU.mult))
                step(dve.tensor_tensor(y[:, j, :], y[:, j, :], bias[:], ALU.add))
                step(dve.tensor_tensor(c.x[:, j, :], c.x[:, j, :], y[:, j, :], ALU.add))


def store(c):
    with ExitStack() as ctx:
        stored = c.sem("out_stored")
        blk = ctx.enter_context(c.nc.Block())

        @blk.sync
        def _(sp):
            sp.dma_start(c.a["out"].rearrange("(j p) d -> p j d", p=P), c.x[:]).then_inc(stored, 16)
            sp.wait_ge(stored, 16)


def program(nc, a):
    ctx = ExitStack()
    with ctx:
        c = Core(nc, ctx, a)
        buf = lambda s, name, shape: s.enter_context(nc.sbuf_tensor(name, shape, F32))
        setup(c)
        if STAGES >= 1:
            with ExitStack() as s:
                c.norm_room(s)
                norm(c)
                h_self = buf(s, "h_self", [P, J, D])
                rel_tables(c, h_self)
                rel_edges(c, h_self)
        c.recycle()
        if STAGES >= 2:
            ffn_large(c)
        c.norm_room(ctx)
        with ExitStack() as s1:
            f1 = small_weights(c, s1, "f1")
            if STAGES >= 3:
                mace_nodes(c)
                with ExitStack() as s:
                    agg_s, agg_v = buf(s, "agg_s", [P, J, D]), buf(s, "agg_v", [P, J, D])
                    with ExitStack() as s2:
                        h3T = buf(s2, "h3T", [128, E // 2])
                        mace_mlp(c, h3T)
                        mace_edges(c, h3T, False, agg_s, f1)
                        mace_edges(c, h3T, True, agg_v)
                    mace_out(c, agg_s, agg_v)
            c.recycle()
            if STAGES >= 4:
                ffn_small(c, "f1", "switch", ACT.Gelu, f1)
            c.recycle()
        with ExitStack() as s3:
            f2, edge_weights = small_weights(c, s3, "f2"), edge_node_weights(c, s3)
            if STAGES >= 5:
                with ExitStack() as s:
                    degree = buf(s, "degree", [P, J])
                    c.adjT = buf(s, "adjT", [P, J, N])
                    layers = [sage_weights(c, s, l) for l in range(3)]
                    adjacency(c, degree, layers + [f2, edge_weights])
                    norm(c)
                    for l in range(3):
                        sage_layer(c, l, c.xn, degree, l == 2, layers[l])
            if STAGES >= 6:
                ffn_small(c, "f2", "top2_capacity", ACT.Gelu_apprx_tanh, f2)
            c.recycle()
            if STAGES >= 7:
                edge_nodes(c, edge_weights)
        if STAGES >= 7:
            with ExitStack() as s:
                agg = buf(s, "agg_e", [P, J, D])
                edge_messages(c, agg)
                f3 = small_weights(c, s, "f3")
                edge_out(c, agg, f3)
                if STAGES >= 8:
                    ffn_small(c, "f3", "top2_scores", ACT.Gelu, f3)
        store(c)


STAGES = 8


def kernel(**v):
    import numpy as np
    import concourse.bacc as bacc
    from concourse.bass_utils import run_bass_kernel_spmd as run

    v = {k: np.asarray(x) for k, x in v.items()}
    cut = lambda x: x.reshape(2, TILES // 2, P, -1).transpose(1, 0, 2, 3).reshape(TILES, P, -1)
    tiles = lambda x: cut(x)[:, :, 0].T
    row = lambda x: x.reshape(1, -1)
    arrays = {
        "x": v["x"], "src": tiles(v["src"]), "dst": tiles(v["dst"]), "rel": tiles(v["edge_type_8"]),
        "dst_by_tile": v["dst"].reshape(2, TILES // 2, P).transpose(1, 0, 2),
        "ea4": cut(v["edge_attr_4"]).transpose(1, 0, 2),
        "ea8T": v["edge_attr_8"].reshape(2, E // 2, 8).transpose(0, 2, 1).reshape(16, E // 2),
        "ea64T": cut(v["edge_attr_64"]).reshape(E, 64).T,
        "iota": np.arange(N, dtype=np.float32), "ident": np.eye(128, dtype=np.float32),
        "spread": np.repeat(np.eye(NE, dtype=np.float32), 64, axis=1),
        "number": np.repeat(np.arange(1, N + 1, dtype=np.float32).reshape(J, P).T[:, :, None], 2, axis=2),
        "earlier": np.triu(np.ones((P, P), dtype=np.float32), 1),
        "W_rel": np.concatenate([v["L0_gnn_W_rel"], v["L0_gnn_W_self"][None]]).transpose(0, 2, 1).reshape(-1, D),
        "b_rel": np.concatenate([v["L0_gnn_b_rel"], v["L0_gnn_b_self"][None]]),
        "fl_wg": v["L0_ffn_wg"], "fl_bg": row(v["L0_ffn_bg"]), "fl_w1": v["L0_ffn_w1"], "fl_w3": v["L0_ffn_w3"],
        "fl_w2": v["L0_ffn_w2"], "a_prelu": v["L2_gnn_a_prelu"],
    }
    for n in ("W_up0", "W_up1", "W_mlp1", "W_mlp2", "W_mlp3", "W_mlp4", "W_out0", "W_out1"):
        arrays[n] = v["L1_gnn_" + n]
    for l in range(3):
        arrays[f"Wl{l}"], arrays[f"Wr{l}"] = v[f"L2_gnn_Wl{l}"].T, v[f"L2_gnn_Wr{l}"].T
        arrays[f"bl{l}"], arrays[f"g{l}"], arrays[f"b{l}"] = v[f"L2_gnn_bl{l}"], v[f"L2_gnn_g{l}"], v[f"L2_gnn_b{l}"]
    for n in ("W1", "W2", "W3", "W4", "gamma", "beta", "b2", "b3", "b4"):
        arrays["E_" + n] = v["L3_gnn_" + n]
    arrays["E_b1"] = row(v["L3_gnn_b1"])
    zero_bias = np.zeros((1, NE), np.float32)
    for tag, wg, bg, m in (("f1", "L1_ffn_Ws", "L1_ffn_bs", ("W1", "b1", "W2", "b2")),
                           ("f2", "L2_ffn_router_w", None, ("w1", "b1", "w2", "b2")),
                           ("f3", "L3_ffn_Wg", "L3_ffn_bg", ("W1", "b1", "W2", "b2"))):
        w1, b1, w2, b2 = (v[wg[:7] + n] for n in m)
        arrays[tag + "_wg"], arrays[tag + "_bg"] = v[wg], row(v[bg]) if bg else zero_bias
        arrays[tag + "_w1"] = w1.transpose(1, 0, 2).reshape(D, D)
        arrays[tag + "_b1"] = b1.reshape(KT, 128).T
        arrays[tag + "_w2"], arrays[tag + "_b2"] = w2.reshape(D, D), b2
    arrays = {k: np.ascontiguousarray(x) for k, x in arrays.items()}
    nc = bacc.Bacc("TRN2", target_bir_lowering=False, num_devices=1)
    a = {k: nc.dram_tensor("in_" + k, x.shape, mybir.dt.from_np(x.dtype), kind="ExternalInput").ap()
         for k, x in arrays.items()}
    a["out"] = nc.dram_tensor("out", (N, D), F32, kind="ExternalOutput").ap()
    program(nc, a)
    r = run(nc, [{"in_" + k: x for k, x in arrays.items()}], core_ids=[0])
    return r.results[0]["out"]
```
